# Optimizing a Trainium2 kernel written in Bass

```python
import numpy as np
import jax
import jax.numpy as jnp

def _softmax(x, axis=-1):
    return jax.nn.softmax(x, axis=axis)

def _gelu(x):
    return jax.nn.gelu(x, approximate=True)

def _silu(x):
    return jax.nn.silu(x)

def _sigmoid(x):
    return jax.nn.sigmoid(x)

def _layernorm(x, axis=-1, eps=1e-05):
    m = jnp.mean(x, axis=axis, keepdims=True)
    v = jnp.var(x, axis=axis, keepdims=True)
    return (x - m) / jnp.sqrt(v + eps)

def _scatter_add(tgt, idx, src, axis=0):
    return tgt.at[idx].add(src)

def _segment_sum(src, seg, n):
    return jax.ops.segment_sum(src, seg, n)
kernel_name = 'mk_xattn_ffn_d4_seqx_r8_1cff67'

def setup_inputs(seed: int=0):
    np.random.seed(seed)
    _w = jnp.asarray

    def _rec_inputs():
        import jax
        import jax.numpy as jnp
        _rk = jax.random.key(seed)
        x = -0.0003929 + 0.9999 * jax.random.normal(jax.random.fold_in(_rk, 1), (2, 256, 512), jnp.float32)
        _lenS = 256 - jax.random.randint(jax.random.fold_in(_rk, 7), (2,), 0, max(1, 256 // 4) + 1, jnp.int32)
        _lenS2 = 512 - jax.random.randint(jax.random.fold_in(_rk, 8), (2,), 0, max(1, 512 // 4) + 1, jnp.int32)
        _ctx_4096P = jax.random.normal(jax.random.fold_in(_rk, 11), (2, 16, 512), jnp.float32)
        _ctx_4096c = jax.random.dirichlet(jax.random.fold_in(_rk, 511), 0.3 * jnp.ones((16,), jnp.float32), (2, 512))
        _ctx_4096t = jnp.einsum('bsk,bkd->bsd', _ctx_4096c, _ctx_4096P)
        _ctx_4096t = _ctx_4096t * jax.lax.rsqrt(jnp.mean(jnp.square(_ctx_4096t)) + 1e-12) * 0.953939
        ctx_4096 = 2.81802e-05 + 1.00001 * (_ctx_4096t + 0.3 * jax.random.normal(jax.random.fold_in(_rk, 611), (2, 512, 512), jnp.float32))
        _validS = jnp.arange(256)[None, :] < _lenS[:, None]
        _validS2 = jnp.arange(512)[None, :] < _lenS2[:, None]
        _causal = jnp.tril(jnp.ones((256, 256), dtype=bool))
        mask_BxSxS2_ff0 = jnp.where(jnp.ones((2, 256, 512), dtype=bool), 0.0, -1000000000.0).astype(jnp.float32)
        mask_SxS2_bk0 = jnp.logical_not(jnp.broadcast_to(_validS2[0:1, :], (256, 512)))
        return (x, ctx_4096, mask_BxSxS2_ff0, mask_SxS2_bk0)
    x, ctx_4096, mask_BxSxS2_ff0, mask_SxS2_bk0 = _rec_inputs()

    def _L0_xattn_setup():
        import jax, jax.numpy as jnp
        import numpy as np
        BS, SEQ, D_MODEL = (4, 128, 512)
        N_Q_HEADS, N_KV_HEADS, D_K, D_V = (32, 8, 128, 128)
        ROPE_BASE = 10000.0

        def _rotate_half(x):
            x1, x2 = jnp.split(x, 2, axis=-1)
            return jnp.concatenate([-x2, x1], axis=-1)

        def _apply_rope(x, pos0):
            d = x.shape[-1]
            seq = x.shape[2]
            inv_freq = 1.0 / ROPE_BASE ** (jnp.arange(0, d, 2, dtype=jnp.float32) / d)
            pos = (pos0 + jnp.arange(seq)).astype(jnp.float32)
            ang = pos[:, None] * inv_freq[None, :]
            cos = jnp.concatenate([jnp.cos(ang), jnp.cos(ang)], axis=-1)
            sin = jnp.concatenate([jnp.sin(ang), jnp.sin(ang)], axis=-1)
            return x * cos[None, None] + _rotate_half(x) * sin[None, None]
        key = jax.random.key(seed)
        ks = jax.random.split(key, 8)
        w_scale = 0.02
        return {'query': jax.random.normal(ks[0], (BS, SEQ, D_MODEL), dtype=jnp.float32), 'key': jax.random.normal(ks[1], (BS, SEQ, D_MODEL), dtype=jnp.float32), 'value': jax.random.normal(ks[2], (BS, SEQ, D_MODEL), dtype=jnp.float32), 'mask': jnp.zeros((BS, SEQ, SEQ), dtype=jnp.float32), 'wq': jax.random.normal(ks[3], (D_MODEL, N_Q_HEADS * D_K), dtype=jnp.float32) * w_scale, 'wk': jax.random.normal(ks[4], (D_MODEL, N_KV_HEADS * D_K), dtype=jnp.float32) * w_scale, 'wv': jax.random.normal(ks[5], (D_MODEL, N_KV_HEADS * D_V), dtype=jnp.float32) * w_scale, 'wo': jax.random.normal(ks[6], (N_Q_HEADS * D_V, D_MODEL), dtype=jnp.float32) * w_scale, 'curr_seq_pos': 0}
    _L0_xattn_all = _L0_xattn_setup()
    _L0_xattn_in = {k: v for k, v in _L0_xattn_all.items() if k in ('wq', 'wk', 'wv', 'wo')}
    del _L0_xattn_all

    def _L0_ffn_setup():
        import jax, jax.numpy as jnp
        import numpy as np
        M = 512
        K = 512

        def _make_2to4_mask(key, shape):
            scores = jax.random.normal(key, shape)
            g = scores.reshape(shape[0], shape[1] // 4, 4)
            rank = jnp.argsort(jnp.argsort(-jnp.abs(g), axis=-1), axis=-1)
            return (rank < 2).reshape(shape).astype(jnp.float32)
        key = jax.random.key(seed)
        k_x, k_w12, k_b12, k_w3, k_b3, k_m = jax.random.split(key, 6)
        x = jax.random.normal(k_x, (4, 256, K), dtype=jnp.float32)
        w12_dense = jax.random.normal(k_w12, (2 * M, K), dtype=jnp.float32) * (1.0 / np.sqrt(K))
        mask12 = _make_2to4_mask(k_m, (2 * M, K))
        w12 = w12_dense * mask12
        b12 = jax.random.normal(k_b12, (2 * M,), dtype=jnp.float32) * 0.01
        w3 = jax.random.normal(k_w3, (M, M), dtype=jnp.float32) * (1.0 / np.sqrt(M))
        b3 = jax.random.normal(k_b3, (M,), dtype=jnp.float32) * 0.01
        return {'x': x, 'w12': w12, 'b12': b12, 'w3': w3, 'b3': b3}
    _L0_ffn_all = _L0_ffn_setup()
    _L0_ffn_in = {k: v for k, v in _L0_ffn_all.items() if k in ('w12', 'b12', 'w3', 'b3')}
    del _L0_ffn_all

    def _L1_xattn_setup():
        import jax, jax.numpy as jnp
        import numpy as np
        B, Q, D = (8, 64, 512)
        CTX = 512
        H, KV, HD = (16, 4, 96)
        G = H // KV
        key = jax.random.key(seed)
        ks = jax.random.split(key, 6)
        s = 0.02
        return {'latents': jax.random.normal(ks[0], (B, Q, D), jnp.float32), 'context': jax.random.normal(ks[1], (B, CTX, D), jnp.float32), 'Wq': jax.random.normal(ks[2], (H * HD, D), jnp.float32) * s, 'Wk': jax.random.normal(ks[3], (KV * HD, D), jnp.float32) * s, 'Wv': jax.random.normal(ks[4], (KV * HD, D), jnp.float32) * s, 'Wo': jax.random.normal(ks[5], (D, H * HD), jnp.float32) * s}
    _L1_xattn_all = _L1_xattn_setup()
    _L1_xattn_in = {k: v for k, v in _L1_xattn_all.items() if k in ('Wq', 'Wk', 'Wv', 'Wo')}
    del _L1_xattn_all

    def _L1_ffn_setup():
        import jax, jax.numpy as jnp
        import numpy as np

        def sparsemax(z):
            E = z.shape[-1]
            z_sorted = -jnp.sort(-z, axis=-1)
            z_cum = jnp.cumsum(z_sorted, axis=-1)
            k = jnp.arange(1, E + 1, dtype=z.dtype)
            support = 1.0 + k * z_sorted > z_cum
            k_z = jnp.sum(support, axis=-1, keepdims=True)
            tau_sum = jnp.take_along_axis(z_cum, k_z.astype(jnp.int32) - 1, axis=-1)
            tau = (tau_sum - 1.0) / k_z.astype(z.dtype)
            return jnp.maximum(z - tau, 0.0)
        key = jax.random.key(seed)
        ks = jax.random.split(key, 6)
        B, S, D_IN, D_OUT, E, R = (8, 256, 512, 512, 8, 16)
        x = jax.random.normal(ks[0], (B, S, D_IN), dtype=jnp.float32)
        W_base = jax.random.normal(ks[1], (D_OUT, D_IN), dtype=jnp.float32) * D_IN ** (-0.5)
        b_base = jax.random.normal(ks[2], (D_OUT,), dtype=jnp.float32) * 0.01
        W_router = jax.random.normal(ks[3], (E, D_IN), dtype=jnp.float32) * D_IN ** (-0.5)
        b_router = jnp.zeros((E,), dtype=jnp.float32)
        lora_A = jax.random.normal(ks[4], (E, D_IN, R), dtype=jnp.float32) * D_IN ** (-0.5)
        lora_B = jnp.zeros((E, R, D_OUT), dtype=jnp.float32)
        return {'x': x, 'W_base': W_base, 'b_base': b_base, 'W_router': W_router, 'b_router': b_router, 'lora_A': lora_A, 'lora_B': lora_B}
    _L1_ffn_all = _L1_ffn_setup()
    _L1_ffn_in = {k: v for k, v in _L1_ffn_all.items() if k in ('W_base', 'b_base', 'W_router', 'b_router', 'lora_A', 'lora_B')}
    del _L1_ffn_all

    def _L2_xattn_setup():
        import jax, jax.numpy as jnp
        import numpy as np
        import math
        HIDDEN = 512
        N_HEADS = 32
        HEAD_DIM = 128
        N_KV_HEADS = 4
        N_GROUPS = N_HEADS // N_KV_HEADS
        key = jax.random.key(seed)
        ks = jax.random.split(key, 6)
        B, NL, S = (8, 64, 512)
        latents = jax.random.normal(ks[0], (B, NL, HIDDEN), dtype=jnp.float32)
        context = jax.random.normal(ks[1], (B, S, HIDDEN), dtype=jnp.float32)
        scale = 1.0 / math.sqrt(HIDDEN)
        Wq = jax.random.normal(ks[2], (HIDDEN, N_HEADS * HEAD_DIM), dtype=jnp.float32) * scale
        Wk = jax.random.normal(ks[3], (HIDDEN, N_KV_HEADS * HEAD_DIM), dtype=jnp.float32) * scale
        Wv = jax.random.normal(ks[4], (HIDDEN, N_KV_HEADS * HEAD_DIM), dtype=jnp.float32) * scale
        Wo = jax.random.normal(ks[5], (N_HEADS * HEAD_DIM, HIDDEN), dtype=jnp.float32) * scale
        return {'latents': latents, 'context': context, 'Wq': Wq, 'Wk': Wk, 'Wv': Wv, 'Wo': Wo}
    _L2_xattn_all = _L2_xattn_setup()
    _L2_xattn_in = {k: v for k, v in _L2_xattn_all.items() if k in ('Wq', 'Wk', 'Wv', 'Wo')}
    del _L2_xattn_all

    def _L2_ffn_setup():
        import jax, jax.numpy as jnp
        import numpy as np
        BATCH, SEQ, D = (2, 256, 512)
        K, TOPK, RANK = (64, 16, 16)
        ALPHA = 32.0
        SCALING = ALPHA / RANK
        key = jax.random.key(seed)
        k1, k2, k3, k4 = jax.random.split(key, 4)
        x = jax.random.normal(k1, (BATCH, SEQ, D), dtype=jnp.float32)
        A = jax.random.normal(k2, (K, RANK, D), dtype=jnp.float32) * 0.02
        B = jax.random.normal(k3, (K, D, RANK), dtype=jnp.float32) * 0.02
        Wr = jax.random.normal(k4, (K, D), dtype=jnp.float32) * 0.02
        return {'x': x, 'A': A, 'B': B, 'Wr': Wr}
    _L2_ffn_all = _L2_ffn_setup()
    _L2_ffn_in = {k: v for k, v in _L2_ffn_all.items() if k in ('A', 'B', 'Wr')}
    del _L2_ffn_all

    def _L3_xattn_setup():
        import jax, jax.numpy as jnp
        import numpy as np
        N_HEAD = 32
        D_MODEL = 512
        N_KV_GROUPS = 8
        D_HEAD = D_MODEL // N_HEAD
        H_PER_G = N_HEAD // N_KV_GROUPS
        KV_DIM = N_KV_GROUPS * D_HEAD
        B, S = (2, 256)
        key = jax.random.key(seed)
        ks = jax.random.split(key, 8)
        q = jax.random.normal(ks[0], (B, S, D_MODEL), dtype=jnp.float32)
        k = jax.random.normal(ks[1], (B, S, D_MODEL), dtype=jnp.float32)
        v = jax.random.normal(ks[2], (B, S, D_MODEL), dtype=jnp.float32)
        mask = jnp.tril(jnp.ones((S, S), dtype=bool))
        w_q = jax.random.uniform(ks[3], (D_MODEL, D_MODEL), dtype=jnp.float32) * 0.02
        w_k = jax.random.uniform(ks[4], (KV_DIM, D_MODEL), dtype=jnp.float32) * 0.02
        w_v = jax.random.uniform(ks[5], (KV_DIM, D_MODEL), dtype=jnp.float32) * 0.02
        w_out = jax.random.uniform(ks[6], (D_MODEL, D_MODEL), dtype=jnp.float32) * 0.02
        return {'q': q, 'k': k, 'v': v, 'w_q': w_q, 'w_k': w_k, 'w_v': w_v, 'w_out': w_out, 'mask': mask}
    _L3_xattn_all = _L3_xattn_setup()
    _L3_xattn_in = {k: v for k, v in _L3_xattn_all.items() if k in ('w_q', 'w_k', 'w_v', 'w_out')}
    del _L3_xattn_all

    def _L3_ffn_setup():
        import jax, jax.numpy as jnp
        import numpy as np
        THRESHOLD = 3.0

        def _ste_quant_rows(a):
            scale = jnp.max(jnp.abs(a), axis=-1, keepdims=True) / 127.0
            scale = jnp.maximum(scale, 1e-08)
            q = jnp.clip(jnp.round(a / scale), -127.0, 127.0) * scale
            return a + jax.lax.stop_gradient(q - a)

        def _linear8bit(x, W, b):
            col_max = jnp.max(jnp.abs(x), axis=tuple(range(x.ndim - 1)))
            outlier = col_max > THRESHOLD
            x_in = jnp.where(outlier, 0.0, x)
            x_out = jnp.where(outlier, x, 0.0)
            y = _ste_quant_rows(x_in) @ _ste_quant_rows(W).T
            y = y + x_out @ W.T + b
            return y
        key = jax.random.key(seed)
        k1, k2, k3, k4, k5 = jax.random.split(key, 5)
        dim1, dim2 = (512, 2048)
        x = jax.random.normal(k1, (4, 256, dim1), dtype=jnp.float32)
        W1 = jax.random.normal(k2, (dim2, dim1), dtype=jnp.float32) * 0.02
        b1 = jax.random.normal(k3, (dim2,), dtype=jnp.float32) * 0.01
        W2 = jax.random.normal(k4, (dim1, dim2), dtype=jnp.float32) * 0.02
        b2 = jax.random.normal(k5, (dim1,), dtype=jnp.float32) * 0.01
        return {'x': x, 'W1': W1, 'b1': b1, 'W2': W2, 'b2': b2}
    _L3_ffn_all = _L3_ffn_setup()
    _L3_ffn_in = {k: v for k, v in _L3_ffn_all.items() if k in ('W1', 'b1', 'W2', 'b2')}
    del _L3_ffn_all
    return {'x': x, 'ctx_4096': ctx_4096, 'mask_BxSxS2_ff0': mask_BxSxS2_ff0, 'mask_SxS2_bk0': mask_SxS2_bk0, 'L0_xattn_wq': _L0_xattn_in['wq'], 'L0_xattn_wk': _L0_xattn_in['wk'], 'L0_xattn_wv': _L0_xattn_in['wv'], 'L0_xattn_wo': _L0_xattn_in['wo'], 'L0_ffn_w12': _L0_ffn_in['w12'], 'L0_ffn_b12': _L0_ffn_in['b12'], 'L0_ffn_w3': _L0_ffn_in['w3'], 'L0_ffn_b3': _L0_ffn_in['b3'], 'L1_xattn_Wq': _L1_xattn_in['Wq'], 'L1_xattn_Wk': _L1_xattn_in['Wk'], 'L1_xattn_Wv': _L1_xattn_in['Wv'], 'L1_xattn_Wo': _L1_xattn_in['Wo'], 'L1_ffn_W_base': _L1_ffn_in['W_base'], 'L1_ffn_b_base': _L1_ffn_in['b_base'], 'L1_ffn_W_router': _L1_ffn_in['W_router'], 'L1_ffn_b_router': _L1_ffn_in['b_router'], 'L1_ffn_lora_A': _L1_ffn_in['lora_A'], 'L1_ffn_lora_B': _L1_ffn_in['lora_B'], 'L2_xattn_Wq': _L2_xattn_in['Wq'], 'L2_xattn_Wk': _L2_xattn_in['Wk'], 'L2_xattn_Wv': _L2_xattn_in['Wv'], 'L2_xattn_Wo': _L2_xattn_in['Wo'], 'L2_ffn_A': _L2_ffn_in['A'], 'L2_ffn_B': _L2_ffn_in['B'], 'L2_ffn_Wr': _L2_ffn_in['Wr'], 'L3_xattn_w_q': _L3_xattn_in['w_q'], 'L3_xattn_w_k': _L3_xattn_in['w_k'], 'L3_xattn_w_v': _L3_xattn_in['w_v'], 'L3_xattn_w_out': _L3_xattn_in['w_out'], 'L3_ffn_W1': _L3_ffn_in['W1'], 'L3_ffn_b1': _L3_ffn_in['b1'], 'L3_ffn_W2': _L3_ffn_in['W2'], 'L3_ffn_b2': _L3_ffn_in['b2']}

def reference(x, ctx_4096, mask_BxSxS2_ff0, mask_SxS2_bk0, L0_xattn_wq, L0_xattn_wk, L0_xattn_wv, L0_xattn_wo, L0_ffn_w12, L0_ffn_b12, L0_ffn_w3, L0_ffn_b3, L1_xattn_Wq, L1_xattn_Wk, L1_xattn_Wv, L1_xattn_Wo, L1_ffn_W_base, L1_ffn_b_base, L1_ffn_W_router, L1_ffn_b_router, L1_ffn_lora_A, L1_ffn_lora_B, L2_xattn_Wq, L2_xattn_Wk, L2_xattn_Wv, L2_xattn_Wo, L2_ffn_A, L2_ffn_B, L2_ffn_Wr, L3_xattn_w_q, L3_xattn_w_k, L3_xattn_w_v, L3_xattn_w_out, L3_ffn_W1, L3_ffn_b1, L3_ffn_W2, L3_ffn_b2):
    import jax
    import jax.numpy as jnp

    def _L0_xattn_ref(query, key, value, mask, wq, wk, wv, wo, curr_seq_pos):
        import jax, jax.numpy as jnp
        import numpy as np
        BS, SEQ, D_MODEL = (4, 128, 512)
        N_Q_HEADS, N_KV_HEADS, D_K, D_V = (32, 8, 128, 128)
        ROPE_BASE = 10000.0

        def _rotate_half(x):
            x1, x2 = jnp.split(x, 2, axis=-1)
            return jnp.concatenate([-x2, x1], axis=-1)

        def _apply_rope(x, pos0):
            d = x.shape[-1]
            seq = x.shape[2]
            inv_freq = 1.0 / ROPE_BASE ** (jnp.arange(0, d, 2, dtype=jnp.float32) / d)
            pos = (pos0 + jnp.arange(seq)).astype(jnp.float32)
            ang = pos[:, None] * inv_freq[None, :]
            cos = jnp.concatenate([jnp.cos(ang), jnp.cos(ang)], axis=-1)
            sin = jnp.concatenate([jnp.sin(ang), jnp.sin(ang)], axis=-1)
            return x * cos[None, None] + _rotate_half(x) * sin[None, None]
        bs, sq, _ = query.shape
        n_groups = N_Q_HEADS // N_KV_HEADS
        q = (query @ wq).reshape(bs, sq, N_Q_HEADS, D_K).transpose((0, 2, 1, 3))
        sk = key.shape[1]
        k = (key @ wk).reshape(bs, sk, N_KV_HEADS, 1, D_K)
        k = jnp.repeat(k, n_groups, axis=3).reshape(bs, sk, N_Q_HEADS, D_K).transpose((0, 2, 1, 3))
        v = (value @ wv).reshape(bs, sk, N_KV_HEADS, 1, D_V)
        v = jnp.repeat(v, n_groups, axis=3).reshape(bs, sk, N_Q_HEADS, D_V).transpose((0, 2, 1, 3))
        scale = jnp.sqrt(jnp.float32(D_K))
        q = _apply_rope(q, curr_seq_pos)
        k = _apply_rope(k, curr_seq_pos)
        raw = jnp.einsum('bhqd,bhkd->bhqk', q, k) / scale
        masked = raw + mask[:bs, None, curr_seq_pos:curr_seq_pos + sq, :sk]
        attn = jax.nn.softmax(masked, axis=-1)
        out = jnp.einsum('bhqk,bhkd->bhqd', attn, v)
        out = out.transpose((0, 2, 1, 3)).reshape(bs, sq, N_Q_HEADS * D_V)
        return out @ wo

    def _L0_ffn_ref(x, w12, b12, w3, b3):
        import jax, jax.numpy as jnp
        import numpy as np
        M = 512
        K = 512

        def _make_2to4_mask(key, shape):
            scores = jax.random.normal(key, shape)
            g = scores.reshape(shape[0], shape[1] // 4, 4)
            rank = jnp.argsort(jnp.argsort(-jnp.abs(g), axis=-1), axis=-1)
            return (rank < 2).reshape(shape).astype(jnp.float32)
        x12 = jnp.einsum('bsk,mk->bsm', x, w12) + b12
        x1, x2 = jnp.split(x12, 2, axis=-1)
        x4 = jax.nn.silu(x1) * x2
        return jnp.einsum('bsm,nm->bsn', x4, w3) + b3

    def _L1_xattn_ref(latents, context, Wq, Wk, Wv, Wo):
        import jax, jax.numpy as jnp
        import numpy as np
        B, Q, D = (8, 64, 512)
        CTX = 512
        H, KV, HD = (16, 4, 96)
        G = H // KV
        b, q_len, _ = latents.shape
        hidden = jnp.concatenate([context, latents], axis=1)
        s_len = hidden.shape[1]
        q = (latents @ Wq.T).reshape(b, q_len, H, HD)
        k = (hidden @ Wk.T).reshape(b, s_len, KV, HD)
        v = (hidden @ Wv.T).reshape(b, s_len, KV, HD)
        q = q.transpose(0, 2, 1, 3).reshape(b, KV, G, q_len, HD)
        k = k.transpose(0, 2, 1, 3)
        v = v.transpose(0, 2, 1, 3)
        scale = 1.0 / jnp.sqrt(jnp.asarray(HD, q.dtype))
        scores = jnp.einsum('bkgqd,bksd->bkgqs', q, k) * scale
        attn = jax.nn.softmax(scores.astype(jnp.float32), axis=-1).astype(q.dtype)
        out = jnp.einsum('bkgqs,bksd->bkgqd', attn, v)
        out = out.reshape(b, H, q_len, HD).transpose(0, 2, 1, 3).reshape(b, q_len, H * HD)
        return out @ Wo.T

    def _L1_ffn_ref(x, W_base, b_base, W_router, b_router, lora_A, lora_B):
        import jax, jax.numpy as jnp
        import numpy as np

        def sparsemax(z):
            E = z.shape[-1]
            z_sorted = -jnp.sort(-z, axis=-1)
            z_cum = jnp.cumsum(z_sorted, axis=-1)
            k = jnp.arange(1, E + 1, dtype=z.dtype)
            support = 1.0 + k * z_sorted > z_cum
            k_z = jnp.sum(support, axis=-1, keepdims=True)
            tau_sum = jnp.take_along_axis(z_cum, k_z.astype(jnp.int32) - 1, axis=-1)
            tau = (tau_sum - 1.0) / k_z.astype(z.dtype)
            return jnp.maximum(z - tau, 0.0)
        base_out = jnp.einsum('bsd,od->bso', x, W_base) + b_base
        logits = jnp.einsum('bsd,ed->bse', x, W_router) + b_router
        weights = sparsemax(logits)
        h = jnp.einsum('bsd,edr->bser', x, lora_A)
        expert_out = jnp.einsum('bser,bse,ero->bso', h, weights, lora_B)
        return base_out + expert_out

    def _L2_xattn_ref(latents, context, Wq, Wk, Wv, Wo):
        import jax, jax.numpy as jnp
        import numpy as np
        import math
        HIDDEN = 512
        N_HEADS = 32
        HEAD_DIM = 128
        N_KV_HEADS = 4
        N_GROUPS = N_HEADS // N_KV_HEADS
        b, q_len, _ = latents.shape
        kv_len = q_len + context.shape[1]
        hidden_states = jnp.concatenate([context, latents], axis=1)
        q = (latents @ Wq).reshape(b, q_len, N_KV_HEADS, N_GROUPS, HEAD_DIM)
        k = (hidden_states @ Wk).reshape(b, kv_len, N_KV_HEADS, HEAD_DIM)
        v = (hidden_states @ Wv).reshape(b, kv_len, N_KV_HEADS, HEAD_DIM)
        scale = 1.0 / math.sqrt(HEAD_DIM)
        scores = jnp.einsum('bqhgd,bkhd->bhgqk', q, k) * scale
        attn = jax.nn.softmax(scores.astype(jnp.float32), axis=-1).astype(q.dtype)
        out = jnp.einsum('bhgqk,bkhd->bqhgd', attn, v)
        out = out.reshape(b, q_len, N_HEADS * HEAD_DIM)
        return out @ Wo

    def _L2_ffn_ref(x, A, B, Wr):
        import jax, jax.numpy as jnp
        import numpy as np
        BATCH, SEQ, D = (2, 256, 512)
        K, TOPK, RANK = (64, 16, 16)
        ALPHA = 32.0
        SCALING = ALPHA / RANK
        prefix = x.shape[:-1]
        xf = x.reshape(-1, x.shape[-1])
        N = xf.shape[0]
        scores = xf @ Wr.T
        top_vals, top_idx = jax.lax.top_k(scores, TOPK)
        gates = jax.nn.softmax(top_vals, axis=-1)
        G = jnp.zeros((N, K), xf.dtype).at[jnp.arange(N)[:, None], top_idx].set(gates)
        h = jnp.einsum('nd,krd->nkr', xf, A)
        out = jnp.einsum('nkr,kdr->nd', h * G[:, :, None], B)
        return (out * SCALING).reshape(*prefix, -1)

    def _L3_xattn_ref(q, k, v, w_q, w_k, w_v, w_out, mask):
        import jax, jax.numpy as jnp
        import numpy as np
        N_HEAD = 32
        D_MODEL = 512
        N_KV_GROUPS = 8
        D_HEAD = D_MODEL // N_HEAD
        H_PER_G = N_HEAD // N_KV_GROUPS
        KV_DIM = N_KV_GROUPS * D_HEAD
        B, S = (2, 256)
        b, n, _ = q.shape
        s = k.shape[1]
        query = q @ w_q.T
        key = k @ w_k.T
        value = v @ w_v.T
        query = query.reshape(b, n, N_HEAD, D_HEAD).transpose(0, 2, 1, 3)
        query = query.reshape(b, N_KV_GROUPS, H_PER_G, n, D_HEAD)
        key = key.reshape(b, s, N_KV_GROUPS, D_HEAD).transpose(0, 2, 1, 3)
        value = value.reshape(b, s, N_KV_GROUPS, D_HEAD).transpose(0, 2, 1, 3)
        scores = jnp.einsum('bghnd,bgsd->bghns', query, key) / D_HEAD ** 0.5
        scores = jnp.where(mask, scores, jnp.finfo(scores.dtype).min)
        attention = jax.nn.softmax(scores, axis=-1)
        out = jnp.einsum('bghns,bgsd->bghnd', attention, value)
        out = out.transpose(0, 3, 1, 2, 4).reshape(b, n, D_MODEL)
        return out @ w_out.T

    def _L3_ffn_ref(x, W1, b1, W2, b2):
        import jax, jax.numpy as jnp
        import numpy as np
        THRESHOLD = 3.0

        def _ste_quant_rows(a):
            scale = jnp.max(jnp.abs(a), axis=-1, keepdims=True) / 127.0
            scale = jnp.maximum(scale, 1e-08)
            q = jnp.clip(jnp.round(a / scale), -127.0, 127.0) * scale
            return a + jax.lax.stop_gradient(q - a)

        def _linear8bit(x, W, b):
            col_max = jnp.max(jnp.abs(x), axis=tuple(range(x.ndim - 1)))
            outlier = col_max > THRESHOLD
            x_in = jnp.where(outlier, 0.0, x)
            x_out = jnp.where(outlier, x, 0.0)
            y = _ste_quant_rows(x_in) @ _ste_quant_rows(W).T
            y = y + x_out @ W.T + b
            return y
        h = _linear8bit(x, W1, b1)
        return _linear8bit(h, W2, b2)
    x = x + _L0_xattn_ref(_layernorm(x, axis=-1), ctx_4096, ctx_4096, mask_BxSxS2_ff0, L0_xattn_wq, L0_xattn_wk, L0_xattn_wv, L0_xattn_wo, 0)
    x = x + _L0_ffn_ref(_layernorm(x, axis=-1), L0_ffn_w12, L0_ffn_b12, L0_ffn_w3, L0_ffn_b3)
    x = x + _L1_xattn_ref(_layernorm(x, axis=-1), ctx_4096, L1_xattn_Wq, L1_xattn_Wk, L1_xattn_Wv, L1_xattn_Wo)
    x = x + _L1_ffn_ref(_layernorm(x, axis=-1), L1_ffn_W_base, L1_ffn_b_base, L1_ffn_W_router, L1_ffn_b_router, L1_ffn_lora_A, L1_ffn_lora_B)
    x = x + _L2_xattn_ref(_layernorm(x, axis=-1), ctx_4096, L2_xattn_Wq, L2_xattn_Wk, L2_xattn_Wv, L2_xattn_Wo)
    x = x + _L2_ffn_ref(_layernorm(x, axis=-1), L2_ffn_A, L2_ffn_B, L2_ffn_Wr)
    x = x + _L3_xattn_ref(_layernorm(x, axis=-1), ctx_4096, ctx_4096, L3_xattn_w_q, L3_xattn_w_k, L3_xattn_w_v, L3_xattn_w_out, mask_SxS2_bk0)
    x = x + _L3_ffn_ref(_layernorm(x, axis=-1), L3_ffn_W1, L3_ffn_b1, L3_ffn_W2, L3_ffn_b2)
    return x

_drawn_inputs = setup_inputs


def setup_inputs(seed=0):
    import zlib

    import numpy as np

    out = dict(_drawn_inputs(seed))
    spreads = {'L1_ffn_b_router': (0.0, 0.31), 'L1_ffn_lora_B': (0.0, 0.1)}
    factors = {'L0_xattn_wq': 4.879,
     'L0_xattn_wk': 4.939,
     'L0_ffn_b12': 8.0,
     'L0_ffn_b3': 6.837,
     'L1_xattn_Wq': 7.513,
     'L1_xattn_Wk': 7.501,
     'L1_ffn_b_base': 8.0,
     'L2_ffn_A': 6.163,
     'L2_ffn_B': 5.974,
     'L2_ffn_Wr': 6.831,
     'L3_xattn_w_q': 8.0,
     'L3_xattn_w_k': 8.0,
     'L3_xattn_w_out': 7.086,
     'L3_ffn_b1': 24.683,
     'L3_ffn_b2': 23.885}
    for name, (base, spread) in spreads.items():
        noise = np.random.default_rng([zlib.crc32(name.encode()), seed]).standard_normal(out[name].shape)
        drawn = base * np.exp(spread * noise) if base else spread * noise
        out[name] = jnp.asarray(drawn.astype(out[name].dtype))
    for name, factor in factors.items():
        out[name] = (out[name] * factor).astype(out[name].dtype)
    return out
```

```python
from contextlib import ExitStack

import numpy as np
import concourse.bass as bass
from concourse import mybir

ALU = mybir.AluOpType
ACT = mybir.ActivationFunctionType
AX = mybir.AxisListType
F32 = mybir.dt.float32
F32R = mybir.dt.float32r
BF16 = mybir.dt.bfloat16
U8 = mybir.dt.uint8

P = 128
B, SQ, SK, D = 2, 256, 512, 512
T = B * SQ
C = B * SK
DK = D // P
TT = T // P
HG = 4
NEG = -3.0e38
F32_MAX = 3.4028234663852886e38
MAGIC = 12582912.0
FFN_H = 2048
KB = 1024

class Layer:

    def __init__(self, name, groups, hd, self_keys, kv_every, rope):
        self.name, self.groups, self.hd, self.kv_every, self.rope = name, groups, hd, kv_every, rope
        self.self_keys = self_keys
        self.keys = SK + (SQ if self_keys else 0)
        self.kt = self.keys // P
        self.parts = 3 if self_keys else 2
        self.kv_tiles = 3 * self.parts
        self.kv_hi = 2 * self.parts
        self.pieces = [(0, 4), (4, 2)] if self_keys else [(0, 4)]
        self.scale = float(hd) ** -0.5

L0 = Layer("l0", 8, 128, False, 1, True)
L1 = Layer("l1", 4, 96, True, 1, False)
L2 = Layer("l2", 8, 128, True, 2, False)
TILES = 2 * B * HG
UNITS = B * HG
PIPE = TILES + 4
L3_TILES = 4 * 16
L3_PIPE = L3_TILES + 4

def program(nc, A, out):
    ctx = ExitStack()
    with ctx:
        base = nc.sbuf_base
        base = base() if callable(base) else base
        base = (base + 31) // 32 * 32

        def at(name, shape, dt, kb):
            return nc.alloc_sbuf_tensor_at(name, shape, dt, offset=base + int(kb * KB))

        def sem(name):
            return ctx.enter_context(nc.semaphore(name))

        x = at("x", [P, TT, D], F32, 0)
        xn = at("xn", [P, TT, D], F32, 8)
        xT = [at("xT_hi", [P, DK, T], F32R, 16), at("xT_lo", [P, DK, T], F32R, 24)]
        cT = [at("cT_hi", [P, DK, C], F32R, 32), at("cT_lo", [P, DK, C], F32R, 48)]
        W = {"q": [at("wq_hi", [P, 4, 512], F32R, 64), at("wq_lo", [P, 4, 512], F32R, 72)],
             "o": [at("wo_hi", [P, 4, 512], F32R, 80), at("wo_lo", [P, 4, 512], F32R, 88)],
             "kv": [at("wkv_hi", [P, 4, 256], F32R, 96), at("wkv_lo", [P, 4, 256], F32R, 100)]}
        raw_big = at("raw_big", [P, 4, 512], F32, 104)
        raw_kv = at("raw_kv", [P, 4, 256], F32, 112)
        RAW = {"q": raw_big, "o": raw_big, "kv": raw_kv}
        ident = at("ident", [P, P], F32, 116)
        st = at("st", [P, TT, 6], F32, 116.5)
        mv = at("mv", [P, TT, 2], F32, 116.625)
        veps = at("veps", [P, TT], F32, 116.6875)
        rstd = at("rstd", [P, TT], F32, 116.71875)
        mhalf = at("mhalf", [P, TT], F32, 116.75)
        one = at("one", [P, 1], F32, 117)
        nmax = at("nmax", [P, TILES], F32, 116.8125)
        rsum = at("rsum", [P, TILES], F32, 116.875)
        rinv = at("rinv", [P, TILES], F32, 116.9375)
        R0 = 117.5

        craw = at("craw", [P, DK, C], F32, R0)

        class Space:
            pass

        def attention_space(l):
            s = Space()
            o = R0

            def take(name, shape, dt):
                nonlocal o
                size = int(np.prod(shape[1:])) * 4
                a = at(f"{l.name}_{name}", shape, dt, o)
                o += size / KB
                return a
            s.q = [take("q_hi", [P, HG, T], F32R), take("q_lo", [P, HG, T], F32R)]
            s.k = [take("k_hi", [P, B, l.keys], F32R), take("k_lo", [P, B, l.keys], F32R)]
            s.v = [take("v_hi", [P, B, l.kt, P], F32R), take("v_lo", [P, B, l.kt, P], F32R)]
            s.pt = [[take(f"pt{i}_{n}", [P, l.kt, SQ], F32R) for n in ("hi", "lo")] for i in range(2)]
            s.ot = [take("ot_hi", [P, HG, T], F32R), take("ot_lo", [P, HG, T], F32R)]
            s.p = take("p", [P, 3, l.keys], F32)
            if l.rope:
                s.cos, s.sin = take("cos", [P, SK], F32), take("sin", [P, SK], F32)
                s.ra, s.rb = take("ra", [P, 2, 512], F32), take("rb", [P, 2, 512], F32)
                s.mask = take("mask", [P, TT, SK], F32)
            return s
        SP = {l.name: attention_space(l) for l in (L0, L1, L2)}

        l3x = at("l3_x", [P, 4, T], F32R, R0)
        l3y = [at("l3_y_hi", [P, C], F32R, R0 + 8), at("l3_y_lo", [P, C], F32R, R0 + 12)]
        l3v = at("l3_v", [P, C // P, 4, 2, 16], F32R, R0 + 16)
        l3pt = [[at(f"l3_pt{i}_{n}", [P, 4, P], F32R, R0 + 20 + 4 * i + 2 * j) for j, n in enumerate(("hi", "lo"))]
                for i in range(2)]
        l3p = at("l3_p", [P, 3, SK], F32, R0 + 28)
        l3m8 = at("l3_m8", [P, 2, SK], U8, R0 + 34)
        l3mask = at("l3_mask", [P, 2, SK], F32, R0 + 35)
        l3t = at("l3_t", [P, 2, 512], F32R, R0 + 39)
        l3k = at("l3_k", [P, 2, 512], F32, R0 + 43)
        l3sel = at("l3_sel", [P, 2], F32, R0 + 47)
        l3half = at("l3_half", [P, 256], F32, R0 + 48)
        l3rs = at("l3_rs", [P, 64], F32, R0 + 49)
        l3nm = at("l3_nm", [P, 64], F32, R0 + 49.25)
        l3ri = at("l3_ri", [P, 16], F32, R0 + 49.5)

        f_rowb = at("f_rowb", [P, 512], F32, R0)
        f0_b12 = at("f0_b12", [P, 8], F32, R0 + 2)
        f0_nb = at("f0_nb", [P, 8], F32, R0 + 2.25)
        f0_e = at("f0_e", [P, 2, 512], F32, R0 + 3)
        f0_s = at("f0_s", [P, 512], F32, R0 + 7)
        f0_g = at("f0_g", [P, 512], F32, R0 + 9)
        f_h = [at("f_h_hi", [P, 4, T], F32R, R0 + 11), at("f_h_lo", [P, 4, T], F32R, R0 + 19)]
        f1_br = at("f1_br", [P, 8], F32, R0 + 2)
        f1_z = at("f1_z", [P, TT, 8], F32, R0 + 3)
        f1_zs = at("f1_zs", [P, TT, 8], F32, R0 + 3.25)
        f1_c = at("f1_c", [P, TT, 8], F32, R0 + 3.5)
        f1_tau = at("f1_tau", [P, TT], F32, R0 + 3.75)
        f1_w = at("f1_w", [P, TT, 8], F32, R0 + 4)
        f1_h = at("f1_h", [P, TT, P], F32, R0 + 5)
        f1_ht = [at("f1_ht_hi", [P, T], F32R, R0 + 7), at("f1_ht_lo", [P, T], F32R, R0 + 9)]
        f2_s = at("f2_s", [P, TT, 64], F32, R0)
        f2_a = at("f2_a", [P, TT, 64], F32, R0 + 1)
        f2_b = at("f2_b", [P, TT, 64], F32, R0 + 2)
        f2_g = at("f2_g", [P, TT, 64], F32, R0 + 3)
        f2_m = at("f2_m", [P, TT, 2, 8], F32, R0 + 4)
        f2_nm = at("f2_nm", [P, TT], F32, R0 + 4.25)
        f2_sum = at("f2_sum", [P, TT], F32, R0 + 4.5)
        f2_r = at("f2_r", [P, TT], F32, R0 + 4.75)
        f2_tok = at("f2_tok", [P, 2, TT, 512], F32, R0 + 5)
        f2_h = [[at(f"f2_h{c}_{n}", [P, 4, T], F32R, R0 + 21 + 16 * c + 8 * j) for j, n in enumerate(("hi", "lo"))]
                for c in range(2)]

        HT = FFN_H // P
        q_w2 = at("q_w2", [P, HT, D], BF16, 32)
        q_nat = at("q_nat", [P, 2048], F32, 48)
        q_int = at("q_int", [P, 2048], BF16, 56)
        identb = at("identb", [P, P], BF16, 60)
        ones = at("ones", [P, P], F32, 60.25)
        diag4 = at("diag4", [P, 4, P], F32, 62)
        q_b1 = at("q_b1", [P, HT], F32, 61.25)
        q_am = at("q_am", [P, 32], F32, 61.3125)
        q_sw1 = at("q_sw1", [P, HT], F32, 61.4375)
        q_sw2 = at("q_sw2", [P, DK], F32, 61.5)
        q_rs = at("q_rs", [P, 2], F32, 61.53125)
        q_cm = at("q_cm", [P, HT], F32, 61.5625)
        q_mo = at("q_mo", [P, HT], F32, 61.625)
        q_mi = at("q_mi", [P, HT], F32, 61.6875)
        q_tm = at("q_tm", [P, TT], F32, 61.75)
        q_ts = at("q_ts", [P, TT], F32, 61.78125)
        h = at("h", [P, HT, T], F32, R0)
        q_w1 = at("q_w1", [P, DK, FFN_H], BF16, R0 + 32)
        xF = at("xF", [P, DK, T], F32, R0 + 48)
        xq = at("xq", [P, DK, T], BF16, R0 + 56)
        q_srow = at("q_srow", [P, T], F32, R0 + 60)
        q_rrow = at("q_rrow", [P, T], F32, R0 + 62)
        q_amx = at("q_amx", [P, T], F32, R0 + 64)
        q_t = at("q_t", [P, 2, 512], F32, R0 + 66)
        q_amn = at("q_amn", [P, T], F32, R0 + 78)
        hq = at("hq", [P, HT, T], BF16, R0 + 32)
        ho = [at("ho_hi", [P, 4, T], F32R, R0 + 48), at("ho_lo", [P, 4, T], F32R, R0 + 70)]
        q_s2row = at("q_s2row", [P, D], F32, R0 + 80)
        q_b2 = at("q_b2", [P, D], F32, R0 + 82)

        ps_s = [ctx.enter_context(nc.psum_tensor(f"ps_s{i}", [P, 2, 512], F32)) for i in range(2)]
        ps_t = [ctx.enter_context(nc.psum_tensor(f"ps_t{i}", [P, 512], F32)) for i in range(3)]
        ps_o = ctx.enter_context(nc.psum_tensor("ps_o", [P, 512], F32))
        ring = [ps_s[0][:, 0, :], ps_s[0][:, 1, :], ps_s[1][:, 0, :], ps_s[1][:, 1, :]]

        s_const = sem("const_in")
        s_x = sem("x_in")
        s_ctx = sem("context_in")
        s_lay = sem("layer_consts_in")
        s_ident = sem("ident_made")
        s_csplit = sem("context_split")
        s_chi = sem("context_hi")
        s_ve = sem("var_eps_ready")
        s_rstd = sem("rstd_ready")
        s_xn = sem("xn_ready")
        w_in = {r: sem(f"w_{r}_in") for r in ("q", "kv", "o")}
        w_rdy = {r: sem(f"w_{r}_split") for r in ("q", "kv", "o")}
        g_full = sem("gemm_tile_full")
        g_hi = sem("gemm_tile_hi_out")
        g_free = sem("gemm_tile_out")
        s_link = sem("dve_chain")
        s_plink = sem("pool_chain")
        s_ra = sem("rotated")
        s_S = sem("scores_ready")
        s_max = sem("max_ready")
        s_exp = sem("probs_ready")
        s_rec = sem("sum_inverse_ready")
        s_scl = [sem("even_probs_normalised"), sem("odd_probs_normalised")]
        s_T = sem("probs_turned")
        s_thi = sem("turned_hi_out")
        s_tlo = sem("turned_lo_out")
        s_pv = sem("attention_out_ready")
        s_ohi = sem("attention_out_hi")
        s_olo = sem("attention_out_lo")
        s_go = sem("tile_taken")
        s_rot = sem("rotation_parts")
        s_swap = sem("halves_swapped")
        s_nat = sem("rows_in")
        s_out = sem("stored")

        class Start:

            def __init__(self, g, hi, tile, piece, unit, q, kv, o, ra):
                self.g, self.hi, self.tile, self.piece, self.unit = g, hi, tile, piece, unit
                self.q, self.kv, self.o, self.ra = q, kv, o, ra
        counts = {n: 0 for n in ("g", "hi", "tile", "piece", "unit", "q", "kv", "o", "ra")}
        START = {}

        def phase(name, **adds):
            START[name] = Start(**counts)
            for k, v in adds.items():
                counts[k] += v

        def attention_counts(l):
            n = l.groups
            kv = n // l.kv_every
            phase(l.name, g=kv * l.kv_tiles + n * 8, hi=kv * l.kv_hi + n * HG, tile=n * TILES,
                  piece=n * TILES * len(l.pieces), unit=n * UNITS, q=n, kv=kv, o=n,
                  ra=n * (HG + 2) if l.rope else 0)
        phase("ln0", g=4, hi=4)
        attention_counts(L0)
        phase("ln1", g=4, hi=4)
        phase("f0", g=8 + 4, hi=0, q=2, o=1)
        phase("ln2", g=4, hi=4)
        attention_counts(L1)
        phase("ln3", g=4, hi=4)
        phase("f1", g=4 + 4 + 1 + 4, hi=1, q=1, kv=1, o=1)
        phase("ln4", g=4, hi=4)
        attention_counts(L2)
        phase("ln5", g=4, hi=4)
        phase("f2", g=1 + 8 + 8 + 4, hi=8, q=2, kv=1, o=2)
        phase("ln6", g=4, hi=4)
        phase("l3", g=2 * (4 + 2 + 2) + 4 + 4, hi=2 * (4 + 2 + 2) + 4, tile=128, piece=128, unit=8, q=2, kv=2, o=1)
        phase("ln7", g=4, hi=4)
        phase("f3", q=4, o=4)

        def passes(pe, o, a, b, start, stop):
            pe.matmul(o, a[0], b[0], start=start, stop=False)
            pe.matmul(o, a[0], b[1], start=False, stop=False)
            return pe.matmul(o, a[1], b[0], start=False, stop=stop)

        def planes(t, *index):
            return [p[index] for p in t]

        def load(sp, role, n, src, before, parts=P, cols=512, tiles=4):
            if before is not None:
                sp.wait_ge(w_rdy[before[0]], before[1] * 8)
            sp.dma_start(RAW[role][0:parts, 0:tiles, 0:cols], src).then_inc(w_in[role], 16)

        def split(pool, role, n, used, piece, parts=P, cols=512):
            if piece == 0:
                pool.wait_ge(w_in[role], n * 16 + 16)
                if used is not None:
                    pool.wait_ge(g_full, used)
            w = RAW[role][0:parts, piece, 0:cols]
            hi = W[role][0][0:parts, piece, 0:cols]
            lo = W[role][1][0:parts, piece, 0:cols]
            pool.tensor_tensor(hi, w, one[0:parts, 0:1].to_broadcast([parts, cols]), ALU.mult).then_inc(w_rdy[role], 1)
            pool.wait_ge(w_rdy[role], n * 8 + (2 * piece + 1))
            pool.tensor_tensor(lo, w, hi.bitcast(F32), ALU.subtract).then_inc(w_rdy[role], 1)

        def split_all(pool, role, n, used, parts=P, cols=512):
            for piece in range(4):
                split(pool, role, n, used, piece, parts, cols)

        class Norm:

            def __init__(self, i):
                self.i, self.c = i, START[f"ln{i}"]

            def dve(self, e, link):
                if self.c.g:
                    e.wait_ge(g_free, self.c.g)
                for t in range(TT):
                    last = e.bn_stats(st[:, t, :], x[:, t, :])
                link(last)
                for t in range(TT):
                    last = e.bn_aggr(mv[:, t, :], st[:, t, :])
                link(last)
                e.tensor_scalar(veps[:, :], mv[:, :, 1], 1e-5, None, ALU.add).then_inc(s_ve, 1)
                e.wait_ge(s_rstd, self.i + 1)
                if self.i:
                    e.wait_ge(g_full, self.c.g)
                for t in range(TT):
                    e.tensor_scalar(xn[:, t, :], x[:, t, :], mv[:, t, 0:1], rstd[:, t:t + 1],
                                    ALU.subtract, ALU.mult).then_inc(s_xn, 1)
                turn_dve(e, self.c.g, self.c.hi, xT)

            def pool(self, e):
                e.wait_ge(s_ve, self.i + 1)
                e.tensor_tensor(rstd[:, :], veps[:, :], mhalf[:, :], ALU.pow).then_inc(s_rstd, 1)

            def pe(self, e):
                e.wait_ge(s_xn, TT * (self.i + 1))
                turn_pe(e, xn, self.c.g)

            def act(self, e):
                turn_act(e, self.c.g, self.c.hi, xT)

        def turn_pe(e, src, g):
            for d in range(4):
                if g + d > 3:
                    e.wait_ge(g_free, g + d - 3)
                for t in range(TT):
                    mm = e.transpose(ring[(g + d) % 4][:, t * P:(t + 1) * P], src[:, t, d * P:(d + 1) * P], ident[:, :])
                mm.then_inc(g_full, 1)

        def hi_act(e, dst, src, g, scale=1.0):
            e.wait_ge(g_full, g + 1)
            e.activation(dst, src, ACT.Copy, scale=scale).then_inc(g_hi, 1)

        def lo_dve(e, dst, hi, src, hin, scale=1.0):
            e.wait_ge(g_hi, hin + 1)
            if scale == 1.0:
                e.tensor_tensor(dst, src, hi.bitcast(F32), ALU.subtract).then_inc(g_free, 1)
                return
            e.scalar_tensor_tensor(out=dst, in0=src, scalar=scale, in1=hi.bitcast(F32),
                                   op0=ALU.mult, op1=ALU.subtract).then_inc(g_free, 1)

        def turn_act(e, g, hi, dst):
            for d in range(4):
                hi_act(e, dst[0][:, d, :], ring[(g + d) % 4], g + d)

        def turn_dve(e, g, hi, dst):
            for d in range(4):
                lo_dve(e, dst[1][:, d, :], dst[0][:, d, :], ring[(g + d) % 4], hi + d)

        class Attention:
            def __init__(self, l, A, first_before):
                self.l, self.s, self.c = l, SP[l.name], START[l.name]
                self.wkv, self.wq, self.wo = A[l.name + "_wkv"], A[l.name + "_wq"], A[l.name + "_wo"]
                self.first_before = first_before
                self.per = l.kv_every

            def loop(self, e, body, extra=()):
                n = self.l.groups // self.per
                with e.Fori(0, n - 1) as i:
                    body(e, i, False)
                body(e, n - 1, True)

            def g_start(self, it, s):
                per_it = self.l.kv_tiles + 8 * self.per
                return it * per_it + (self.c.g + self.l.kv_tiles + 8 * s)

            def hi_start(self, it, s):
                return it * (self.l.kv_hi + HG * self.per) + (self.c.hi + self.l.kv_hi + HG * s)

            def grp(self, it, s):
                return it * self.per + s

            def sp_first(self, e):
                l, c = self.l, self.c
                load(e, "kv", c.kv, self.wkv[0], ("kv", c.kv) if c.kv else None, cols=2 * l.hd)
                load(e, "q", c.q, self.wq[0], self.first_before, cols=HG * l.hd)

            def sp(self, e):
                l, c = self.l, self.c

                def body(e, it, last):
                    for s in range(self.per):
                        g = self.grp(it, s)
                        load(e, "o", None, self.wo[g], ("q", g + (c.q + 1)), parts=l.hd)
                        if s == self.per - 1 and not last:
                            load(e, "kv", None, self.wkv[it + 1], ("kv", it + (c.kv + 1)), cols=2 * l.hd)
                        if not (last and s == self.per - 1):
                            load(e, "q", None, self.wq[g + 1], ("o", g + (c.o + 1)), cols=HG * l.hd)
                self.loop(e, body)

            def pool_first(self, e):
                l, c = self.l, self.c
                split_all(e, "kv", c.kv, c.g - 8 if c.kv else None, cols=2 * l.hd)
                split_all(e, "q", c.q, c.g - 4 if c.q else None, cols=HG * l.hd)

            def pool(self, e):
                l, c, sp = self.l, self.c, self.s

                def body(e, it, last):
                    for s in range(self.per):
                        g = self.grp(it, s)
                        gs = self.g_start(it, s)
                        more = [("o", g + c.o, gs, p, l.hd, 512) for p in range(4)]
                        if s == self.per - 1 and not last:
                            more += [("kv", it + (c.kv + 1), gs, p, P, 2 * l.hd) for p in range(4)]
                        if not (last and s == self.per - 1):
                            more += [("q", g + (c.q + 1), gs + HG, p, P, HG * l.hd) for p in range(4)]
                        for job in more:
                            split(e, *job)
                self.loop(e, body)

            def pe(self, e):
                l, c, sp = self.l, self.c, self.s
                hd = l.hd

                def body(e, it, last):
                    g0 = self.g_start(it, 0) - l.kv_tiles
                    n = 0
                    e.wait_ge(w_rdy["kv"], it * 8 + (8 * c.kv + 8))

                    def bank_of(n, g0):
                        e.wait_ge(g_free, g0 + max(0, n - 3))
                        return ring[n % 4]
                    for src, w, lo in [(cT, SK, b * SK) for b in range(B)] + ([(xT, T, 0)] if l.self_keys else []):
                        o = bank_of(n, g0)
                        for d in range(DK):
                            mm = passes(e, o[0:hd, 0:w], planes(W["kv"], slice(None), d, slice(0, hd)),
                                        planes(src, slice(None), d, slice(lo, lo + w)), d == 0, d == DK - 1)
                        mm.then_inc(g_full, 1)
                        n += 1
                    for src, lo in [(cT, b * SK) for b in range(B)] + ([(xT, 0)] if l.self_keys else []):
                        o = bank_of(n, g0)
                        for d in range(DK):
                            mm = passes(e, o[0:hd, :], planes(W["kv"], slice(None), d, slice(hd, 2 * hd)),
                                        planes(src, slice(None), d, slice(lo, lo + 512)), d == 0, d == DK - 1)
                        mm.then_inc(g_full, 1)
                        n += 1
                    for j in range(l.parts):
                        o = bank_of(n, g0)
                        e.wait_ge(g_free, g0 + (l.parts + j + 1))
                        for t in range(4):
                            mm = e.transpose(o[:, t * P:t * P + hd], xn[0:hd, j, t * P:(t + 1) * P], ident[0:hd, 0:hd])
                        mm.then_inc(g_full, 1)
                        n += 1
                    for s in range(self.per):
                        g = self.grp(it, s)
                        gs = self.g_start(it, s)
                        e.wait_ge(w_rdy["q"], g * 8 + (8 * c.q + 8))
                        for hh in range(HG):
                            nn = n + hh if s == 0 else hh
                            o = bank_of(nn, g0 if s == 0 else gs)
                            for d in range(DK):
                                mm = passes(e, o[0:hd, :], planes(W["q"], slice(None), d, slice(hh * hd, (hh + 1) * hd)),
                                            planes(xT, slice(None), d, slice(None)), d == 0, d == DK - 1)
                            mm.then_inc(g_full, 1)
                        e.wait_ge(g_free, gs + HG)

                        def scores(i):
                            u, qt = i // 2, i % 2
                            b, hh = u // HG, u % HG
                            if i >= 2:
                                e.wait_ge(s_exp, g * TILES + (c.tile + i - 1))
                            q = planes(sp.q, slice(0, hd), hh, slice(b * SQ + qt * P, b * SQ + (qt + 1) * P))
                            for j, (lo, w) in enumerate([(0, SK)] + ([(SK, SQ)] if l.self_keys else [])):
                                mm = passes(e, ps_s[i % 2][:, j, 0:w], q,
                                            planes(sp.k, slice(0, hd), b, slice(lo, lo + w)), True, True)
                            mm.then_inc(s_S, 1)

                        def turn(i):
                            e.wait_ge(s_scl[i % 2], g * (TILES // 2) + (c.tile // 2 + i // 2 + 1))
                            for j, (k0, nk) in enumerate(l.pieces):
                                p = i * len(l.pieces) + j
                                if p >= 3:
                                    e.wait_ge(s_tlo, g * (TILES * len(l.pieces)) + (c.piece + p - 2))
                                for k in range(nk):
                                    mm = e.transpose(ps_t[p % 3][:, k * P:(k + 1) * P],
                                                     sp.p[:, i % 3, (k0 + k) * P:(k0 + k + 1) * P], ident[:, :])
                                mm.then_inc(s_T, 1)

                        def attend(u):
                            b = u // HG
                            np_ = len(l.pieces)
                            e.wait_ge(s_tlo, g * (TILES * np_) + (c.piece + (2 * u + 2) * np_))
                            if u >= (2 if l.rope else 1):
                                e.wait_ge(s_olo, g * UNITS + (c.unit + u - (1 if l.rope else 0)))
                            for k in range(l.kt):
                                mm = passes(e, out_of(l, u)[0:hd, :], planes(sp.v, slice(None), b, k, slice(0, hd)),
                                            planes(sp.pt[u % 2], slice(None), k, slice(None)), k == 0, k == l.kt - 1)
                            mm.then_inc(s_pv, 1)
                        for i in range(PIPE):
                            if i < TILES:
                                scores(i)
                            if 0 <= i - 2 < TILES:
                                turn(i - 2)
                            if i >= 4 and i % 2 == 0 and (i - 4) // 2 < UNITS:
                                attend((i - 4) // 2)
                        e.wait_ge(w_rdy["o"], g * 8 + (8 * c.o + 8))
                        e.wait_ge(s_olo, g * UNITS + (c.unit + UNITS))
                        for t in range(TT):
                            for hh in range(HG):
                                mm = passes(e, ring[t], planes(sp.ot, slice(0, hd), hh, slice(t * P, (t + 1) * P)),
                                            planes(W["o"], slice(0, hd), hh, slice(None)), hh == 0, hh == HG - 1)
                            mm.then_inc(g_full, 1)
                self.loop(e, body)

            def act(self, e):
                l, c, sp = self.l, self.c, self.s
                hd = l.hd

                def body(e, it, last):
                    g0 = self.g_start(it, 0) - l.kv_tiles
                    h0 = self.hi_start(it, 0) - l.kv_hi
                    n = 0

                    def swap(n, gn, r, ra):
                        e.wait_ge(g_full, gn + 1)
                        if r >= 2:
                            e.wait_ge(s_ra, ra - 1)
                        for p0, p1 in ((0, 64), (64, 0)):
                            e.activation(sp.rb[p0:p0 + 64, r % 2, :], ring[n % 4][p1:p1 + 64, :], ACT.Copy)\
                                .then_inc(s_swap, 1)

                    def rotated(n, r, dst, scale, ra):
                        e.wait_ge(s_ra, ra + 1)
                        e.activation(dst, sp.ra[:, r % 2, :], ACT.Copy, scale=scale).then_inc(g_hi, 1)
                    ra0 = it * (HG + 2) + c.ra if l.rope else 0
                    for b in range(B):
                        if l.rope:
                            if b == 0:
                                for b_ in range(B):
                                    swap(b_, g0 + b_, b_, ra0 + b_)
                            rotated(n, b, sp.k[0][:, b, :], 1.0, ra0 + b)
                        else:
                            hi_act(e, sp.k[0][0:hd, b, 0:SK], ring[n % 4][0:hd, :], g0 + n)
                        n += 1
                    if l.self_keys:
                        hi_act(e, sp.k[0][0:hd, :, SK:l.keys], ring[n % 4][0:hd, :].rearrange("p (b t) -> p b t", b=B), g0 + n)
                        n += 1
                    n += l.parts
                    for dst, src in v_tiles(l, sp, 0, n):
                        hi_act(e, dst, src, g0 + n)
                        n += 1
                    for s in range(self.per):
                        g = self.grp(it, s)
                        gs = self.g_start(it, s)
                        for hh in range(HG):
                            nn = n + hh if s == 0 else hh
                            if l.rope:
                                if hh == 0:
                                    swap(nn, gs, 2, ra0 + 2)
                                if hh + 1 < HG:
                                    swap(nn + 1, gs + (hh + 1), 3 + hh, ra0 + (3 + hh))
                                rotated(nn, 2 + hh, sp.q[0][:, hh, :], l.scale, ra0 + 2 + hh)
                            else:
                                hi_act(e, sp.q[0][0:hd, hh, :], ring[nn % 4][0:hd, :], gs + hh, l.scale)
                        np_ = len(l.pieces)
                        for i in range(PIPE):
                            if i >= 5 and i % 2 == 1 and (i - 5) // 2 < UNITS:
                                u = (i - 5) // 2
                                b, hh = u // HG, u % HG
                                e.wait_ge(s_pv, g * UNITS + (c.unit + u + 1))
                                e.activation(sp.ot[0][0:hd, hh, b * SQ:(b + 1) * SQ], out_of(l, u)[0:hd, :],
                                             ACT.Copy).then_inc(s_ohi, 1)
                            if i % 2 == 1 and i - 1 < TILES:
                                e.wait_ge(s_rec, g * TILES + (c.tile + i))
                                pr = sp.p[:, (i - 1) % 3, :]
                                e.activation(pr, pr, ACT.Copy, scale=rinv[:, i - 1:i]).then_inc(s_scl[0], 1)
                            if 0 <= i - 2 < TILES:
                                j = i - 2
                                u, qt = j // 2, j % 2
                                if qt == 0:
                                    if u >= 2:
                                        e.wait_ge(s_pv, g * UNITS + (c.unit + u - 1))
                                for m, (k0, nk) in enumerate(l.pieces):
                                    p = j * np_ + m
                                    e.wait_ge(s_T, g * (TILES * np_) + (c.piece + p + 1))
                                    e.activation(sp.pt[u % 2][0][:, k0:k0 + nk, qt * P:(qt + 1) * P],
                                                 ps_t[p % 3][:, 0:nk * P].rearrange("p (k q) -> p k q", q=P),
                                                 ACT.Copy).then_inc(s_thi, 1)
                            if i < TILES:
                                e.wait_ge(s_max, g * TILES + (c.tile + i + 1))
                                src = sp.p[:, i % 3, :] if l.rope else ps_flat(i)[:, 0:l.keys]
                                e.activation(sp.p[:, i % 3, :], src, ACT.Exp, bias=nmax[:, i:i + 1],
                                             scale=-1.0 if l.rope else 1.0,
                                             accum_out=rsum[:, i:i + 1]).then_inc(s_exp, 1)
                self.loop(e, body)

            def dve(self, e, link):
                l, c, sp = self.l, self.c, self.s
                hd = l.hd

                def body(e, it, last):
                    g0 = self.g_start(it, 0) - l.kv_tiles
                    h0 = self.hi_start(it, 0) - l.kv_hi
                    n = 0
                    ra0 = it * (HG + 2) + c.ra if l.rope else None

                    def rotate(n, gn, r, ra):
                        b2 = 1 if r < 2 else B
                        w = 512 // b2

                        def v3(a):
                            return a.rearrange("p (b t) -> p b t", b=b2)

                        def tab(t, p0, p1):
                            a = t[p0:p1, 0:w]
                            return a.rearrange("p (b t) -> p b t", b=1) if b2 == 1 else \
                                a.unsqueeze(1).to_broadcast([p1 - p0, b2, w])
                        e.wait_ge(g_full, gn + 1)
                        if r >= 2:
                            e.wait_ge(g_free, gn - 1)
                        pt = ring[n % 4]
                        e.wait_ge(s_swap, ra * 2 + 2)
                        e.tensor_tensor(v3(sp.ra[:, r % 2, :]), v3(pt), tab(sp.cos, 0, P), ALU.mult).then_inc(s_rot, 1)
                        e.tensor_tensor(v3(sp.rb[:, r % 2, :]), v3(sp.rb[:, r % 2, :]), tab(sp.sin, 0, P), ALU.mult)\
                            .then_inc(s_rot, 1)
                        e.wait_ge(s_rot, ra * 2 + 2)
                        e.tensor_tensor(sp.ra[:, r % 2, :], sp.ra[:, r % 2, :], sp.rb[:, r % 2, :], ALU.add).then_inc(s_ra, 1)

                    def rotated_lo(r, dst, hi, scale, hn, ra):
                        e.wait_ge(s_ra, ra + 1)
                        lo_dve(e, dst, hi, sp.ra[:, r % 2, :], hn, scale)
                    if l.rope:
                        for b in range(B):
                            rotate(b, g0 + b, b, ra0 + b)
                        for b in range(B):
                            rotated_lo(b, sp.k[1][:, b, :], sp.k[0][:, b, :], 1.0, h0 + b, ra0 + b)
                        n = 2
                    else:
                        for b in range(B):
                            lo_dve(e, sp.k[1][0:hd, b, 0:SK], sp.k[0][0:hd, b, 0:SK], ring[n % 4][0:hd, :], h0 + n)
                            n += 1
                        lo_dve(e, sp.k[1][0:hd, :, SK:l.keys], sp.k[0][0:hd, :, SK:l.keys],
                               ring[n % 4][0:hd, :].rearrange("p (b t) -> p b t", b=B), h0 + n)
                        n += 1
                    for j in range(l.parts):
                        e.wait_ge(g_full, g0 + (n + 1))
                        e.tensor_copy(xn[0:hd, j, :], ring[n % 4][0:hd, :]).then_inc(g_free, 1)
                        n += 1
                    for (dst, src), (hi, _) in zip(v_tiles(l, sp, 1, n), v_tiles(l, sp, 0, n)):
                        lo_dve(e, dst, hi, src, h0 + (n - l.parts))
                        n += 1
                    np_ = len(l.pieces)
                    for s in range(self.per):
                        g = self.grp(it, s)
                        gs = self.g_start(it, s)
                        hs = self.hi_start(it, s)
                        for hh in range(HG):
                            nn = n + hh if s == 0 else hh
                            if l.rope:
                                if hh == 0:
                                    rotate(nn, gs, 2, ra0 + 2)
                                if hh + 1 < HG:
                                    rotate(nn + 1, gs + (hh + 1), 3 + hh, ra0 + (3 + hh))
                                rotated_lo(2 + hh, sp.q[1][:, hh, :], sp.q[0][:, hh, :], l.scale, hs + hh, ra0 + (2 + hh))
                            else:
                                lo_dve(e, sp.q[1][0:hd, hh, :], sp.q[0][0:hd, hh, :], ring[nn % 4][0:hd, :], hs + hh, l.scale)
                        for i in range(PIPE):
                            if 0 <= i - 1 < TILES:
                                e.wait_ge(s_exp, g * TILES + (c.tile + i))
                                e.reciprocal(rinv[:, i - 1:i], rsum[:, i - 1:i]).then_inc(s_rec, 1)
                            if i >= 5 and i % 2 == 1 and (i - 5) // 2 < UNITS:
                                u = (i - 5) // 2
                                b, hh = u // HG, u % HG
                                e.wait_ge(s_ohi, g * UNITS + (c.unit + u + 1))
                                ot = [a[0:hd, hh, b * SQ:(b + 1) * SQ] for a in sp.ot]
                                e.tensor_tensor(ot[1], out_of(l, u)[0:hd, :], ot[0].bitcast(F32), ALU.subtract).then_inc(s_olo, 1)
                            if i % 2 == 0 and 0 <= i - 1 < TILES:
                                e.wait_ge(s_rec, g * TILES + (c.tile + i))
                                pr = sp.p[:, (i - 1) % 3, :]
                                e.tensor_scalar(pr, pr, rinv[:, i - 1:i], None, ALU.mult).then_inc(s_scl[1], 1)
                            if i < TILES:
                                b, qt = i // (2 * HG), i % 2
                                e.wait_ge(s_S, g * TILES + (c.tile + i + 1))
                                if l.rope:
                                    if i >= 3:
                                        e.wait_ge(s_T, g * TILES + (c.piece + i - 2))
                                    e.sem_inc(s_go, 1)
                                    e.tensor_tensor_reduce(out=sp.p[:, i % 3, :], in0=ps_s[i % 2][:, 0, :],
                                                           in1=sp.mask[:, 2 * b + qt, :], scale=-1.0, scalar=F32_MAX,
                                                           op0=ALU.add, op1=ALU.min,
                                                           accum_out=nmax[:, i:i + 1]).then_inc(s_max, 1)
                                else:
                                    e.tensor_reduce(nmax[:, i:i + 1], ps_flat(i)[:, 0:l.keys], AX.X, ALU.max,
                                                    negate=True).then_inc(s_max, 1)
                            if 0 <= i - 2 < TILES:
                                j = i - 2
                                u, qt = j // 2, j % 2
                                for m, (k0, nk) in enumerate(l.pieces):
                                    p = j * np_ + m
                                    e.wait_ge(s_thi, g * (TILES * np_) + (c.piece + p + 1))
                                    pt = [a[:, k0:k0 + nk, qt * P:(qt + 1) * P] for a in sp.pt[u % 2]]
                                    e.tensor_tensor(pt[1], ps_t[p % 3][:, 0:nk * P].rearrange("p (k q) -> p k q", q=P),
                                                    pt[0].bitcast(F32), ALU.subtract).then_inc(s_tlo, 1)
                        for t in range(TT):
                            e.wait_ge(g_full, gs + (HG + t + 1))
                            e.wait_ge(g_free, gs + HG)
                            e.tensor_tensor(x[:, t, :], ring[t], x[:, t, :], ALU.add).then_inc(g_free, 1)
                self.loop(e, body)

        def out_of(l, u):
            return ps_s[0][:, 1, 0:SQ] if l.rope and u % 2 else ps_o[:, 0:SQ]

        def ps_flat(i):
            return ps_s[i % 2][:, :, :].rearrange("p a n -> p (a n)")

        def v_tiles(l, sp, plane, n):
            hd = l.hd
            out_ = []
            for b in range(B):
                out_.append((sp.v[plane][:, b, 0:4, 0:hd], ring[(n + b) % 4].rearrange("p (t d) -> p t d", d=P)[:, :, 0:hd]))
            if l.self_keys:
                out_.append((sp.v[plane][:, :, 4:6, 0:hd],
                             ring[(n + 2) % 4].rearrange("p (b t d) -> p b t d", b=B, d=P)[:, :, :, 0:hd]))
            return out_

        def ring_of(n, c):
            return ring[(c.g + n) % 4]

        def take_bank(e, n, c):
            if c.g + n > 3:
                e.wait_ge(g_free, c.g + n - 3)
            return ring_of(n, c)

        def token_gemm(e, n, c, a, b, kts, width=512):
            for t in range(TT):
                o = take_bank(e, n + t, c)
                for k in kts:
                    mm = passes(e, o[:, 0:width], a(k, t), b(k), k == kts[0], k == kts[-1])
                mm.then_inc(g_full, 1)

        def add_to_x(e, n, c):
            for t in range(TT):
                e.wait_ge(g_full, c.g + n + t + 1)
                e.tensor_tensor(x[:, t, :], ring_of(n + t, c), x[:, t, :], ALU.add).then_inc(g_free, 1)

        def add_row(e, row, link):
            for t in range(TT):
                last = e.tensor_tensor(x[:, t, :], x[:, t, :], row, ALU.add)
            link(last)

        def xT_of(d, t):
            return planes(xT, slice(None), d, slice(t * P, (t + 1) * P))

        c0 = START["f0"]
        s_f0e, s_f0s, s_f0hi, s_f0lo = (sem(f"f0_{n}") for n in ("exp", "bias_negated", "hi", "lo"))

        def f0_sp(e):
            load(e, "q", c0.q, A["f0_w12"][0], ("o", c0.o))
            e.wait_ge(g_full, c0.g - 4)
            e.dma_start(f0_b12[:, :], A["f0_b12"]).then_inc(s_lay, 16)
            e.dma_start(f_rowb[:, :], A["f0_b3"]).then_inc(s_lay, 16)
            load(e, "o", c0.o, A["f0_w12"][1], ("q", c0.q + 1))
            load(e, "q", c0.q + 1, A["f0_w3"], ("o", c0.o + 1))

        def f0_pool_first(e):
            split_all(e, "q", c0.q, c0.g - 8)

        def f0_pool(e):
            split_all(e, "o", c0.o, c0.g - 4)
            split_all(e, "q", c0.q + 1, c0.g + 8)

        def f0_pe(e):
            for j in range(4):
                for role in ("q", "o"):
                    e.wait_ge(w_rdy[role], 8 * ((c0.q if role == "q" else c0.o) + 1))
                    n = 2 * j + (role == "o")
                    o = take_bank(e, n, c0)
                    for d in range(DK):
                        mm = passes(e, o, planes(W[role], slice(None), d, slice(j * P, (j + 1) * P)),
                                    planes(xT, slice(None), d, slice(None)), d == 0, d == DK - 1)
                    mm.then_inc(g_full, 1)
            e.wait_ge(w_rdy["q"], 8 * (c0.q + 2))
            e.wait_ge(s_f0lo, 4)
            token_gemm(e, 8, c0, lambda k, t: planes(f_h, slice(None), k, slice(t * P, (t + 1) * P)),
                       lambda k: planes(W["q"], slice(None), k, slice(None)), range(4))

        def f0_act(e):
            for j in range(4):
                e.wait_ge(g_full, c0.g + 2 * j + 1)
                e.wait_ge(s_f0s, 1)
                if j >= 2:
                    e.wait_ge(g_free, c0.g + 2 * j - 3)
                e.activation(f0_e[:, j % 2, :], ring_of(2 * j, c0), ACT.Exp, bias=f0_nb[:, j:j + 1],
                             scale=-1.0).then_inc(s_f0e, 1)
                e.wait_ge(g_free, c0.g + 2 * j + 2)
                e.activation(f_h[0][:, j, :], f0_g[:, :], ACT.Copy).then_inc(s_f0hi, 1)

        def f0_dve(e, link):
            e.wait_ge(s_lay, LAY["f0"])
            e.tensor_scalar(f0_nb[:, :], f0_b12[:, :], -1.0, None, ALU.mult).then_inc(s_f0s, 1)
            for j in range(4):
                e.wait_ge(s_f0e, j + 1)
                link(e.tensor_scalar(f0_s[:, :], f0_e[:, j % 2, :], 1.0, None, ALU.add))
                link(e.reciprocal(f0_e[:, j % 2, :], f0_s[:, :]))
                e.scalar_tensor_tensor(out=f0_s[:, :], in0=ring_of(2 * j, c0), scalar=f0_b12[:, j:j + 1],
                                       in1=f0_e[:, j % 2, :], op0=ALU.add, op1=ALU.mult).then_inc(g_free, 1)
                e.wait_ge(g_full, c0.g + 2 * j + 2)
                e.wait_ge(g_free, c0.g + 2 * j + 1)
                e.scalar_tensor_tensor(out=f0_g[:, :], in0=ring_of(2 * j + 1, c0), scalar=f0_b12[:, 4 + j:5 + j],
                                       in1=f0_s[:, :], op0=ALU.add, op1=ALU.mult).then_inc(g_free, 1)
                e.wait_ge(s_f0hi, j + 1)
                e.tensor_tensor(f_h[1][:, j, :], f0_g[:, :], f_h[0][:, j, :].bitcast(F32),
                                ALU.subtract).then_inc(s_f0lo, 1)
            add_row(e, f_rowb[:, :], link)
            add_to_x(e, 8, c0)

        c1 = START["f1"]

        def f1_sp(e):
            load(e, "kv", c1.kv, A["f1_wa"], ("kv", c1.kv), cols=136)
            load(e, "q", c1.q, A["f1_wb"], ("o", c1.o))
            e.wait_ge(g_full, c1.g - 4)
            e.dma_start(f_rowb[:, :], A["f1_bb"]).then_inc(s_lay, 16)
            e.dma_start(f1_br[:, :], A["f1_br"]).then_inc(s_lay, 16)
            load(e, "o", c1.o, A["f1_lb"], ("q", c1.q + 1), cols=128)

        def f1_pool_first(e):
            split_all(e, "kv", c1.kv, c1.g - 8, cols=136)
            split_all(e, "q", c1.q, c1.g - 8)

        def f1_pool(e):
            split_all(e, "o", c1.o, c1.g - 4, cols=128)

        s_f1h = sem("f1_experts_weighted")

        def f1_pe(e):
            e.wait_ge(w_rdy["kv"], 8 * (c1.kv + 1))
            token_gemm(e, 0, c1, xT_of, lambda k: planes(W["kv"], slice(None), k, slice(0, 136)), range(DK), 136)
            e.wait_ge(w_rdy["q"], 8 * (c1.q + 1))
            token_gemm(e, 4, c1, xT_of, lambda k: planes(W["q"], slice(None), k, slice(None)), range(DK))
            e.wait_ge(s_f1h, TT)
            o = take_bank(e, 8, c1)
            for t in range(TT):
                mm = e.transpose(o[:, t * P:(t + 1) * P], f1_h[:, t, :], ident[:, :])
            mm.then_inc(g_full, 1)
            e.wait_ge(g_free, c1.g + 9)
            e.wait_ge(w_rdy["o"], 8 * (c1.o + 1))
            for t in range(TT):
                o = take_bank(e, 9 + t, c1)
                mm = passes(e, o.rearrange("p (a n) -> p a n", a=4), planes(f1_ht, slice(None), slice(t * P, (t + 1) * P)),
                            planes(W["o"], slice(None), slice(None), slice(0, 128)), True, True)
                mm.then_inc(g_full, 1)

        def f1_act(e):
            hi_act(e, f1_ht[0][:, :], ring_of(8, c1), c1.g + 8)

        def f1_dve(e, link):
            e.wait_ge(s_lay, LAY["f1"])
            for t in range(TT):
                e.wait_ge(g_full, c1.g + t + 1)
                e.tensor_tensor(f1_z[:, t, :], ring_of(t, c1)[:, 128:136], f1_br[:, :], ALU.add)
                e.tensor_copy(f1_h[:, t, :], ring_of(t, c1)[:, 0:128]).then_inc(g_free, 1)
            e.wait_ge(g_free, c1.g + 4)
            for t in range(TT):
                last = e.max(f1_zs[:, t, :], f1_z[:, t, :])
            link(last)
            link(e.tensor_copy(f1_c[:, :, 0:1], f1_zs[:, :, 0:1]))
            for k in range(1, 8):
                link(e.tensor_tensor(f1_c[:, :, k:k + 1], f1_c[:, :, k - 1:k], f1_zs[:, :, k:k + 1], ALU.add))
            for k in range(8):
                last = e.tensor_scalar(f1_zs[:, :, k:k + 1], f1_c[:, :, k:k + 1], -1.0, 1.0 / (k + 1), ALU.add, ALU.mult)
            link(last)
            link(e.tensor_reduce(f1_tau[:, :], f1_zs[:, :, :], AX.X, ALU.max))
            link(e.tensor_tensor(f1_w[:, :, :], f1_z[:, :, :], f1_tau[:, :].unsqueeze(2).to_broadcast([P, TT, 8]), ALU.subtract))
            link(e.tensor_scalar(f1_w[:, :, :], f1_w[:, :, :], 0.0, None, ALU.max))
            for t in range(TT):
                hv = f1_h[:, t, :].rearrange("p (e r) -> p e r", e=8)
                e.tensor_tensor(hv, hv, f1_w[:, t, :].unsqueeze(2).to_broadcast([P, 8, 16]), ALU.mult).then_inc(s_f1h, 1)
            add_row(e, f_rowb[:, :], link)
            add_to_x(e, 4, c1)
            lo_dve(e, f1_ht[1][:, :], f1_ht[0][:, :], ring_of(8, c1), c1.hi)
            add_to_x(e, 9, c1)

        c2 = START["f2"]
        s_f2m, s_f2e = sem("f2_max"), sem("f2_exp")

        def f2_sp(e):
            load(e, "kv", c2.kv, A["f2_wr"], ("kv", c2.kv), cols=64)
            for half in range(2):
                load(e, "q", c2.q + half, A["f2_wa"][0] if half == 0 else A["f2_wb"][0], ("o", c2.o + half))
                load(e, "o", c2.o + half, A["f2_wa"][1] if half == 0 else A["f2_wb"][1], ("q", c2.q + half + 1))

        def f2_pool_first(e):
            split_all(e, "kv", c2.kv, c2.g - 8, cols=64)
            split_all(e, "q", c2.q, c2.g - 8)

        def f2_pool(e):
            split_all(e, "o", c2.o, c2.g - 4)
            split_all(e, "q", c2.q + 1, c2.g + 5)
            split_all(e, "o", c2.o + 1, c2.g + 9)

        def f2_pe(e):
            e.wait_ge(w_rdy["kv"], 8 * (c2.kv + 1))
            o = take_bank(e, 0, c2)
            for t in range(TT):
                for d in range(DK):
                    mm = passes(e, o[:, t * 64:(t + 1) * 64], xT_of(d, t), planes(W["kv"], slice(None), d, slice(0, 64)),
                                d == 0, d == DK - 1)
            mm.then_inc(g_full, 1)
            for half, role in enumerate(("q", "o")):
                e.wait_ge(w_rdy[role], 8 * ((c2.q, c2.o)[half] + 1))
                token_gemm(e, 1 + 4 * half, c2, xT_of, lambda k: planes(W[role], slice(None), k, slice(None)), range(DK))
            for half in range(2):
                e.wait_ge(g_free, c2.g + 5 + 4 * half)
                turn_pe(e, f2_tok[:, half, :, :], c2.g + 9 + 4 * half)
            e.wait_ge(w_rdy["q"], 8 * (c2.q + 2))
            e.wait_ge(w_rdy["o"], 8 * (c2.o + 2))
            e.wait_ge(g_free, c2.g + 17)
            token_gemm(e, 17, c2, lambda k, t: planes(f2_h[k // 4], slice(None), k % 4, slice(t * P, (t + 1) * P)),
                       lambda k: planes(W["qo"[k // 4]], slice(None), k % 4, slice(None)), range(8))

        def f2_act(e):
            for t in range(TT):
                e.wait_ge(s_f2m, 1)
                e.activation(f2_g[:, t, :], f2_s[:, t, :], ACT.Exp, bias=f2_nm[:, t:t + 1]).then_inc(s_f2e, 1)
            for half in range(2):
                turn_act(e, c2.g + 9 + 4 * half, c2.hi + 4 * half, f2_h[half])

        def f2_dve(e, link):
            e.wait_ge(g_full, c2.g + 1)
            e.tensor_copy(f2_s[:, :, :].rearrange("p t k -> p (t k)"), ring_of(0, c2)[:, 0:256]).then_inc(g_free, 1)
            e.wait_ge(g_free, c2.g + 1)
            for src, k, dst in ((f2_s, 0, f2_a), (f2_a, 1, f2_b)):
                for t in range(TT):
                    last = e.max(f2_m[:, t, k, :], src[:, t, :])
                link(last)
                for t in range(TT):
                    last = e.match_replace(dst[:, t, :], f2_m[:, t, k, :], src[:, t, :], -F32_MAX)
                link(last)
            e.tensor_scalar(f2_nm[:, :], f2_m[:, :, 0, 0], -1.0, None, ALU.mult).then_inc(s_f2m, 1)
            link(e.tensor_tensor(f2_a[:, :, :], f2_b[:, :, :], f2_s[:, :, :], ALU.not_equal))
            e.wait_ge(s_f2e, TT)
            link(e.tensor_tensor(f2_g[:, :, :], f2_g[:, :, :], f2_a[:, :, :], ALU.mult))
            link(e.tensor_reduce(f2_sum[:, :], f2_g[:, :, :], AX.X, ALU.add))
            link(e.reciprocal(f2_r[:, :], f2_sum[:, :]))
            for t in range(TT):
                last = e.tensor_scalar(f2_g[:, t, :], f2_g[:, t, :], f2_r[:, t:t + 1], 2.0, ALU.mult, ALU.mult)
            link(last)
            for half in range(2):
                for t in range(TT):
                    n = 1 + 4 * half + t
                    e.wait_ge(g_full, c2.g + n + 1)
                    e.tensor_tensor(f2_tok[:, half, t, :].rearrange("p (k r) -> p k r", r=16),
                                    ring_of(n, c2).rearrange("p (k r) -> p k r", r=16),
                                    f2_g[:, t, 32 * half:32 * half + 32].unsqueeze(2).to_broadcast([P, 32, 16]),
                                    ALU.mult).then_inc(g_free, 1)
            for half in range(2):
                turn_dve(e, c2.g + 9 + 4 * half, c2.hi + 4 * half, f2_h[half])
            add_to_x(e, 17, c2)

        c3 = START["l3"]
        s3 = {n: sem(f"l3_{n}") for n in ("S", "max", "exp", "T", "thi", "tlo", "pv", "oout", "mask", "hi", "k")}

        def l3_sp(e):
            load(e, "kv", c3.kv, A["l3_wkv"][0], ("kv", c3.kv), cols=192)
            load(e, "q", c3.q, A["l3_wq"][0], ("o", c3.o))
            e.wait_ge(g_full, c3.g - 4)
            e.dma_start(l3m8[:, :, :], A["l3_mask"]).then_inc(s_lay, 16)
            e.dma_start(l3sel[:, :], A["l3_sel"]).then_inc(s_lay, 16)
            load(e, "kv", c3.kv + 1, A["l3_wkv"][1], ("kv", c3.kv + 1), cols=192)
            load(e, "q", c3.q + 1, A["l3_wq"][1], ("q", c3.q + 1))
            load(e, "o", c3.o, A["l3_wo"], ("q", c3.q + 2))

        def l3_pool_first(e):
            split_all(e, "kv", c3.kv, c3.g - 8, cols=192)
            split_all(e, "q", c3.q, c3.g - 4)

        def l3_pool(e):
            split_all(e, "kv", c3.kv + 1, c3.g + 8, cols=192)
            split_all(e, "q", c3.q + 1, c3.g + 8)
            split_all(e, "o", c3.o, c3.g - 4)

        def l3_tile(i):
            bq, idx = i // 16, i % 16
            return bq // 2, bq % 2, idx // 4, idx % 4

        def l3_pe(e):
            for G in range(2):
                n = 8 * G
                e.wait_ge(w_rdy["kv"], 8 * (c3.kv + G + 1))
                for b in range(B):
                    o = take_bank(e, n + b, c3)
                    for d in range(DK):
                        mm = passes(e, o, planes(W["kv"], slice(None), d, slice(0, P)),
                                    planes(cT, slice(None), d, slice(b * SK, (b + 1) * SK)), d == 0, d == DK - 1)
                    mm.then_inc(g_full, 1)
                for b in range(B):
                    o = take_bank(e, n + 2 + b, c3)
                    for t in range(4):
                        for d in range(DK):
                            mm = passes(e, o[:, t * 64:(t + 1) * 64],
                                        planes(cT, slice(None), d, slice(b * SK + t * P, b * SK + (t + 1) * P)),
                                        planes(W["kv"], slice(None), d, slice(P, 192)), d == 0, d == DK - 1)
                    mm.then_inc(g_full, 1)
                e.wait_ge(w_rdy["q"], 8 * (c3.q + G + 1))
                for m in range(4):
                    o = take_bank(e, n + 4 + m, c3)
                    for d in range(DK):
                        mm = passes(e, o, planes(W["q"], slice(None), d, slice(m * P, (m + 1) * P)),
                                    planes(xT, slice(None), d, slice(None)), d == 0, d == DK - 1)
                    mm.then_inc(g_full, 1)
                e.wait_ge(g_free, c3.g + n + 8)
                k0 = G * L3_TILES
                for i in range(L3_PIPE):
                    if i < L3_TILES:
                        b, qt, m, g = l3_tile(i)
                        if i >= 2:
                            e.wait_ge(s3["max"], k0 + i - 1)
                        for y in range(2):
                            mm = e.matmul(ps_s[i % 2][:, 0, :],
                                          l3x[32 * g:32 * g + 32, m, b * SQ + qt * P:b * SQ + (qt + 1) * P],
                                          l3y[y][32 * g:32 * g + 32, b * SK:(b + 1) * SK], start=y == 0, stop=y == 1)
                        mm.then_inc(s3["S"], 1)
                    j = i - 2
                    if 0 <= j < L3_TILES:
                        e.wait_ge(s3["exp"], k0 + j + 1)
                        if k0 + j >= 3:
                            e.wait_ge(s3["tlo"], k0 + j - 2)
                        for k in range(4):
                            mm = e.transpose(ps_t[j % 3][:, k * P:(k + 1) * P], l3p[:, j % 3, k * P:(k + 1) * P], ident[:, :])
                        mm.then_inc(s3["T"], 1)
                    j = i - 4
                    if 0 <= j < L3_TILES:
                        b, qt, m, g = l3_tile(j)
                        e.wait_ge(s3["tlo"], k0 + j + 1)
                        if j % 16 == 0 and k0 + j:
                            e.wait_ge(s3["oout"], (k0 + j) // 16)
                        o = ps_o[:, (j % 16) * 32:(j % 16) * 32 + 32]
                        for k in range(4):
                            for y in range(2):
                                mm = e.matmul(o, l3pt[j % 2][y][:, k, :],
                                              l3v[:, b * 4 + k, g, :, :].rearrange("p a d -> p (a d)"),
                                              start=k == 0 and y == 0, stop=k == 3 and y == 1)
                        mm.then_inc(s3["pv"], 1)
            e.wait_ge(s3["oout"], 8)
            turn_pe(e, xn, c3.g + 16)
            e.wait_ge(w_rdy["o"], 8 * (c3.o + 1))
            e.wait_ge(g_free, c3.g + 20)
            token_gemm(e, 20, c3, xT_of, lambda k: planes(W["o"], slice(None), k, slice(None)), range(4))

        def l3_act(e):
            hc = c3.hi
            for G in range(2):
                n = c3.g + 8 * G
                for b in range(B):
                    hi_act(e, l3y[0][:, b * SK:(b + 1) * SK], ring[(n + b) % 4], n + b)
                for b in range(B):
                    hi_act(e, l3v[:, b * 4:b * 4 + 4, :, 0, :],
                           ring[(n + 2 + b) % 4][:, 0:256].rearrange("p (t g d) -> p t g d", t=4, d=16), n + 2 + b)
                for m in range(4):
                    if m >= 2:
                        e.wait_ge(g_free, n + 4 + m - 1)
                    hi_act(e, l3t[:, m % 2, :], ring[(n + 4 + m) % 4], n + 4 + m, 0.25)
                k0 = G * L3_TILES
                for i in range(L3_PIPE):
                    j = i - 3
                    if 0 <= j < L3_TILES:
                        e.wait_ge(s3["T"], k0 + j + 1)
                        if k0 + j >= 2:
                            e.wait_ge(s3["pv"], k0 + j - 1)
                        e.activation(l3pt[j % 2][0][:, :, :].rearrange("p k q -> p (k q)"), ps_t[j % 3][:, :],
                                     ACT.Copy).then_inc(s3["thi"], 1)
                    if i < L3_TILES:
                        e.wait_ge(s3["max"], k0 + i + 1)
                        e.activation(l3p[:, i % 3, :], l3p[:, i % 3, :], ACT.Exp, bias=l3nm[:, i:i + 1], scale=-1.0,
                                     accum_out=l3rs[:, i:i + 1]).then_inc(s3["exp"], 1)
            turn_act(e, c3.g + 16, hc + 16, xT)

        def l3_dve(e, link):
            e.wait_ge(s_lay, LAY["l3"])
            link(e.tensor_scalar(l3mask[:, :, :], l3m8[:, :, :], -1.0, -NEG, ALU.add, ALU.mult))
            for G in range(2):
                n = 8 * G
                h0 = c3.hi + 8 * G
                for b in range(B):
                    lo_dve(e, l3y[1][:, b * SK:(b + 1) * SK], l3y[0][:, b * SK:(b + 1) * SK], ring_of(n + b, c3), h0 + b)
                for b in range(B):
                    e.wait_ge(g_hi, h0 + 2 + b + 1)
                    e.tensor_tensor(l3v[:, b * 4:b * 4 + 4, :, 1, :],
                                    ring_of(n + 2 + b, c3)[:, 0:256].rearrange("p (t g d) -> p t g d", t=4, d=16),
                                    l3v[:, b * 4:b * 4 + 4, :, 0, :].bitcast(F32), ALU.subtract).then_inc(g_free, 1)
                for m in range(4):
                    e.wait_ge(g_hi, h0 + 4 + m + 1)
                    link(e.tensor_scalar(l3k[:, m % 2, :], ring_of(n + 4 + m, c3), l3sel[:, 0:1], None, ALU.mult))
                    e.scalar_tensor_tensor(out=l3x[:, m, :], in0=l3t[:, m % 2, :].bitcast(F32), scalar=l3sel[:, 1:2],
                                           in1=l3k[:, m % 2, :], op0=ALU.mult, op1=ALU.add).then_inc(g_free, 1)
                k0 = G * L3_TILES
                for i in range(L3_PIPE + 1):
                    if i < L3_TILES:
                        b, qt, m, g = l3_tile(i)
                        e.wait_ge(s3["S"], k0 + i + 1)
                        if k0 + i >= 3:
                            e.wait_ge(s3["T"], k0 + i - 2)
                        e.tensor_tensor_reduce(out=l3p[:, i % 3, :], in0=ps_s[i % 2][:, 0, :], in1=l3mask[:, qt, :],
                                               scale=-1.0, scalar=F32_MAX, op0=ALU.add, op1=ALU.min,
                                               accum_out=l3nm[:, i:i + 1]).then_inc(s3["max"], 1)
                    j = i - 3
                    if 0 <= j < L3_TILES:
                        e.wait_ge(s3["thi"], k0 + j + 1)
                        e.tensor_tensor(l3pt[j % 2][1][:, :, :].rearrange("p k q -> p (k q)"), ps_t[j % 3][:, :],
                                        l3pt[j % 2][0][:, :, :].rearrange("p k q -> p (k q)").bitcast(F32),
                                        ALU.subtract).then_inc(s3["tlo"], 1)
                    j = i - 5
                    if 0 <= j < L3_TILES and j % 16 == 15:
                        bq = j // 16
                        e.wait_ge(s3["pv"], k0 + j + 1)
                        acc = ps_o[:, :].rearrange("p (h a d) -> p h a d", a=2, d=16)
                        dst = xn[:, bq, G * 256:(G + 1) * 256].rearrange("p (h d) -> p h d", d=16)
                        half = l3half[:, :].rearrange("p (h d) -> p h d", d=16)
                        e.reciprocal(l3ri[:, :], l3rs[:, bq * 16:bq * 16 + 16])
                        link(e.tensor_copy(half, acc[:, :, 1, :]))
                        e.tensor_tensor(half, acc[:, :, 0, :], half, ALU.add).then_inc(s3["k"], 1)
                        e.wait_ge(s3["k"], G * 4 + bq + 1)
                        e.tensor_tensor(dst, half, l3ri[:, :].unsqueeze(2).to_broadcast([P, 16, 16]), ALU.mult)\
                            .then_inc(s3["oout"], 1)
            turn_dve(e, c3.g + 16, c3.hi + 16, xT)
            add_to_x(e, 20, c3)

        cf = START["f3"]
        s4 = {n: sem(f"f3_{n}") for n in ("A", "B", "C", "turned", "out", "b1", "qx", "xo", "row", "diag",
                                         "srow", "bias", "hi", "lo", "used", "acc", "hq", "fin", "pw")}

        def f3_sp(e):
            e.wait_ge(g_full, cf.g - 4)
            e.dma_start(q_b1[:, :], A["f3_b1"]).then_inc(s_lay, 16)
            for cc in range(8):
                if cc:
                    e.wait_ge(s4["C"], cc)
                e.dma_start(q_nat[:, :], A["f3_w1n"][cc] if cc < 4 else A["f3_w2n"][cc - 4]).then_inc(s_nat, 16)
            for cc in range(8):
                role = "qo"[cc % 2]
                src = A["f3_w1"][cc] if cc < 4 else A["f3_w2"][cc - 4]
                before = ("o", cf.o + cc // 2) if role == "q" else ("q", cf.q + cc // 2 + 1)
                load(e, role, (cf.q if role == "q" else cf.o) + cc // 2, src, before)
            e.wait_ge(s4["fin"], TT)
            e.dma_start(out.rearrange("b (t p) d -> p (b t) d", p=P), x[:, :, :]).then_inc(s_out, 16)
            e.wait_ge(s_out, 16)

        def f3_pool(e):
            def used(cc):
                if cc < 2:
                    return cf.g - 4
                return cf.g + 3 + 8 * (cc - 1)
            for cc in range(2):
                split_all(e, "qo"[cc % 2], (cf.q, cf.o)[cc % 2] + cc // 2, used(cc))
            for cc in range(2, 6):
                split_all(e, "qo"[cc % 2], (cf.q, cf.o)[cc % 2] + cc // 2, used(cc))
            for cc in range(6, 8):
                e.wait_ge(s4["used"], 4 * (cc - 5))
                split_all(e, "qo"[cc % 2], (cf.q, cf.o)[cc % 2] + cc // 2, cf.g)

        def f3_pe(e):
            for cc in range(8):
                e.wait_ge(s4["C"], cc + 1)
                for part in range(2):
                    n = 2 * cc + part
                    if n >= 2:
                        e.wait_ge(s4["out"], n - 1)
                    for k in range(8):
                        if cc < 4:
                            src = q_int[:, (k % 4) * 512 + (2 * part + k // 4) * P:(k % 4) * 512 + (2 * part + k // 4 + 1) * P]
                        else:
                            src = q_int[:, (8 * part + k) * P:(8 * part + k + 1) * P]
                        mm = e.transpose(ps_t[n % 2][:, :].bitcast(BF16)[:, k * P:(k + 1) * P], src, identb[:, :])
                    mm.then_inc(s4["turned"], 1)
            g = 0

            def rows(src_sem, src_count, g, which):
                e.wait_ge(src_sem, src_count)
                o = take_bank(e, g, cf)
                for t in range(TT):
                    mm = e.transpose(o[:, t * P:(t + 1) * P], q_amx[:, t * P:(t + 1) * P], ident[:, :])
                mm.then_inc(g_full, 1)
                spread(g + 1, which)

            def spread(g, which):
                e.wait_ge(s4["diag"], which + 1)
                o = take_bank(e, g, cf)
                for t in range(TT):
                    mm = e.matmul(o[:, t * P:(t + 1) * P], ones[:, :], diag4[:, t, :], start=True, stop=True)
                mm.then_inc(g_full, 1)
            spread(0, 0)
            rows(s4["row"], 1, 1, 1)
            e.wait_ge(s4["qx"], DK)
            e.wait_ge(s4["xo"], 1)
            for j in range(HT):
                n = 3 + 2 * j
                o = take_bank(e, n, cf)
                for d in range(DK):
                    mm = e.matmul(o, q_w1[:, d, j * P:(j + 1) * P], xq[:, d, :], start=d == 0, stop=d == DK - 1)
                mm.then_inc(g_full, 1)
                cc, role = j // 4, "qo"[(j // 4) % 2]
                e.wait_ge(w_rdy[role], 8 * ((cf.q, cf.o)[cc % 2] + cc // 2 + 1))
                o = take_bank(e, n + 1, cf)
                for d in range(DK):
                    mm = passes(e, o, planes(W[role], slice(None), d, slice((j % 4) * P, (j % 4 + 1) * P)),
                                planes(xT, slice(None), d, slice(None)), d == 0, d == DK - 1)
                mm.then_inc(g_full, 1)
            rows(s4["row"], 2, 35, 2)
            e.wait_ge(g_free, cf.g + 37)
            acc_i = [ps_t[0][:, :], ps_t[1][:, :], ps_t[2][:, :], ps_o[:, :]]
            for hb in range(HT):
                cc, role = 4 + hb // 4, "qo"[(hb // 4) % 2]
                e.wait_ge(w_rdy[role], 8 * ((cf.q, cf.o)[cc % 2] + cc // 2 + 1))
                e.wait_ge(s4["lo"], hb + 1)
                for t in range(TT):
                    mm = passes(e, ring[t], planes(ho, slice(None), hb % 4, slice(t * P, (t + 1) * P)),
                                planes(W[role], slice(None), hb % 4, slice(None)), hb == 0, hb == HT - 1)
                mm.then_inc(s4["used"], 1)
                e.wait_ge(s4["hq"], hb + 1)
                for t in range(TT):
                    mm = e.matmul(acc_i[t], hq[:, hb, t * P:(t + 1) * P], q_w2[:, hb, :], start=hb == 0, stop=hb == HT - 1)
            mm.then_inc(s4["acc"], 1)

        def f3_act(e):
            for cc in range(8):
                e.wait_ge(s4["B"], cc + 1)
                if cc:
                    e.wait_ge(s4["turned"], 2 * cc)
                e.activation(q_int[:, :], q_nat[:, :], ACT.Copy, bias=-MAGIC).then_inc(s4["C"], 1)
                for part in range(2):
                    n = 2 * cc + part
                    e.wait_ge(s4["turned"], n + 1)
                    src = ps_t[n % 2][:, :].bitcast(BF16).rearrange("p (k w) -> p k w", k=2 if cc < 4 else 8)
                    dst = q_w1[:, 2 * part:2 * part + 2, cc * 512:(cc + 1) * 512] if cc < 4 else \
                        q_w2[:, 8 * part:8 * part + 8, (cc - 4) * P:(cc - 3) * P]
                    e.activation(dst, src, ACT.Copy).then_inc(s4["out"], 1)
            e.wait_ge(s_lay, LAY["f3"])
            for j in range(HT):
                e.wait_ge(g_free, cf.g + 3 + 2 * j + 2)
                e.activation(h[:, j, :], h[:, j, :], ACT.Identity, bias=q_b1[:, j:j + 1]).then_inc(s4["bias"], 1)
            e.wait_ge(s4["row"], 2)
            for hb in range(HT):
                if hb >= 4:
                    e.wait_ge(s4["used"], hb - 3)
                e.activation(ho[0][:, hb % 4, :], h[:, hb, :], ACT.Copy, scale=q_mo[:, hb:hb + 1]).then_inc(s4["hi"], 1)

        def f3_dve(e, link):
            e.memset(ones[:, :], 1.0)
            link(e.tensor_copy(identb[:, :], ident[:, :]))
            for cc in range(8):
                e.wait_ge(s_nat, 16 * (cc + 1))
                if cc < 4:
                    am, sw, w = q_am[:, 4 * cc:4 * cc + 4], q_sw1[:, 4 * cc:4 * cc + 4], 4
                else:
                    am, sw, w = q_am[:, 4 * cc:4 * cc + 1], q_sw2[:, cc - 4:cc - 3], 1
                link(e.tensor_reduce(am, q_nat[:, :].rearrange("p (a n) -> p a n", a=w), AX.X, ALU.max,
                                     apply_absolute_value=True))
                link(e.tensor_scalar(sw, am, 1.0 / 127.0, 1e-8, ALU.mult, ALU.max))
                link(e.reciprocal(q_cm[:, 0:w], sw))
                for a in range(w):
                    v = q_nat[:, a * (2048 // w):(a + 1) * (2048 // w)]
                    last = e.tensor_scalar(v, v, q_cm[:, a:a + 1], MAGIC, ALU.mult, ALU.add)
                link(last)
                e.tensor_scalar(q_nat[:, :], q_nat[:, :], MAGIC + 127.0, MAGIC - 127.0, ALU.min, ALU.max).then_inc(s4["B"], 1)

            def largest(v, tiles):
                e.memset(q_amn[:, :], 0.0)
                link(e.memset(q_amx[:, :], 0.0))
                for j in range(tiles):
                    for row, op in ((q_amx, ALU.max), (q_amn, ALU.min)):
                        last = e.scalar_tensor_tensor(out=row[:, :], in0=v[:, j, :], scalar=q_mi[:, j:j + 1],
                                                      in1=row[:, :], op0=ALU.mult, op1=op)
                    link(last)
                e.scalar_tensor_tensor(out=q_amx[:, :], in0=q_amn[:, :], scalar=-1.0, in1=q_amx[:, :],
                                       op0=ALU.mult, op1=ALU.max).then_inc(s4["row"], 1)

            def make_diag(scales, which):
                for t in range(4):
                    last = e.tensor_scalar(diag4[:, t, :], ident[:, :], scales[:, t:t + 1], None, ALU.mult)
                last.then_inc(s4["diag"], 1)

            def token_scales(g, which):
                e.wait_ge(g_full, cf.g + g + 1)
                e.tensor_reduce(q_tm[:, :], ring_of(g, cf).rearrange("p (t n) -> p t n", t=TT), AX.X, ALU.max).then_inc(g_free, 1)
                e.wait_ge(g_free, cf.g + g + 1)
                link(e.tensor_scalar(q_ts[:, :], q_tm[:, :], 1.0 / 127.0, 1e-8, ALU.mult, ALU.max))
                make_diag(q_ts, which)
                e.wait_ge(g_full, cf.g + g + 2)
                e.tensor_copy(q_srow[:, :], ring_of(g + 1, cf)).then_inc(g_free, 1)
                e.wait_ge(g_free, cf.g + g + 2)
                link(e.reciprocal(q_rrow[:, :], q_srow[:, :]))

            def quantise(dst, src, keep, i, done):
                t = q_t[:, i % 2, :]
                link(e.scalar_tensor_tensor(out=t, in0=src, scalar=keep, in1=q_rrow[:, :], op0=ALU.mult, op1=ALU.mult))
                link(e.tensor_scalar(t, t, MAGIC, MAGIC + 127.0, ALU.add, ALU.min))
                e.tensor_scalar(dst, t, MAGIC - 127.0, -MAGIC, ALU.max, ALU.add).then_inc(done, 1)

            make_diag(q_sw2, 0)
            e.wait_ge(g_full, cf.g + 1)
            e.tensor_copy(q_s2row[:, :], ring_of(0, cf)).then_inc(g_free, 1)
            link(e.tensor_tensor(xF[:, :, :].rearrange("p d t -> p (d t)"),
                                 xT[0][:, :, :].rearrange("p d t -> p (d t)").bitcast(F32),
                                 xT[1][:, :, :].rearrange("p d t -> p (d t)").bitcast(F32), ALU.add))
            link(e.tensor_reduce(q_cm[:, 0:DK], xF[:, :, :], AX.X, ALU.max, apply_absolute_value=True))
            e.tensor_scalar(q_mo[:, 0:DK], q_cm[:, 0:DK], 3.0, None, ALU.is_gt)
            link(e.tensor_scalar(q_mi[:, 0:DK], q_cm[:, 0:DK], 3.0, None, ALU.is_le))
            largest(xF, DK)
            for d in range(DK):
                for y in range(2):
                    last = e.tensor_scalar(xT[y][:, d, :], xT[y][:, d, :].bitcast(F32), q_mo[:, d:d + 1], None, ALU.mult)
            last.then_inc(s4["xo"], 1)
            token_scales(1, 1)
            for d in range(DK):
                quantise(xq[:, d, :], xF[:, d, :], q_mi[:, d:d + 1], d, s4["qx"])
            for j in range(HT):
                n = 3 + 2 * j
                e.wait_ge(g_full, cf.g + n + 1)
                e.tensor_tensor(q_t[:, j % 2, :], ring_of(n, cf), q_srow[:, :], ALU.mult).then_inc(g_free, 1)
                e.wait_ge(g_full, cf.g + n + 2)
                e.wait_ge(g_free, cf.g + n + 1)
                e.scalar_tensor_tensor(out=h[:, j, :], in0=q_t[:, j % 2, :], scalar=q_sw1[:, j:j + 1], in1=ring_of(n + 1, cf),
                                       op0=ALU.mult, op1=ALU.add).then_inc(g_free, 1)
                if j % 4 == 3:
                    e.wait_ge(s4["bias"], j - 3)
            for j in range(0, HT, 4):
                e.wait_ge(s4["bias"], j + 4)
                last = e.tensor_reduce(q_cm[:, j:j + 4], h[:, j:j + 4, :], AX.X, ALU.max, apply_absolute_value=True)
            link(last)
            e.tensor_scalar(q_mo[:, :], q_cm[:, :], 3.0, None, ALU.is_gt)
            link(e.tensor_scalar(q_mi[:, :], q_cm[:, :], 3.0, None, ALU.is_le))
            largest(h, HT)
            token_scales(35, 2)
            for hb in range(HT):
                e.wait_ge(s4["hi"], hb + 1)
                e.scalar_tensor_tensor(out=ho[1][:, hb % 4, :], in0=h[:, hb, :], scalar=q_mo[:, hb:hb + 1],
                                       in1=ho[0][:, hb % 4, :].bitcast(F32), op0=ALU.mult, op1=ALU.subtract)\
                    .then_inc(s4["lo"], 1)
                quantise(hq[:, hb, :], h[:, hb, :], q_mi[:, hb:hb + 1], hb, s4["hq"])
            e.wait_ge(s_lay, LAY["f3"])
            add_row(e, q_b2[:, :], link)
            e.wait_ge(s4["acc"], 1)
            acc_i = [ps_t[0][:, :], ps_t[1][:, :], ps_t[2][:, :], ps_o[:, :]]
            for t in range(TT):
                e.scalar_tensor_tensor(out=q_t[:, t % 2, :], in0=acc_i[t], scalar=q_ts[:, t:t + 1], in1=q_s2row[:, :],
                                       op0=ALU.mult, op1=ALU.mult)
                link(e.tensor_tensor(x[:, t, :], ring[t], x[:, t, :], ALU.add))
                e.tensor_tensor(x[:, t, :], x[:, t, :], q_t[:, t % 2, :], ALU.add).then_inc(s4["fin"], 1)

        norms = [Norm(i) for i in range(8)]
        a0 = Attention(L0, A, None)
        a1 = Attention(L1, A, ("q", START["l1"].q))
        a2 = Attention(L2, A, ("o", START["l2"].o))
        LAY = {"l0": 16 * 3, "f0": 16 * 5, "f1": 16 * 7, "l3": 16 * 9, "f3": 16 * 11}

        block = ctx.enter_context(nc.Block())

        @block.sync
        def _(e):
            e.dma_start(x[:, :, :], A["x"]).then_inc(s_x, 16)
            e.dma_start(ident[:, :], A["ident"]).then_inc(s_const, 16)
            e.dma_start(craw[:, :, :], A["ctxT"]).then_inc(s_ctx, 16)
            a0.sp_first(e)
            e.wait_ge(s_csplit, 8)
            e.dma_start(SP["l0"].cos[:, :], A["cos"]).then_inc(s_lay, 16)
            e.dma_start(SP["l0"].sin[:, :], A["sin"]).then_inc(s_lay, 16)
            e.dma_start(SP["l0"].mask[:, :, :], A["l0_mask"]).then_inc(s_lay, 16)
            a0.sp(e)
            f0_sp(e)
            a1.sp_first(e)
            a1.sp(e)
            f1_sp(e)
            a2.sp_first(e)
            a2.sp(e)
            f2_sp(e)
            l3_sp(e)
            e.wait_ge(g_full, START["f3"].g - 4)
            e.dma_start(q_b2[:, :], A["f3_b2"]).then_inc(s_lay, 16)
            f3_sp(e)

        @block.gpsimd
        def _(e):
            e.memset(mhalf[:, :], -0.5).then_inc(s_plink, 1)
            e.memset(one[:, :], 1.0).then_inc(s_plink, 1)
            e.wait_ge(s_plink, 2)
            a0.pool_first(e)
            norms[0].pool(e)
            a0.pool(e)
            f0_pool_first(e)
            norms[1].pool(e)
            f0_pool(e)
            a1.pool_first(e)
            norms[2].pool(e)
            a1.pool(e)
            f1_pool_first(e)
            norms[3].pool(e)
            f1_pool(e)
            a2.pool_first(e)
            norms[4].pool(e)
            a2.pool(e)
            f2_pool_first(e)
            norms[5].pool(e)
            f2_pool(e)
            l3_pool_first(e)
            norms[6].pool(e)
            l3_pool(e)
            norms[7].pool(e)
            f3_pool(e)

        @block.tensor
        def _(e):
            e.wait_ge(s_const, 16)
            norms[0].pe(e)
            e.wait_ge(s_csplit, 8)
            e.wait_ge(g_free, 4)
            a0.pe(e)
            norms[1].pe(e)
            e.wait_ge(g_free, START["f0"].g)
            f0_pe(e)
            norms[2].pe(e)
            e.wait_ge(g_free, START["l1"].g)
            a1.pe(e)
            norms[3].pe(e)
            e.wait_ge(g_free, START["f1"].g)
            f1_pe(e)
            norms[4].pe(e)
            e.wait_ge(g_free, START["l2"].g)
            a2.pe(e)
            norms[5].pe(e)
            e.wait_ge(g_free, START["f2"].g)
            f2_pe(e)
            norms[6].pe(e)
            e.wait_ge(g_free, START["l3"].g)
            l3_pe(e)
            norms[7].pe(e)
            f3_pe(e)

        @block.scalar
        def _(e):
            e.wait_ge(s_ctx, 16)
            for d in range(DK):
                e.activation(cT[0][:, d, :], craw[:, d, :], ACT.Copy).then_inc(s_chi, 1)
            norms[0].act(e)
            a0.act(e)
            norms[1].act(e)
            f0_act(e)
            norms[2].act(e)
            a1.act(e)
            norms[3].act(e)
            f1_act(e)
            norms[4].act(e)
            a2.act(e)
            norms[5].act(e)
            f2_act(e)
            norms[6].act(e)
            l3_act(e)
            norms[7].act(e)
            f3_act(e)

        @block.vector
        def _(e):
            links = [0]

            def link(ins):
                links[0] += 1
                ins.then_inc(s_link, 1)
                e.wait_ge(s_link, links[0])
            e.wait_ge(s_x, 16)
            norms[0].dve(e, link)
            for d in range(DK):
                e.wait_ge(s_chi, d + 1)
                e.tensor_tensor(cT[1][:, d, :], craw[:, d, :], cT[0][:, d, :].bitcast(F32), ALU.subtract)\
                    .then_inc(s_csplit, 2)
            e.wait_ge(s_lay, LAY["l0"])
            a0.dve(e, link)
            norms[1].dve(e, link)
            f0_dve(e, link)
            norms[2].dve(e, link)
            a1.dve(e, link)
            norms[3].dve(e, link)
            f1_dve(e, link)
            norms[4].dve(e, link)
            a2.dve(e, link)
            norms[5].dve(e, link)
            f2_dve(e, link)
            norms[6].dve(e, link)
            l3_dve(e, link)
            norms[7].dve(e, link)
            f3_dve(e, link)

def _layout(i):
    import numpy as np

    def k_tiles(w):
        return w.reshape(-1, 128, w.shape[1]).transpose(1, 0, 2)

    def groups(w, n):
        return np.stack([k_tiles(w[:, j * (w.shape[1] // n):(j + 1) * (w.shape[1] // n)]) for j in range(n)])

    def head_rows(w, n, hd):
        return w.reshape(n, 4, hd, 512).transpose(0, 2, 1, 3)

    def rows(b):
        return np.broadcast_to(b, (128, b.shape[0]))
    a = {"x": i["x"].reshape(4, 128, 512).transpose(1, 0, 2),
         "ctxT": k_tiles(i["ctx_4096"].reshape(1024, 512).T),
         "ident": np.eye(128, dtype=np.float32),
         "l0_mask": i["mask_BxSxS2_ff0"].reshape(4, 128, 512).transpose(1, 0, 2)}
    inv = (1.0 / np.float32(10000.0) ** (np.arange(0, 128, 2, dtype=np.float32) / np.float32(128))).astype(np.float32)
    ang = (np.arange(512, dtype=np.float32)[None, :] * inv[:, None]).astype(np.float32)
    a["cos"] = np.concatenate([np.cos(ang), np.cos(ang)]).astype(np.float32)
    a["sin"] = np.concatenate([-np.sin(ang), np.sin(ang)]).astype(np.float32)
    a["l0_wq"] = groups(i["L0_xattn_wq"], 8)
    a["l0_wkv"] = np.concatenate([groups(i["L0_xattn_wk"], 8), groups(i["L0_xattn_wv"], 8)], -1)
    a["l0_wo"] = head_rows(i["L0_xattn_wo"], 8, 128)
    a["l1_wq"] = groups(i["L1_xattn_Wq"].T, 4)
    a["l1_wkv"] = np.concatenate([groups(i["L1_xattn_Wk"].T, 4), groups(i["L1_xattn_Wv"].T, 4)], -1)
    a["l1_wo"] = head_rows(i["L1_xattn_Wo"].T, 4, 96)
    a["l2_wq"] = groups(i["L2_xattn_Wq"], 8)
    a["l2_wkv"] = np.concatenate([groups(i["L2_xattn_Wk"], 4), groups(i["L2_xattn_Wv"], 4)], -1)
    a["l2_wo"] = head_rows(i["L2_xattn_Wo"], 8, 128)
    a["f0_w12"] = groups(i["L0_ffn_w12"].T, 2)
    a["f0_w3"] = k_tiles(i["L0_ffn_w3"].T)
    a["f0_b12"] = i["L0_ffn_b12"].reshape(8, 128).T
    a["f0_b3"] = rows(i["L0_ffn_b3"])
    a["f1_wb"] = k_tiles(i["L1_ffn_W_base"].T)
    a["f1_bb"] = rows(i["L1_ffn_b_base"])
    a["f1_br"] = rows(i["L1_ffn_b_router"])
    a["f1_wa"] = k_tiles(np.concatenate([i["L1_ffn_lora_A"].transpose(1, 0, 2).reshape(512, 128), i["L1_ffn_W_router"].T], 1))
    a["f1_lb"] = i["L1_ffn_lora_B"].reshape(128, 4, 128)
    a["f2_wr"] = k_tiles(i["L2_ffn_Wr"].T)
    a["f2_wa"] = groups(i["L2_ffn_A"].reshape(1024, 512).T, 2)
    a["f2_wb"] = i["L2_ffn_B"].transpose(0, 2, 1).reshape(2, 4, 128, 512).transpose(0, 2, 1, 3)
    wq = i["L3_xattn_w_q"].reshape(2, 4, 4, 16, 512).transpose(0, 2, 1, 3, 4)
    wq = np.stack([wq, wq], 3).reshape(1024, 512)
    wk = i["L3_xattn_w_k"].reshape(2, 4, 16, 512)
    wk = np.stack([wk, wk], 2).reshape(256, 512)
    a["l3_wq"] = groups(wq.T, 2)
    a["l3_wkv"] = np.concatenate([groups(wk.T, 2), groups(i["L3_xattn_w_v"].T, 2)], -1)
    a["l3_wo"] = k_tiles(i["L3_xattn_w_out"].T.reshape(2, 4, 4, 16, 512).transpose(0, 2, 1, 3, 4).reshape(512, 512))
    a["l3_mask"] = i["mask_SxS2_bk0"].reshape(2, 128, 512).transpose(1, 0, 2)
    lo = (np.arange(128) % 32 >= 16).astype(np.float32)
    a["l3_sel"] = np.stack([lo * np.float32(0.25), 1 - 2 * lo], 1).astype(np.float32)
    a["f3_w1"] = groups(i["L3_ffn_W1"].T, 4)
    a["f3_w1n"] = i["L3_ffn_W1"].reshape(4, 4, 128, 512).transpose(0, 2, 1, 3).reshape(4, 128, 2048)
    a["f3_w2"] = i["L3_ffn_W2"].T.reshape(4, 4, 128, 512).transpose(0, 2, 1, 3)
    a["f3_w2n"] = i["L3_ffn_W2"].reshape(4, 128, 2048)
    a["f3_b1"] = i["L3_ffn_b1"].reshape(16, 128).T
    a["f3_b2"] = rows(i["L3_ffn_b2"])
    return {k: np.ascontiguousarray(v) for k, v in a.items()}

def kernel(**inputs):
    import numpy as _np
    import concourse.bacc as _bacc
    from concourse import mybir as _mybir
    from concourse.bass_utils import run_bass_kernel_spmd as _run

    nc = _bacc.Bacc("TRN2", target_bir_lowering=False, num_devices=1)
    arrays = _layout({k: _np.asarray(v) for k, v in inputs.items()})
    arrays = {f"in_{k}": v for k, v in arrays.items()}
    A = {k[3:]: nc.dram_tensor(k, v.shape, _mybir.dt.from_np(v.dtype), kind="ExternalInput").ap() for k, v in arrays.items()}
    out = nc.dram_tensor("out", (2, 256, 512), _mybir.dt.float32, kind="ExternalOutput").ap()
    program(nc, A, out)
    r = _run(nc, [arrays], core_ids=[0])
    return r.results[0]["out"]
```

```python
from contextlib import ExitStack

import numpy as np
import concourse.bass as bass
from concourse import mybir

ALU = mybir.AluOpType
ACT = mybir.ActivationFunctionType
AX = mybir.AxisListType
F32 = mybir.dt.float32
F32R = mybir.dt.float32r
BF16 = mybir.dt.bfloat16
U8 = mybir.dt.uint8

P = 128
B, SQ, SK, D = 2, 256, 512, 512
T = B * SQ
C = B * SK
DK = D // P
TT = T // P
HG = 4
NEG = -3.0e38
F32_MAX = 3.4028234663852886e38
MAGIC = 12582912.0
FFN_H = 2048
KB = 1024

class Layer:

    def __init__(self, name, groups, hd, self_keys, kv_every, rope):
        self.name, self.groups, self.hd, self.kv_every, self.rope = name, groups, hd, kv_every, rope
        self.self_keys = self_keys
        self.keys = SK + (SQ if self_keys else 0)
        self.kt = self.keys // P
        self.parts = 3 if self_keys else 2
        self.early = 2
        self.kv_tiles = 3 * self.parts
        self.kv_hi = 2 * self.parts
        self.pieces = [(0, 4), (4, 2)] if self_keys else [(0, 4)]
        self.scale = float(hd) ** -0.5

L0 = Layer("l0", 8, 128, False, 1, True)
L1 = Layer("l1", 4, 96, True, 1, False)
L2 = Layer("l2", 8, 128, True, 2, False)
TILES = 2 * B * HG
UNITS = B * HG
PIPE = TILES + 4
L3_TILES = 4 * 16
L3_UNITS = L3_TILES // 2
L3_PIPE = L3_TILES + 5

def program(nc, A, out):
    ctx = ExitStack()
    with ctx:
        base = nc.sbuf_base
        base = base() if callable(base) else base
        base = (base + 31) // 32 * 32

        def at(name, shape, dt, kb):
            return nc.alloc_sbuf_tensor_at(name, shape, dt, offset=base + int(kb * KB))

        def sem(name):
            return ctx.enter_context(nc.semaphore(name))

        x = at("x", [P, TT, D], F32, 0)
        xn = at("xn", [P, TT, D], F32, 8)
        xT = [at("xT_hi", [P, DK, T], F32R, 16), at("xT_lo", [P, DK, T], F32R, 24)]
        cT = [at("cT_hi", [P, DK, C], F32R, 32), at("cT_lo", [P, DK, C], F32R, 48)]
        W = {"q": [at("wq_hi", [P, 4, 512], F32R, 64), at("wq_lo", [P, 4, 512], F32R, 72)],
             "o": [at("wo_hi", [P, 4, 512], F32R, 80), at("wo_lo", [P, 4, 512], F32R, 88)],
             "kv": [at("wkv_hi", [P, 4, 256], F32R, 96), at("wkv_lo", [P, 4, 256], F32R, 100)]}
        raw_big = at("raw_big", [P, 4, 512], F32, 104)
        raw_kv = at("raw_kv", [P, 4, 256], F32, 112)
        RAW = {"q": raw_big, "o": raw_big, "kv": raw_kv}
        ident = at("ident", [P, P], F32, 116)
        st = at("st", [P, TT, 6], F32, 116.5)
        mv = at("mv", [P, TT, 2], F32, 116.625)
        veps = at("veps", [P, TT], F32, 116.6875)
        rstd = at("rstd", [P, TT], F32, 116.71875)
        mhalf = at("mhalf", [P, TT], F32, 116.75)
        one = at("one", [P, 1], F32, 117)
        nmax = at("nmax", [P, TILES], F32, 116.8125)
        rsum = at("rsum", [P, TILES], F32, 116.875)
        rinv = at("rinv", [P, TILES], F32, 116.9375)
        R0 = 117.5

        W["f"] = [at("wf_hi", [P, 4, 512], F32R, R0 + 74), at("wf_lo", [P, 4, 512], F32R, R0 + 82)]
        RAW["f"] = at("raw_f", [P, 4, 512], F32, 8)

        craw = at("craw", [P, DK, C], F32, R0 + 32)

        class Space:
            pass

        def attention_space(l):
            s = Space()
            o = R0

            def take(name, shape, dt):
                nonlocal o
                size = int(np.prod(shape[1:])) * 4
                a = at(f"{l.name}_{name}", shape, dt, o)
                o += size / KB
                return a
            s.q = [take("q_hi", [P, HG, T], F32R), take("q_lo", [P, HG, T], F32R)]
            s.k = [take("k_hi", [P, B, l.keys], F32R), take("k_lo", [P, B, l.keys], F32R)]
            s.v = [take("v_hi", [P, B, l.kt, P], F32R), take("v_lo", [P, B, l.kt, P], F32R)]
            s.pt = [[take(f"pt{i}_{n}", [P, l.kt, SQ], F32R) for n in ("hi", "lo")] for i in range(2)]
            s.ot = [take("ot_hi", [P, HG, T], F32R), take("ot_lo", [P, HG, T], F32R)]
            s.p = take("p", [P, 3, l.keys], F32)
            if l.rope:
                s.cos, s.sin = take("cos", [P, SK], F32), take("sin", [P, SK], F32)
                s.ra, s.rb = take("ra", [P, 2, 512], F32), take("rb", [P, 2, 512], F32)
                s.mask = take("mask", [P, TT, SK], F32)
            return s
        SP = {l.name: attention_space(l) for l in (L0, L1, L2)}

        l3x = at("l3_x", [P, 4, T], F32R, R0)
        l3v = at("l3_v", [P, C // P, 4, 2, 16], F32R, R0 + 8)
        l3pt = [[at(f"l3_pt{i}_{n}", [P, 4, SQ], F32R, R0 + 12 + 8 * i + 4 * j) for j, n in enumerate(("hi", "lo"))]
                for i in range(2)]
        l3p = at("l3_p", [P, 4, SK], F32, R0 + 28)
        l3mask = at("l3_mask", [P, 2, SK], F32, R0 + 36)
        l3m8 = at("l3_m8", [P, 2, SK], U8, R0 + 40)
        l3sel = at("l3_sel", [P, 2], F32, R0 + 41)
        l3ot = [at(f"l3_ot_{n}", [P, 4, T], F32R, R0 + 42 + 8 * j) for j, n in enumerate(("hi", "lo"))]
        l3y = [[at(f"l3_y{g}_{n}", [P, C], F32R, R0 + 58 + 8 * g + 4 * j) for j, n in enumerate(("hi", "lo"))]
               for g in range(4)]
        l3t = at("l3_t", [P, 2, 512], F32R, 8)
        l3k = at("l3_k", [P, 2, 512], F32, 12)

        f_rowb = at("f_rowb", [P, 512], F32, R0)
        f0_b12 = at("f0_b12", [P, 8], F32, R0 + 2)
        f0_nb = at("f0_nb", [P, 8], F32, R0 + 2.25)
        f0_e = at("f0_e", [P, 2, 512], F32, R0 + 3)
        f0_s = at("f0_s", [P, 512], F32, R0 + 7)
        f0_g = at("f0_g", [P, 512], F32, R0 + 9)
        f_h = [at("f_h_hi", [P, 4, T], F32R, R0 + 11), at("f_h_lo", [P, 4, T], F32R, R0 + 19)]
        f1_br = at("f1_br", [P, 8], F32, R0 + 2)
        f1_z = at("f1_z", [P, TT, 8], F32, R0 + 3)
        f1_zs = at("f1_zs", [P, TT, 8], F32, R0 + 3.25)
        f1_c = at("f1_c", [P, TT, 8], F32, R0 + 3.5)
        f1_tau = at("f1_tau", [P, TT], F32, R0 + 3.75)
        f1_w = at("f1_w", [P, TT, 8], F32, R0 + 4)
        f1_h = at("f1_h", [P, TT, P], F32, R0 + 5)
        f1_ht = [at("f1_ht_hi", [P, T], F32R, R0 + 7), at("f1_ht_lo", [P, T], F32R, R0 + 9)]
        f2_s = at("f2_s", [P, TT, 64], F32, R0)
        f2_a = at("f2_a", [P, TT, 64], F32, R0 + 1)
        f2_b = at("f2_b", [P, TT, 64], F32, R0 + 2)
        f2_g = at("f2_g", [P, TT, 64], F32, R0 + 3)
        f2_m = at("f2_m", [P, TT, 2, 8], F32, R0 + 4)
        f2_nm = at("f2_nm", [P, TT], F32, R0 + 4.25)
        f2_sum = at("f2_sum", [P, TT], F32, R0 + 4.5)
        f2_r = at("f2_r", [P, TT], F32, R0 + 4.75)
        f2_tok = at("f2_tok", [P, 2, TT, 512], F32, R0 + 5)
        f2_h = [[at(f"f2_h{c}_{n}", [P, 4, T], F32R, R0 + 21 + 16 * c + 8 * j) for j, n in enumerate(("hi", "lo"))]
                for c in range(2)]

        HT = FFN_H // P
        q_w2 = at("q_w2", [P, HT, D], BF16, 32)
        q_nat = [at(f"q_nat{i}", [P, 2048], F32, kb) for i, kb in enumerate((48, 8))]
        q_int = [at(f"q_int{i}", [P, 2048], BF16, kb) for i, kb in enumerate((56, R0 + 84))]
        q_ab = at("q_ab", [P, 4, 512], F32, 48)
        identb = at("identb", [P, P], BF16, 60)
        ones = at("ones", [P, P], F32, 60.25)
        diag4 = at("diag4", [P, 4, P], F32, 62)
        q_b1 = at("q_b1", [P, HT], F32, 61.25)
        q_am = at("q_am", [P, 32], F32, 61.3125)
        q_sw1 = at("q_sw1", [P, HT], F32, 61.4375)
        q_sw2 = at("q_sw2", [P, DK], F32, 61.5)
        q_rs = at("q_rs", [P, 2], F32, 61.53125)
        q_cm = at("q_cm", [P, HT], F32, 61.5625)
        q_mo = at("q_mo", [P, HT], F32, 61.625)
        q_mi = at("q_mi", [P, HT], F32, 61.6875)
        q_tm = at("q_tm", [P, TT], F32, 61.75)
        q_ts = at("q_ts", [P, TT], F32, 61.78125)
        h = at("h", [P, HT, T], F32, R0)
        q_w1 = at("q_w1", [P, DK, FFN_H], BF16, R0 + 32)
        xF = at("xF", [P, DK, T], F32, R0 + 48)
        xq = at("xq", [P, DK, T], BF16, R0 + 56)
        q_amx = at("q_amx", [P, T], F32, R0 + 64)
        q_xm = at("q_xm", [P, DK, T], F32, R0 + 74)
        q_srow = at("q_srow", [P, T], F32, R0 + 66)
        q_rrow = at("q_rrow", [P, T], F32, R0 + 68)
        q_t = at("q_t", [P, 2, 512], F32, R0 + 70)
        hq = at("hq", [P, HT, T], BF16, R0 + 32)
        ho = [at("ho_hi", [P, 8, T], F32R, 16), at("ho_lo", [P, 8, T], F32R, R0 + 48)]
        q_s2row = at("q_s2row", [P, D], F32, R0 + 80)
        q_b2 = at("q_b2", [P, D], F32, R0 + 82)

        ps_s = [ctx.enter_context(nc.psum_tensor(f"ps_s{i}", [P, 2, 512], F32)) for i in range(2)]
        ps_t = [ctx.enter_context(nc.psum_tensor(f"ps_t{i}", [P, 512], F32)) for i in range(3)]
        ps_o = ctx.enter_context(nc.psum_tensor("ps_o", [P, 512], F32))
        turn_banks = [ps_t[0], ps_t[1], ps_t[2], ps_o]
        ring = [ps_s[0][:, 0, :], ps_s[0][:, 1, :], ps_s[1][:, 0, :], ps_s[1][:, 1, :]]

        s_const = sem("const_in")
        s_x = sem("x_in")
        s_ctx = sem("context_in")
        s_lay = sem("layer_consts_in")
        s_csplit = sem("context_split")
        s_chi = sem("context_hi")
        s_ve = sem("var_eps_ready")
        s_rstd = sem("rstd_ready")
        s_xn = sem("xn_ready")
        w_in = {r: sem(f"w_{r}_in") for r in ("q", "kv", "o", "f")}
        w_rdy = {r: sem(f"w_{r}_split") for r in ("q", "kv", "o", "f")}
        g_full = sem("gemm_tile_full")
        g_hi = sem("gemm_tile_hi_out")
        g_free = sem("gemm_tile_out")
        s_link = sem("dve_chain")
        s_plink = sem("pool_chain")
        s_ra = sem("rotated")
        s_S = sem("scores_ready")
        s_max = sem("max_ready")
        s_exp = sem("probs_ready")
        s_rec = sem("sum_inverse_ready")
        s_scl = [sem("even_probs_normalised"), sem("odd_probs_normalised")]
        s_T = sem("probs_turned")
        s_thi = sem("turned_hi_out")
        s_tlo = sem("turned_lo_out")
        s_pv = sem("attention_out_ready")
        s_ohi = sem("attention_out_hi")
        s_olo = sem("attention_out_lo")
        s_go = sem("tile_taken")
        s_rot = sem("rotation_parts")
        s_swap = sem("halves_swapped")
        s_nat = [sem("even_rows_in"), sem("odd_rows_in")]
        s_out = sem("stored")

        class Start:

            def __init__(self, g, hi, tile, piece, unit, q, kv, o, ra):
                self.g, self.hi, self.tile, self.piece, self.unit = g, hi, tile, piece, unit
                self.q, self.kv, self.o, self.ra = q, kv, o, ra
        counts = {n: 0 for n in ("g", "hi", "tile", "piece", "unit", "q", "kv", "o", "ra")}
        START = {}

        def phase(name, **adds):
            START[name] = Start(**counts)
            for k, v in adds.items():
                counts[k] += v

        def attention_counts(l):
            n = l.groups
            kv = n // l.kv_every
            phase(l.name, g=kv * l.kv_tiles + n * 8, hi=kv * l.kv_hi + n * HG, tile=n * TILES,
                  piece=n * TILES * len(l.pieces), unit=n * UNITS, q=n, kv=kv, o=n,
                  ra=n * (HG + 2) if l.rope else 0)
        phase("ln0", g=4, hi=4)
        attention_counts(L0)
        phase("ln1", g=4, hi=4)
        phase("f0", g=8 + 4, hi=0, q=1, o=1)
        phase("ln2", g=4, hi=4)
        attention_counts(L1)
        phase("ln3", g=4, hi=4)
        phase("f1", g=4 + 4 + 1 + 4, hi=1, q=1, kv=1, o=1)
        phase("ln4", g=4, hi=4)
        attention_counts(L2)
        phase("ln5", g=4, hi=4)
        phase("f2", g=1 + 8 + 8 + 4, hi=8, q=2, kv=1, o=1)
        phase("ln6", g=4, hi=4)
        phase("l3", g=2 * (2 + 2 + 2 + 4 + 4), hi=2 * (2 + 2 + 4), q=2, kv=2, o=2)
        phase("ln7", g=4, hi=4)
        phase("f3", q=4, o=4)

        def passes(pe, o, a, b, start, stop):
            pe.matmul(o, a[0], b[0], start=start, stop=False)
            pe.matmul(o, a[0], b[1], start=False, stop=False)
            return pe.matmul(o, a[1], b[0], start=False, stop=stop)

        def planes(t, *index):
            return [p[index] for p in t]

        def load(sp, role, n, src, before, parts=P, cols=512, tiles=4):
            if before is not None:
                sp.wait_ge(w_rdy[before[0]], before[1] * 8)
            sp.dma_start(RAW[role][0:parts, 0:tiles, 0:cols], src).then_inc(w_in[role], 16)

        def split(pool, role, n, used, piece, parts=P, cols=512):
            if piece == 0:
                pool.wait_ge(w_in[role], n * 16 + 16)
                if used is not None:
                    pool.wait_ge(g_full, used)
            w = RAW[role][0:parts, piece, 0:cols]
            hi = W[role][0][0:parts, piece, 0:cols]
            lo = W[role][1][0:parts, piece, 0:cols]
            pool.tensor_tensor(hi, w, one[0:parts, 0:1].to_broadcast([parts, cols]), ALU.mult).then_inc(w_rdy[role], 1)
            pool.wait_ge(w_rdy[role], n * 8 + (2 * piece + 1))
            pool.tensor_tensor(lo, w, hi.bitcast(F32), ALU.subtract).then_inc(w_rdy[role], 1)

        def split_all(pool, role, n, used, parts=P, cols=512):
            for piece in range(4):
                split(pool, role, n, used, piece, parts, cols)

        class Norm:

            def __init__(self, i):
                self.i, self.c = i, START[f"ln{i}"]

            def dve(self, e, link):
                if self.c.g:
                    e.wait_ge(g_free, self.c.g)
                for t in range(TT - 1 if self.c.g else 0, TT):
                    last = e.bn_stats(st[:, t, :], x[:, t, :])
                link(last)
                for t in range(TT):
                    last = e.bn_aggr(mv[:, t, :], st[:, t, :])
                link(last)
                e.tensor_scalar(veps[:, :], mv[:, :, 1], 1e-5, None, ALU.add).then_inc(s_ve, 1)
                e.wait_ge(s_rstd, self.i + 1)
                if self.i:
                    e.wait_ge(g_full, self.c.g)
                for t in range(TT):
                    e.tensor_scalar(xn[:, t, :], x[:, t, :], mv[:, t, 0:1], rstd[:, t:t + 1],
                                    ALU.subtract, ALU.mult).then_inc(s_xn, 1)
                turn_dve(e, self.c.g, self.c.hi, xT, turn_banks)

            def pool(self, e):
                e.wait_ge(s_ve, self.i + 1)
                e.tensor_tensor(rstd[:, :], veps[:, :], mhalf[:, :], ALU.pow).then_inc(s_rstd, 1)

            def pe(self, e):
                e.wait_ge(s_xn, TT * (self.i + 1))
                turn_pe(e, xn, self.c.g, turn_banks)

            def act(self, e):
                turn_act(e, self.c.g, self.c.hi, xT, turn_banks)

        def banks_at(g):
            return [ring[(g + d) % 4] for d in range(4)]

        def turn_pe(e, src, g, banks):
            for d in range(4):
                if g + d > 3:
                    e.wait_ge(g_free, g + d - 3)
                for t in range(TT):
                    mm = e.transpose(banks[d][:, t * P:(t + 1) * P], src[:, t, d * P:(d + 1) * P], ident[:, :])
                mm.then_inc(g_full, 1)

        def hi_act(e, dst, src, g, scale=1.0):
            e.wait_ge(g_full, g + 1)
            e.activation(dst, src, ACT.Copy, scale=scale).then_inc(g_hi, 1)

        def lo_dve(e, dst, hi, src, hin, scale=1.0):
            e.wait_ge(g_hi, hin + 1)
            if scale == 1.0:
                e.tensor_tensor(dst, src, hi.bitcast(F32), ALU.subtract).then_inc(g_free, 1)
                return
            e.scalar_tensor_tensor(out=dst, in0=src, scalar=scale, in1=hi.bitcast(F32),
                                   op0=ALU.mult, op1=ALU.subtract).then_inc(g_free, 1)

        def turn_act(e, g, hi, dst, banks):
            for d in range(4):
                hi_act(e, dst[0][:, d, :], banks[d][:, :], g + d)

        def turn_dve(e, g, hi, dst, banks):
            for d in range(4):
                lo_dve(e, dst[1][:, d, :], dst[0][:, d, :], banks[d][:, :], hi + d)

        class Attention:
            def __init__(self, l, A, first_before, free=None):
                self.free = free
                self.l, self.s, self.c = l, SP[l.name], START[l.name]
                self.wkv, self.wq, self.wo = A[l.name + "_wkv"], A[l.name + "_wq"], A[l.name + "_wo"]
                self.first_before = first_before
                self.per = l.kv_every

            def loop(self, e, body):
                n = self.l.groups // self.per
                with e.Fori(0, n - 1) as i:
                    body(e, i, False)
                body(e, n - 1, True)

            def q_start(self, it, s):
                return it * (self.l.kv_tiles + 8 * self.per) + (self.c.g + (self.l.kv_tiles + 8 * s if s else 0))

            def o_start(self, it, s):
                return it * (self.l.kv_tiles + 8 * self.per) + (self.c.g + self.l.kv_tiles + 8 * s + HG)

            def hi_start(self, it, s):
                return it * (self.l.kv_hi + HG * self.per) + (self.c.hi + (self.l.kv_hi + HG * s if s else 0))

            def grp(self, it, s):
                return it * self.per + s

            def sp_first(self, e):
                l, c = self.l, self.c
                load(e, "q", c.q, self.wq[0], self.first_before, cols=HG * l.hd)
                load(e, "kv", c.kv, self.wkv[0], ("kv", c.kv) if c.kv else None, cols=2 * l.hd)

            def sp(self, e):
                l, c = self.l, self.c

                def body(e, it, last):
                    for s in range(self.per):
                        g = self.grp(it, s)
                        load(e, "o", None, self.wo[g], ("q", g + (c.q + 1)), parts=l.hd)
                        if s == self.per - 1 and not last:
                            load(e, "kv", None, self.wkv[it + 1], ("kv", it + (c.kv + 1)), cols=2 * l.hd)
                        if not (last and s == self.per - 1):
                            load(e, "q", None, self.wq[g + 1], ("o", g + (c.o + 1)), cols=HG * l.hd)
                self.loop(e, body)

            def pool_first(self, e):
                l, c = self.l, self.c
                split_all(e, "kv", c.kv, self.free["kv"], cols=2 * l.hd)
                for piece in range(2):
                    split(e, "q", c.q, self.free["q"], piece, cols=HG * l.hd)

            def pool_second(self, e):
                for piece in range(2, 4):
                    split(e, "q", self.c.q, None, piece, cols=HG * self.l.hd)

            def pool(self, e):
                l, c, sp = self.l, self.c, self.s

                def body(e, it, last):
                    for s in range(self.per):
                        g = self.grp(it, s)
                        q0, o0 = self.q_start(it, s), self.o_start(it, s)
                        more = [("o", g + c.o, q0, p, l.hd, 512) for p in range(4)]
                        if s == self.per - 1 and not last:
                            more += [("kv", it + (c.kv + 1), o0, p, P, 2 * l.hd) for p in range(4)]
                        if not (last and s == self.per - 1):
                            more += [("q", g + (c.q + 1), o0, p, P, HG * l.hd) for p in range(4)]
                        if l.rope:
                            ra0 = it * (HG + 2) + c.ra
                            for t in range(HG + B):
                                e.wait_ge(s_rot, ra0 * 2 + (2 * t + 2))
                                e.tensor_tensor(sp.ra[:, t % 2, :], sp.ra[:, t % 2, :], sp.rb[:, t % 2, :], ALU.add)\
                                    .then_inc(s_ra, 1)
                        for job in more:
                            split(e, *job)
                self.loop(e, body)

            def pe(self, e):
                l, c, sp = self.l, self.c, self.s
                hd = l.hd

                def body(e, it, last):
                    def bank(n, q0):
                        e.wait_ge(g_free, q0 + (n - 3))
                        return ring[n % 4]
                    for s in range(self.per):
                        g = self.grp(it, s)
                        q0, o0 = self.q_start(it, s), self.o_start(it, s)

                        def project_in(o, role, c0, src, lo, first=False):
                            for d in range(DK):
                                if first:
                                    e.wait_ge(g_free, c.g - 3 + d)
                                    e.wait_ge(w_rdy["q"], g * 8 + (8 * c.q + 2 * d + 2))
                                mm = passes(e, o[0:hd, :], planes(W[role], slice(None), d, slice(c0, c0 + hd)),
                                            planes(src, slice(None), d, slice(lo, lo + 512)), d == 0, d == DK - 1)
                            mm.then_inc(g_full, 1)
                        for hh in range(HG if s == 0 else HG - 1):
                            project_in(bank(hh, q0), "q", hh * hd, xT, 0, hh == 0)
                        if s == 0:
                            e.wait_ge(w_rdy["kv"], it * 8 + (8 * c.kv + 8))
                            e.wait_ge(s_csplit, DK)
                            for n, (src, lo) in enumerate([(cT, b * SK) for b in range(B)] + ([(xT, 0)] if l.self_keys else []), HG):
                                project_in(bank(n, q0), "kv", 0, src, lo)
                            for j, (src, lo) in enumerate([(cT, 0), (xT, 0) if l.self_keys else (cT, SK)]):
                                n = HG + l.parts + j
                                project_in(ps_t[2] if n % 4 == 0 else bank(n, q0), "kv", hd, src, lo)

                        def late_tile():
                            if s == 0:
                                if l.self_keys:
                                    project_in(ps_o, "kv", hd, cT, SK)
                            else:
                                project_in(ps_o, "q", (HG - 1) * hd, xT, 0)

                        def turn_values(j, o, count):
                            e.wait_ge(g_free, q0 + count)
                            for t in range(4):
                                mm = e.transpose(o[:, t * P:t * P + hd], xn[0:hd, j, t * P:(t + 1) * P],
                                                 ident[0:hd, 0:hd])
                            mm.then_inc(g_full, 1)

                        def scores(i):
                            u, qt = i // 2, i % 2
                            b, hh = u // HG, u % HG
                            if i < 2:
                                if s:
                                    out = 2 + i
                                elif l.rope:
                                    out = HG + l.parts + i
                                else:
                                    out = HG + l.parts + i
                                e.wait_ge(g_free, q0 + out)
                            else:
                                e.wait_ge(s_exp, g * TILES + (c.tile + i - 1))
                            q = planes(sp.q, slice(0, hd), hh, slice(b * SQ + qt * P, b * SQ + (qt + 1) * P))
                            for j, (lo, w) in enumerate([(0, SK)] + ([(SK, SQ)] if l.self_keys else [])):
                                mm = passes(e, ps_s[i % 2][:, j, 0:w], q,
                                            planes(sp.k, slice(0, hd), b, slice(lo, lo + w)), True, True)
                            mm.then_inc(s_S, 1)

                        def turn(i):
                            e.wait_ge(s_scl[i % 2], g * (TILES // 2) + (c.tile // 2 + i // 2 + 1))
                            for j, (k0, nk) in enumerate(l.pieces):
                                p = i * len(l.pieces) + j
                                if i == 0 and j == 0 and s == 0:
                                    e.wait_ge(g_free, q0 + (HG + l.parts + 2 * l.early))
                                if p >= 3:
                                    e.wait_ge(s_tlo, g * (TILES * len(l.pieces)) + (c.piece + p - 2))
                                for k in range(nk):
                                    mm = e.transpose(ps_t[p % 3][:, k * P:(k + 1) * P],
                                                     sp.p[:, i % 3, (k0 + k) * P:(k0 + k + 1) * P], ident[:, :])
                                mm.then_inc(s_T, 1)

                        def attend(u):
                            b = u // HG
                            np_ = len(l.pieces)
                            e.wait_ge(s_tlo, g * (TILES * np_) + (c.piece + (2 * u + 2) * np_))
                            if u >= (2 if l.rope else 1):
                                e.wait_ge(s_olo, g * UNITS + (c.unit + u - (1 if l.rope else 0)))
                            if u == 0:
                                e.wait_ge(g_free, o0)
                            for k in range(l.kt):
                                mm = passes(e, out_of(l, u)[0:hd, :], planes(sp.v, slice(None), b, k, slice(0, hd)),
                                            planes(sp.pt[u % 2], slice(None), k, slice(None)), k == 0, k == l.kt - 1)
                            mm.then_inc(s_pv, 1)
                        def project(t):
                            for hh in range(HG):
                                if t == 0 and hh == 0:
                                    e.wait_ge(w_rdy["o"], g * 8 + (8 * c.o + 8))
                                    e.wait_ge(s_olo, g * UNITS + (c.unit + HG))
                                    e.wait_ge(s_exp, g * TILES + (c.tile + TILES - 1))
                                if t == 2 and hh == 0:
                                    e.wait_ge(s_olo, g * UNITS + (c.unit + UNITS - 1))
                                if t == 2 and hh == HG - 1:
                                    e.wait_ge(s_olo, g * UNITS + (c.unit + UNITS))
                                mm = passes(e, ring[t], planes(sp.ot, slice(0, hd), hh, slice(t * P, (t + 1) * P)),
                                            planes(W["o"], slice(0, hd), hh, slice(None)), hh == 0, hh == HG - 1)
                            mm.then_inc(g_full, 1)
                        for i in range(PIPE):
                            if i < TILES:
                                scores(i)
                            if s == 0 and i < l.early:
                                turn_values(i, ps_t[i], HG + l.parts + i + 1)
                            if i == 1:
                                late_tile()
                            if l.self_keys and s == 0 and i == 3:
                                turn_values(l.early, ps_o, HG + l.parts + 2 * l.early + 1)
                            if 0 <= i - 2 < TILES:
                                turn(i - 2)
                            if i == TILES + 1:
                                project(1)
                            if i >= 4 and i % 2 == 0 and (i - 4) // 2 < UNITS:
                                attend((i - 4) // 2)
                            if i == TILES:
                                project(0)
                        e.wait_ge(s_exp, g * TILES + (c.tile + TILES))
                        project(2)
                        project(3)
                self.loop(e, body)

            def act(self, e):
                l, c, sp = self.l, self.c, self.s
                hd = l.hd

                def body(e, it, last):
                    def swap(r, g, ra):
                        e.wait_ge(g_full, g + (r + 1))
                        if r >= 2:
                            e.wait_ge(s_ra, ra + (r - 1))
                        for p0, p1 in ((0, 64), (64, 0)):
                            e.activation(sp.rb[p0:p0 + 64, r % 2, :], ring[r % 4][p1:p1 + 64, :], ACT.Copy)\
                                .then_inc(s_swap, 1)
                    for s in range(self.per):
                        g = self.grp(it, s)
                        q0 = self.q_start(it, s)
                        if l.rope:
                            ra0 = it * (HG + 2) + c.ra
                            swap(0, q0, ra0)
                            for r, dst in enumerate(rotated_tiles(sp, 0)):
                                if r + 1 < HG + B:
                                    swap(r + 1, q0, ra0)
                                e.wait_ge(s_ra, ra0 + (r + 1))
                                e.activation(dst, sp.ra[:, r % 2, :], ACT.Copy, scale=l.scale if r < HG else 1.0)\
                                    .then_inc(g_hi, 1)
                        else:
                            for hh in range(HG if s == 0 else HG - 1):
                                hi_act(e, sp.q[0][0:hd, hh, :], ring[hh][0:hd, :], q0 + hh, l.scale)
                            if s == 0:
                                for n, (dst, src) in enumerate(k_tiles(l, sp, 0), HG):
                                    hi_act(e, dst, src, q0 + n)
                        np_ = len(l.pieces)
                        for i in range(PIPE):
                            if i >= 5 and i % 2 == 1 and (i - 5) // 2 < UNITS:
                                u = (i - 5) // 2
                                b, hh = u // HG, u % HG
                                e.wait_ge(s_pv, g * UNITS + (c.unit + u + 1))
                                e.activation(sp.ot[0][0:hd, hh, b * SQ:(b + 1) * SQ], out_of(l, u)[0:hd, :],
                                             ACT.Copy).then_inc(s_ohi, 1)
                            if i % 2 == 1 and i - 1 < TILES:
                                e.wait_ge(s_rec, g * TILES + (c.tile + i))
                                pr = sp.p[:, (i - 1) % 3, :]
                                e.activation(pr, pr, ACT.Copy, scale=rinv[:, i - 1:i]).then_inc(s_scl[0], 1)
                            if 0 <= i - 2 < TILES:
                                j = i - 2
                                u, qt = j // 2, j % 2
                                if qt == 0:
                                    if u >= 2:
                                        e.wait_ge(s_pv, g * UNITS + (c.unit + u - 1))
                                for m, (k0, nk) in enumerate(l.pieces):
                                    p = j * np_ + m
                                    e.wait_ge(s_T, g * (TILES * np_) + (c.piece + p + 1))
                                    e.activation(sp.pt[u % 2][0][:, k0:k0 + nk, qt * P:(qt + 1) * P],
                                                 ps_t[p % 3][:, 0:nk * P].rearrange("p (k q) -> p k q", q=P),
                                                 ACT.Copy).then_inc(s_thi, 1)
                            if s == 0 and i < l.early:
                                hi_act(e, *v_tile(l, sp, 0, i), q0 + (HG + l.parts + l.early + i))
                            if l.self_keys and s == 0 and i == 3:
                                hi_act(e, *v_tile(l, sp, 0, l.early), q0 + (HG + l.kv_tiles - 1))
                            if s and i == 2:
                                hi_act(e, sp.q[0][0:hd, HG - 1, :], ps_o[0:hd, :], q0 + (HG - 1), l.scale)
                            if i < TILES:
                                e.wait_ge(s_max, g * TILES + (c.tile + i + 1))
                                src = sp.p[:, i % 3, :] if l.rope else ps_flat(i)[:, 0:l.keys]
                                e.activation(sp.p[:, i % 3, :], src, ACT.Exp, bias=nmax[:, i:i + 1],
                                             scale=-1.0 if l.rope else 1.0,
                                             accum_out=rsum[:, i:i + 1]).then_inc(s_exp, 1)
                self.loop(e, body)

            def dve(self, e, link):
                l, c, sp = self.l, self.c, self.s
                hd = l.hd

                def body(e, it, last):
                    def rotate(r, g, ra):
                        b2 = B if r < HG else 1

                        def v3(a):
                            return a.rearrange("p (b t) -> p b t", b=b2)

                        def tab(t):
                            a = t[:, 0:512 // b2]
                            return a.rearrange("p (b t) -> p b t", b=1) if b2 == 1 else \
                                a.unsqueeze(1).to_broadcast([P, b2, SQ])
                        if r >= 2:
                            e.wait_ge(g_free, g + (r - 1))
                        e.wait_ge(s_swap, ra * 2 + (2 * r + 2))
                        ra_, rb_ = v3(sp.ra[:, r % 2, :]), v3(sp.rb[:, r % 2, :])
                        e.tensor_tensor(ra_, v3(ring[r % 4]), tab(sp.cos), ALU.mult).then_inc(s_rot, 1)
                        e.tensor_tensor(rb_, rb_, tab(sp.sin), ALU.mult).then_inc(s_rot, 1)
                    np_ = len(l.pieces)
                    for s in range(self.per):
                        g = self.grp(it, s)
                        q0, o0 = self.q_start(it, s), self.o_start(it, s)
                        h0 = self.hi_start(it, s)
                        if l.rope:
                            ra0 = it * (HG + 2) + c.ra
                            rotate(0, q0, ra0)
                            for r, (dst, hi) in enumerate(zip(rotated_tiles(sp, 1), rotated_tiles(sp, 0))):
                                if r + 1 < HG + B:
                                    rotate(r + 1, q0, ra0)
                                e.wait_ge(s_ra, ra0 + (r + 1))
                                lo_dve(e, dst, hi, sp.ra[:, r % 2, :], h0 + r, l.scale if r < HG else 1.0)
                        else:
                            for hh in range(HG if s == 0 else HG - 1):
                                lo_dve(e, sp.q[1][0:hd, hh, :], sp.q[0][0:hd, hh, :], ring[hh][0:hd, :], h0 + hh, l.scale)
                            if s == 0:
                                for n, ((dst, src), (hi, _)) in enumerate(zip(k_tiles(l, sp, 1), k_tiles(l, sp, 0)), HG):
                                    lo_dve(e, dst, hi, src, h0 + n)
                        if s == 0:
                            for j in range(l.early):
                                e.wait_ge(g_full, q0 + (HG + l.parts + j + 1))
                                e.tensor_copy(xn[0:hd, j, :], value_bank(l, j)[0:hd, :]).then_inc(g_free, 1)
                        for i in range(PIPE):
                            if 0 <= i - 1 < TILES:
                                e.wait_ge(s_exp, g * TILES + (c.tile + i))
                                e.reciprocal(rinv[:, i - 1:i], rsum[:, i - 1:i]).then_inc(s_rec, 1)
                            if i >= 5 and i % 2 == 1 and (i - 5) // 2 < UNITS:
                                u = (i - 5) // 2
                                b, hh = u // HG, u % HG
                                e.wait_ge(s_ohi, g * UNITS + (c.unit + u + 1))
                                ot = [a[0:hd, hh, b * SQ:(b + 1) * SQ] for a in sp.ot]
                                e.tensor_tensor(ot[1], out_of(l, u)[0:hd, :], ot[0].bitcast(F32), ALU.subtract).then_inc(s_olo, 1)
                            if i < TILES:
                                b, qt = i // (2 * HG), i % 2
                                e.wait_ge(s_S, g * TILES + (c.tile + i + 1))
                                if l.rope:
                                    if i >= 3:
                                        e.wait_ge(s_T, g * TILES + (c.piece + i - 2))
                                    e.sem_inc(s_go, 1)
                                    e.tensor_tensor_reduce(out=sp.p[:, i % 3, :], in0=ps_s[i % 2][:, 0, :],
                                                           in1=sp.mask[:, 2 * b + qt, :], scale=-1.0, scalar=F32_MAX,
                                                           op0=ALU.add, op1=ALU.min,
                                                           accum_out=nmax[:, i:i + 1]).then_inc(s_max, 1)
                                else:
                                    e.tensor_reduce(nmax[:, i:i + 1], ps_flat(i)[:, 0:l.keys], AX.X, ALU.max,
                                                    negate=True).then_inc(s_max, 1)
                            if i % 2 == 0 and 0 <= i - 1 < TILES:
                                e.wait_ge(s_rec, g * TILES + (c.tile + i))
                                pr = sp.p[:, (i - 1) % 3, :]
                                e.tensor_scalar(pr, pr, rinv[:, i - 1:i], None, ALU.mult).then_inc(s_scl[1], 1)
                            if s == 0 and (i < l.early or i == 3 and l.self_keys):
                                j = i if i < l.early else l.early
                                dst, src = v_tile(l, sp, 1, j)
                                lo_dve(e, dst, v_tile(l, sp, 0, j)[0], src, h0 + (HG + l.parts + j))
                            if l.self_keys and s == 0 and i == 2:
                                e.wait_ge(g_full, q0 + (HG + l.kv_tiles - 1))
                                e.tensor_copy(xn[0:hd, l.early, :], ps_o[0:hd, :]).then_inc(g_free, 1)
                            if s and i == 2:
                                lo_dve(e, sp.q[1][0:hd, HG - 1, :], sp.q[0][0:hd, HG - 1, :], ps_o[0:hd, :],
                                       h0 + (HG - 1), l.scale)
                            if 0 <= i - 2 < TILES:
                                j = i - 2
                                u, qt = j // 2, j % 2
                                for m, (k0, nk) in enumerate(l.pieces):
                                    p = j * np_ + m
                                    e.wait_ge(s_thi, g * (TILES * np_) + (c.piece + p + 1))
                                    pt = [a[:, k0:k0 + nk, qt * P:(qt + 1) * P] for a in sp.pt[u % 2]]
                                    e.tensor_tensor(pt[1], ps_t[p % 3][:, 0:nk * P].rearrange("p (k q) -> p k q", q=P),
                                                    pt[0].bitcast(F32), ALU.subtract).then_inc(s_tlo, 1)
                        for t in range(TT):
                            e.wait_ge(g_full, o0 + (t + 1))
                            e.wait_ge(g_free, o0)
                            e.tensor_tensor(x[:, t, :], ring[t], x[:, t, :], ALU.add).then_inc(g_free, 1)
                            if last and s == self.per - 1 and t < TT - 1:
                                e.wait_ge(g_free, o0 + (t + 1))
                                e.bn_stats(st[:, t, :], x[:, t, :])
                self.loop(e, body)

        def out_of(l, u):
            return ps_s[1][:, 1, 0:SQ] if l.rope and u % 2 else ps_o[:, 0:SQ]

        def ps_flat(i):
            return ps_s[i % 2][:, :, :].rearrange("p a n -> p (a n)")

        def rotated_tiles(sp, plane):
            return [sp.q[plane][:, hh, :] for hh in range(HG)] + [sp.k[plane][:, b, :] for b in range(B)]

        def k_tiles(l, sp, plane):
            hd = l.hd
            out_ = [(sp.k[plane][0:hd, b, 0:SK], ring[(HG + b) % 4][0:hd, :]) for b in range(B)]
            return out_ + [(sp.k[plane][0:hd, :, SK:l.keys],
                            ring[(HG + 2) % 4][0:hd, :].rearrange("p (b t) -> p b t", b=B))]

        def value_bank(l, j):
            n = HG + l.parts + j
            return ps_t[2] if n % 4 == 0 else ring[n % 4]

        def v_tile(l, sp, plane, j):
            hd = l.hd
            src = ps_t[j] if j < l.early else ps_o
            if l.self_keys and j == 1:
                return (sp.v[plane][:, :, 4:6, 0:hd],
                        src[:, :].rearrange("p (b t d) -> p b t d", b=B, d=P)[:, :, :, 0:hd])
            return sp.v[plane][:, int(j > 0), 0:4, 0:hd], src[:, :].rearrange("p (t d) -> p t d", d=P)[:, :, 0:hd]

        def ring_of(n, c):
            return ring[(c.g + n) % 4]

        def turned(e, c, d, n=0):
            if n == 0:
                e.wait_ge(g_free, c.g - 3 + d)

        def take_bank(e, n, c):
            if c.g + n > 3:
                e.wait_ge(g_free, c.g + n - 3)
            return ring_of(n, c)

        def token_gemm(e, n, c, a, b, kts, width=512):
            for t in range(TT):
                o = take_bank(e, n + t, c)
                for k in kts:
                    if c is c1:
                        turned(e, c, k, n + t)
                    mm = passes(e, o[:, 0:width], a(k, t), b(k), k == kts[0], k == kts[-1])
                mm.then_inc(g_full, 1)

        def add_to_x(e, n, c, last=False):
            for t in range(TT):
                e.wait_ge(g_full, c.g + n + t + 1)
                e.tensor_tensor(x[:, t, :], ring_of(n + t, c), x[:, t, :], ALU.add).then_inc(g_free, 1)
                if last and t < TT - 1:
                    e.wait_ge(g_free, c.g + n + t + 1)
                    e.bn_stats(st[:, t, :], x[:, t, :])

        def add_row(e, row, link):
            for t in range(TT):
                last = e.tensor_tensor(x[:, t, :], x[:, t, :], row, ALU.add)
            link(last)

        def xT_of(d, t):
            return planes(xT, slice(None), d, slice(t * P, (t + 1) * P))

        c0 = START["f0"]
        s_f0e, s_f0s, s_f0hi, s_f0lo = (sem(f"f0_{n}") for n in ("exp", "bias_negated", "hi", "lo"))

        def f0_sp(e):
            load(e, "q", c0.q, A["f0_w12"][0], ("o", c0.o))
            e.wait_ge(g_full, c0.g - 4)
            e.dma_start(f0_b12[:, :], A["f0_b12"]).then_inc(s_lay, 16)
            e.dma_start(f_rowb[:, :], A["f0_b3"]).then_inc(s_lay, 16)
            load(e, "o", c0.o, A["f0_w12"][1], ("q", c0.q + 1))
            e.wait_ge(g_full, c0.g)
            load(e, "f", 0, A["f0_w3"], None)

        def f0_pool_first(e):
            split_all(e, "q", c0.q, c0.g - 8)

        def f0_pool(e):
            split_all(e, "o", c0.o, c0.g - 4)
            split_all(e, "f", 0, c0.g - 4)

        def f0_pe(e):
            for j in range(4):
                for role in ("q", "o"):
                    e.wait_ge(w_rdy[role], 8 * ((c0.q if role == "q" else c0.o) + 1))
                    n = 2 * j + (role == "o")
                    o = take_bank(e, n, c0)
                    for d in range(DK):
                        turned(e, c0, d, n)
                        mm = passes(e, o, planes(W[role], slice(None), d, slice(j * P, (j + 1) * P)),
                                    planes(xT, slice(None), d, slice(None)), d == 0, d == DK - 1)
                    mm.then_inc(g_full, 1)
            e.wait_ge(w_rdy["f"], 8)
            e.wait_ge(s_f0lo, 4)
            token_gemm(e, 8, c0, lambda k, t: planes(f_h, slice(None), k, slice(t * P, (t + 1) * P)),
                       lambda k: planes(W["f"], slice(None), k, slice(None)), range(4))

        def f0_act(e):
            for j in range(4):
                e.wait_ge(g_full, c0.g + 2 * j + 1)
                e.wait_ge(s_f0s, 1)
                if j >= 2:
                    e.wait_ge(g_free, c0.g + 2 * j - 3)
                e.activation(f0_e[:, j % 2, :], ring_of(2 * j, c0), ACT.Exp, bias=f0_nb[:, j:j + 1],
                             scale=-1.0).then_inc(s_f0e, 1)
                e.wait_ge(g_free, c0.g + 2 * j + 2)
                e.activation(f_h[0][:, j, :], f0_g[:, :], ACT.Copy).then_inc(s_f0hi, 1)

        def f0_dve(e, link):
            e.wait_ge(s_lay, LAY["f0"])
            e.tensor_scalar(f0_nb[:, :], f0_b12[:, :], -1.0, None, ALU.mult).then_inc(s_f0s, 1)
            for j in range(4):
                e.wait_ge(s_f0e, j + 1)
                link(e.tensor_scalar(f0_s[:, :], f0_e[:, j % 2, :], 1.0, None, ALU.add))
                link(e.reciprocal(f0_e[:, j % 2, :], f0_s[:, :]))
                e.scalar_tensor_tensor(out=f0_s[:, :], in0=ring_of(2 * j, c0), scalar=f0_b12[:, j:j + 1],
                                       in1=f0_e[:, j % 2, :], op0=ALU.add, op1=ALU.mult).then_inc(g_free, 1)
                e.wait_ge(g_full, c0.g + 2 * j + 2)
                e.wait_ge(g_free, c0.g + 2 * j + 1)
                e.scalar_tensor_tensor(out=f0_g[:, :], in0=ring_of(2 * j + 1, c0), scalar=f0_b12[:, 4 + j:5 + j],
                                       in1=f0_s[:, :], op0=ALU.add, op1=ALU.mult).then_inc(g_free, 1)
                e.wait_ge(s_f0hi, j + 1)
                e.tensor_tensor(f_h[1][:, j, :], f0_g[:, :], f_h[0][:, j, :].bitcast(F32),
                                ALU.subtract).then_inc(s_f0lo, 1)
            add_row(e, f_rowb[:, :], link)
            add_to_x(e, 8, c0, True)

        c1 = START["f1"]

        def f1_sp(e):
            load(e, "kv", c1.kv, A["f1_wa"], ("kv", c1.kv), cols=256)
            load(e, "q", c1.q, A["f1_wb"], ("o", c1.o))
            e.wait_ge(g_full, c1.g - 4)
            e.dma_start(f_rowb[:, :], A["f1_bb"]).then_inc(s_lay, 16)
            e.dma_start(f1_br[:, :], A["f1_br"]).then_inc(s_lay, 16)
            load(e, "o", c1.o, A["f1_lb"], ("q", c1.q + 1), cols=128)

        def f1_pool_first(e):
            split_all(e, "kv", c1.kv, c1.g - 8, cols=256)
            split_all(e, "q", c1.q, c1.g - 8)

        def f1_pool(e):
            split_all(e, "o", c1.o, c1.g - 4, cols=128)

        s_f1h = sem("f1_experts_weighted")

        def f1_pe(e):
            e.wait_ge(w_rdy["kv"], 8 * (c1.kv + 1))
            token_gemm(e, 0, c1, xT_of, lambda k: planes(W["kv"], slice(None), k, slice(0, 256)), range(DK), 256)
            e.wait_ge(w_rdy["q"], 8 * (c1.q + 1))
            token_gemm(e, 4, c1, xT_of, lambda k: planes(W["q"], slice(None), k, slice(None)), range(DK))
            e.wait_ge(s_f1h, TT)
            o = take_bank(e, 8, c1)
            for t in range(TT):
                mm = e.transpose(o[:, t * P:(t + 1) * P], f1_h[:, t, :], ident[:, :])
            mm.then_inc(g_full, 1)
            e.wait_ge(g_free, c1.g + 9)
            e.wait_ge(w_rdy["o"], 8 * (c1.o + 1))
            for t in range(TT):
                o = take_bank(e, 9 + t, c1)
                mm = passes(e, o.rearrange("p (a n) -> p a n", a=4), planes(f1_ht, slice(None), slice(t * P, (t + 1) * P)),
                            planes(W["o"], slice(None), slice(None), slice(0, 128)), True, True)
                mm.then_inc(g_full, 1)

        def f1_act(e):
            hi_act(e, f1_ht[0][:, :], ring_of(8, c1), c1.g + 8)

        def f1_dve(e, link):
            e.wait_ge(s_lay, LAY["f1"])
            for t in range(TT):
                e.wait_ge(g_full, c1.g + t + 1)
                e.tensor_tensor(f1_z[:, t, :], ring_of(t, c1)[:, 128:136], f1_br[:, :], ALU.add)
                e.tensor_copy(f1_h[:, t, :], ring_of(t, c1)[:, 0:128]).then_inc(g_free, 1)
            e.wait_ge(g_free, c1.g + 4)
            for t in range(TT):
                last = e.max(f1_zs[:, t, :], f1_z[:, t, :])
            link(last)
            link(e.tensor_copy(f1_c[:, :, 0:1], f1_zs[:, :, 0:1]))
            for k in range(1, 8):
                link(e.tensor_tensor(f1_c[:, :, k:k + 1], f1_c[:, :, k - 1:k], f1_zs[:, :, k:k + 1], ALU.add))
            for k in range(8):
                last = e.tensor_scalar(f1_zs[:, :, k:k + 1], f1_c[:, :, k:k + 1], -1.0, 1.0 / (k + 1), ALU.add, ALU.mult)
            link(last)
            link(e.tensor_reduce(f1_tau[:, :], f1_zs[:, :, :], AX.X, ALU.max))
            link(e.tensor_tensor(f1_w[:, :, :], f1_z[:, :, :], f1_tau[:, :].unsqueeze(2).to_broadcast([P, TT, 8]), ALU.subtract))
            link(e.tensor_scalar(f1_w[:, :, :], f1_w[:, :, :], 0.0, None, ALU.max))
            for t in range(TT):
                hv = f1_h[:, t, :].rearrange("p (e r) -> p e r", e=8)
                e.tensor_tensor(hv, hv, f1_w[:, t, :].unsqueeze(2).to_broadcast([P, 8, 16]), ALU.mult).then_inc(s_f1h, 1)
            add_row(e, f_rowb[:, :], link)
            add_to_x(e, 4, c1)
            lo_dve(e, f1_ht[1][:, :], f1_ht[0][:, :], ring_of(8, c1), c1.hi)
            add_to_x(e, 9, c1, True)

        c2 = START["f2"]
        s_f2m, s_f2e = sem("f2_max"), sem("f2_exp")
        s_f2r, s_f2c = sem("f2_router_scores"), sem("f2_router_scores_out")

        def f2_sp(e):
            load(e, "kv", c2.kv, A["f2_wr"], ("kv", c2.kv), cols=64)
            load(e, "q", c2.q, A["f2_wa"][0], ("o", c2.o))
            load(e, "o", c2.o, A["f2_wa"][1], ("q", c2.q + 1))
            load(e, "q", c2.q + 1, A["f2_wb"][1], ("o", c2.o + 1))
            e.wait_ge(g_full, c2.g)
            load(e, "f", 1, A["f2_wb"][0], ("f", 1))

        def f2_pool_first(e):
            split_all(e, "kv", c2.kv, c2.g - 8, cols=64)
            split_all(e, "q", c2.q, c2.g - 8)

        def f2_pool(e):
            split_all(e, "o", c2.o, c2.g - 4)
            split_all(e, "f", 1, c2.g - 4)
            split_all(e, "q", c2.q + 1, c2.g + 5)

        def f2_pe(e):
            e.wait_ge(w_rdy["kv"], 8 * (c2.kv + 1))
            for d in range(DK):
                turned(e, c2, d)
                mm = passes(e, ps_t[0][0:64, :], planes(W["kv"], slice(None), d, slice(0, 64)),
                            planes(xT, slice(None), d, slice(None)), d == 0, d == DK - 1)
            mm.then_inc(s_f2r, 1)
            o = take_bank(e, 0, c2)
            e.wait_ge(s_f2c, 1)
            for t in range(TT):
                mm = e.transpose(o[:, t * 64:(t + 1) * 64], f2_tok[0:64, 0, 0, t * P:(t + 1) * P], ident[0:64, 0:64])
            mm.then_inc(g_full, 1)
            for half, role in enumerate(("q", "o")):
                e.wait_ge(w_rdy[role], 8 * ((c2.q, c2.o)[half] + 1))
                token_gemm(e, 1 + 4 * half, c2, xT_of, lambda k: planes(W[role], slice(None), k, slice(None)), range(DK))
            for half in range(2):
                e.wait_ge(g_free, c2.g + 5 + 4 * half)
                turn_pe(e, f2_tok[:, half, :, :], c2.g + 9 + 4 * half, banks_at(c2.g + 9 + 4 * half))
            e.wait_ge(w_rdy["f"], 8 * 2)
            e.wait_ge(w_rdy["q"], 8 * (c2.q + 2))
            e.wait_ge(g_free, c2.g + 17)
            token_gemm(e, 17, c2, lambda k, t: planes(f2_h[k // 4], slice(None), k % 4, slice(t * P, (t + 1) * P)),
                       lambda k: planes(W["fq"[k // 4]], slice(None), k % 4, slice(None)), range(8))

        def f2_act(e):
            for t in range(TT):
                e.wait_ge(s_f2m, 1)
                e.activation(f2_g[:, t, :], f2_s[:, t, :], ACT.Exp, bias=f2_nm[:, t:t + 1]).then_inc(s_f2e, 1)
            for half in range(2):
                turn_act(e, c2.g + 9 + 4 * half, c2.hi + 4 * half, f2_h[half], banks_at(c2.g + 9 + 4 * half))

        def f2_dve(e, link):
            e.wait_ge(s_f2r, 1)
            e.tensor_copy(f2_tok[0:64, 0, 0, :], ps_t[0][0:64, :]).then_inc(s_f2c, 1)
            e.wait_ge(g_full, c2.g + 1)
            e.tensor_copy(f2_s[:, :, :].rearrange("p t k -> p (t k)"), ring_of(0, c2)[:, 0:256]).then_inc(g_free, 1)
            e.wait_ge(g_free, c2.g + 1)
            for src, k, dst in ((f2_s, 0, f2_a), (f2_a, 1, f2_b)):
                for t in range(TT):
                    last = e.max(f2_m[:, t, k, :], src[:, t, :])
                link(last)
                for t in range(TT):
                    last = e.match_replace(dst[:, t, :], f2_m[:, t, k, :], src[:, t, :], -F32_MAX)
                link(last)
            e.tensor_scalar(f2_nm[:, :], f2_m[:, :, 0, 0], -1.0, None, ALU.mult).then_inc(s_f2m, 1)
            link(e.tensor_tensor(f2_a[:, :, :], f2_b[:, :, :], f2_s[:, :, :], ALU.not_equal))
            e.wait_ge(s_f2e, TT)
            link(e.tensor_tensor(f2_g[:, :, :], f2_g[:, :, :], f2_a[:, :, :], ALU.mult))
            link(e.tensor_reduce(f2_sum[:, :], f2_g[:, :, :], AX.X, ALU.add))
            link(e.reciprocal(f2_r[:, :], f2_sum[:, :]))
            for t in range(TT):
                last = e.tensor_scalar(f2_g[:, t, :], f2_g[:, t, :], f2_r[:, t:t + 1], 2.0, ALU.mult, ALU.mult)
            link(last)
            for half in range(2):
                for t in range(TT):
                    n = 1 + 4 * half + t
                    e.wait_ge(g_full, c2.g + n + 1)
                    e.tensor_tensor(f2_tok[:, half, t, :].rearrange("p (k r) -> p k r", r=16),
                                    ring_of(n, c2).rearrange("p (k r) -> p k r", r=16),
                                    f2_g[:, t, 32 * half:32 * half + 32].unsqueeze(2).to_broadcast([P, 32, 16]),
                                    ALU.mult).then_inc(g_free, 1)
            for half in range(2):
                turn_dve(e, c2.g + 9 + 4 * half, c2.hi + 4 * half, f2_h[half], banks_at(c2.g + 9 + 4 * half))
            add_to_x(e, 17, c2, True)

        c3 = START["l3"]
        s3 = {n: sem(f"l3_{n}") for n in ("S", "max", "exp", "rec", "scl", "T", "thi", "tlo", "pv", "ohi", "olo", "zero")}
        L3_G = 14

        def l3_sp(e):
            load(e, "kv", c3.kv, A["l3_wkv"][0], ("kv", c3.kv), cols=192)
            load(e, "q", c3.q, A["l3_wq"][0], ("q", c3.q))
            e.wait_ge(g_full, c3.g - 4)
            e.dma_start(l3m8[:, :, :], A["l3_mask"]).then_inc(s_lay, 16)
            e.dma_start(l3sel[:, :], A["l3_sel"]).then_inc(s_lay, 16)
            load(e, "kv", c3.kv + 1, A["l3_wkv"][1], ("kv", c3.kv + 1), cols=192)
            load(e, "o", c3.o, A["l3_wo"][0], ("q", c3.q + 1))
            load(e, "q", c3.q + 1, A["l3_wq"][1], ("o", c3.o + 1))
            load(e, "o", c3.o + 1, A["l3_wo"][1], ("q", c3.q + 2))

        def l3_pool_first(e):
            for g in range(4):
                if g == 2:
                    split_all(e, "kv", c3.kv, c2.g + 1, cols=192)
                    e.wait_ge(g_full, c3.g - 4)
                for y in range(2):
                    e.memset(l3y[g][y][:, :].bitcast(F32), 0.0).then_inc(s3["zero"], 1)

        def l3_pool(e):
            split_all(e, "q", c3.q, c3.g - 4)
            split_all(e, "o", c3.o, c3.g - 4)
            split_all(e, "kv", c3.kv + 1, c3.g + 4, cols=192)
            for G in range(2):
                if G == 1:
                    split_all(e, "o", c3.o + 1, c3.g + L3_G)
                for i in range(L3_TILES):
                    e.wait_ge(s3["rec"], G * L3_TILES + i + 1)
                    e.tensor_tensor(l3p[:, i % 4, :], l3p[:, i % 4, :], rinv[:, i % TILES:i % TILES + 1].to_broadcast([P, SK]),
                                    ALU.mult).then_inc(s3["scl"], 1)
                    if i % 16 == 8:
                        split(e, "q", c3.q + 1 + G, c3.g + L3_G * G + 10, i // 16)

        def l3_tile(i):
            return i // 16, i // 4 % 4, i // 2 % 2, i % 2

        def l3_out(u):
            return ps_s[0][:, 1, 0:SQ] if u % 2 else ps_o[:, 0:SQ]

        def l3_pe(e):
            for G in range(2):
                n = L3_G * G
                e.wait_ge(w_rdy["kv"], 8 * (c3.kv + G + 1))
                for lo, hi in ((0, P), (P, 192)):
                    for b in range(B):
                        o = take_bank(e, n, c3)
                        for d in range(DK):
                            mm = passes(e, o[0:hi - lo, :], planes(W["kv"], slice(None), d, slice(lo, hi)),
                                        planes(cT, slice(None), d, slice(b * SK, (b + 1) * SK)), d == 0, d == DK - 1)
                        mm.then_inc(g_full, 1)
                        n += 1
                for b in range(B):
                    o = take_bank(e, n, c3)
                    e.wait_ge(g_free, c3.g + n - 1)
                    for t in range(4):
                        mm = e.transpose(o[:, t * 64:(t + 1) * 64], l3k[0:64, b, t * P:(t + 1) * P], ident[0:64, 0:64])
                    mm.then_inc(g_full, 1)
                    n += 1
                e.wait_ge(w_rdy["q"], 8 * (c3.q + G + 1))
                for m in range(4):
                    o = take_bank(e, n, c3)
                    for d in range(DK):
                        turned(e, c3, d, G + m)
                        mm = passes(e, o, planes(W["q"], slice(None), d, slice(m * P, (m + 1) * P)),
                                    planes(xT, slice(None), d, slice(None)), d == 0, d == DK - 1)
                    mm.then_inc(g_full, 1)
                    n += 1
                e.wait_ge(g_free, c3.g + n)
                k0, u0 = G * L3_TILES, G * L3_UNITS
                for i in range(L3_PIPE):
                    if i < L3_TILES:
                        m, g, b, qt = l3_tile(i)
                        if i >= 2:
                            e.wait_ge(s3["max"], k0 + i - 1)
                        for y in range(2):
                            mm = e.matmul(ps_s[i % 2][:, 0, :], l3x[:, m, b * SQ + qt * P:b * SQ + (qt + 1) * P],
                                          l3y[g][y][:, b * SK:(b + 1) * SK], start=y == 0, stop=y == 1)
                        mm.then_inc(s3["S"], 1)
                    if i >= 6 and i % 2 == 0:
                        u = (i - 6) // 2
                        b = u % B
                        e.wait_ge(s3["tlo"], k0 + 2 * u + 2)
                        if u >= 2:
                            e.wait_ge(s3["olo"], u0 + u - 1)
                        for k in range(4):
                            for y in range(2):
                                mm = e.matmul(l3_out(u), l3v[:, b * 4 + k, :, :, :].rearrange("p g a d -> p (g a d)"),
                                              l3pt[u % 2][y][:, k, :], start=k == 0 and y == 0, stop=k == 3 and y == 1)
                        mm.then_inc(s3["pv"], 1)
                    j = i - 3
                    if 0 <= j < L3_TILES:
                        e.wait_ge(s3["scl"], k0 + j + 1)
                        if k0 + j >= 3:
                            e.wait_ge(s3["tlo"], k0 + j - 2)
                        for k in range(4):
                            mm = e.transpose(ps_t[j % 3][:, k * P:(k + 1) * P], l3p[:, j % 4, k * P:(k + 1) * P], ident[:, :])
                        mm.then_inc(s3["T"], 1)
                e.wait_ge(s3["olo"], u0 + L3_UNITS)
                e.wait_ge(w_rdy["o"], 8 * (c3.o + G + 1))
                token_gemm(e, n, c3, lambda k, t: planes(l3ot, slice(None), k, slice(t * P, (t + 1) * P)),
                           lambda k: planes(W["o"], slice(None), k, slice(None)), range(4))

        def l3_ot(u, y):
            m, g, b, _ = l3_tile(2 * u)
            return l3ot[y][32 * g:32 * g + 32, m, b * SQ:(b + 1) * SQ]

        def l3_act(e):
            e.wait_ge(s3["zero"], 8)
            for G in range(2):
                n = c3.g + L3_G * G
                for b in range(B):
                    e.wait_ge(g_full, n + b + 1)
                    for g in range(4):
                        last = e.activation(l3y[g][0][32 * g:32 * g + 32, b * SK:(b + 1) * SK],
                                            ring[(n + b) % 4][32 * g:32 * g + 32, :], ACT.Copy)
                    last.then_inc(g_hi, 1)
                n += 4
                for b in range(B):
                    hi_act(e, l3v[:, b * 4:b * 4 + 4, :, 0, :],
                           ring[(n + b) % 4][:, 0:256].rearrange("p (t g d) -> p t g d", t=4, d=16), n + b)
                n += 2
                for m in range(4):
                    if m >= 2:
                        e.wait_ge(g_free, n + m - 1)
                    hi_act(e, l3t[:, m % 2, :], ring[(n + m) % 4], n + m, 0.25)
                k0, u0 = G * L3_TILES, G * L3_UNITS
                for i in range(L3_PIPE + 1):
                    if i >= 7 and i % 2 == 1:
                        u = (i - 7) // 2
                        g = u // B % 4
                        e.wait_ge(s3["pv"], u0 + u + 1)
                        e.activation(l3_ot(u, 0), l3_out(u)[32 * g:32 * g + 32, :], ACT.Copy).then_inc(s3["ohi"], 1)
                    j = i - 3
                    if 0 <= j < L3_TILES:
                        u = j // 2
                        e.wait_ge(s3["T"], k0 + j + 1)
                        if u >= 2:
                            e.wait_ge(s3["pv"], u0 + u - 1)
                        e.activation(l3pt[u % 2][0][:, :, j % 2 * P:(j % 2 + 1) * P],
                                     ps_t[j % 3][:, :].rearrange("p (k q) -> p k q", q=P), ACT.Copy).then_inc(s3["thi"], 1)
                    if i < L3_TILES:
                        c = i % TILES
                        e.wait_ge(s3["max"], k0 + i + 1)
                        e.activation(l3p[:, i % 4, :], l3p[:, i % 4, :], ACT.Exp, bias=nmax[:, c:c + 1], scale=-1.0,
                                     accum_out=rsum[:, c:c + 1]).then_inc(s3["exp"], 1)

        def l3_dve(e, link):
            e.wait_ge(s_lay, LAY["l3"])
            link(e.tensor_scalar(l3mask[:, :, :], l3m8[:, :, :], -1.0, -NEG, ALU.add, ALU.mult))
            e.wait_ge(s3["zero"], 8)
            for G in range(2):
                n = L3_G * G
                h0 = c3.hi + 8 * G
                for b in range(B):
                    e.wait_ge(g_hi, h0 + b + 1)
                    for g in range(4):
                        y = [a[32 * g:32 * g + 32, b * SK:(b + 1) * SK] for a in l3y[g]]
                        last = e.tensor_tensor(y[1], ring_of(n + b, c3)[32 * g:32 * g + 32, :], y[0].bitcast(F32), ALU.subtract)
                    last.then_inc(g_free, 1)
                n += 2
                for b in range(B):
                    e.wait_ge(g_full, c3.g + n + b + 1)
                    e.tensor_copy(l3k[0:64, b, :], ring_of(n + b, c3)[0:64, :]).then_inc(g_free, 1)
                n += 2
                for b in range(B):
                    e.wait_ge(g_hi, h0 + 2 + b + 1)
                    e.tensor_tensor(l3v[:, b * 4:b * 4 + 4, :, 1, :],
                                    ring_of(n + b, c3)[:, 0:256].rearrange("p (t g d) -> p t g d", t=4, d=16),
                                    l3v[:, b * 4:b * 4 + 4, :, 0, :].bitcast(F32), ALU.subtract).then_inc(g_free, 1)
                n += 2
                for m in range(4):
                    e.wait_ge(g_hi, h0 + 4 + m + 1)
                    link(e.tensor_scalar(l3k[:, m % 2, :], ring_of(n + m, c3), l3sel[:, 0:1], None, ALU.mult))
                    e.scalar_tensor_tensor(out=l3x[:, m, :], in0=l3t[:, m % 2, :].bitcast(F32), scalar=l3sel[:, 1:2],
                                           in1=l3k[:, m % 2, :], op0=ALU.mult, op1=ALU.add).then_inc(g_free, 1)
                n += 4
                k0, u0 = G * L3_TILES, G * L3_UNITS
                for i in range(L3_PIPE + 1):
                    if i < L3_TILES:
                        m, g, b, qt = l3_tile(i)
                        c = i % TILES
                        e.wait_ge(s3["S"], k0 + i + 1)
                        if k0 + i >= 4:
                            e.wait_ge(s3["T"], k0 + i - 3)
                        e.tensor_tensor_reduce(out=l3p[:, i % 4, :], in0=ps_s[i % 2][:, 0, :], in1=l3mask[:, qt, :],
                                               scale=-1.0, scalar=F32_MAX, op0=ALU.add, op1=ALU.min,
                                               accum_out=nmax[:, c:c + 1]).then_inc(s3["max"], 1)
                    j = i - 1
                    if 0 <= j < L3_TILES:
                        c = j % TILES
                        e.wait_ge(s3["exp"], k0 + j + 1)
                        if k0 + j >= TILES:
                            e.wait_ge(s3["scl"], k0 + j + 1 - TILES)
                        e.reciprocal(rinv[:, c:c + 1], rsum[:, c:c + 1]).then_inc(s3["rec"], 1)
                    if i >= 7 and i % 2 == 1:
                        u = (i - 7) // 2
                        g = u // B % 4
                        e.wait_ge(s3["ohi"], u0 + u + 1)
                        e.tensor_tensor(l3_ot(u, 1), l3_out(u)[32 * g:32 * g + 32, :], l3_ot(u, 0).bitcast(F32),
                                        ALU.subtract).then_inc(s3["olo"], 1)
                    j = i - 3
                    if 0 <= j < L3_TILES:
                        pt = [a[:, :, j % 2 * P:(j % 2 + 1) * P] for a in l3pt[j // 2 % 2]]
                        e.wait_ge(s3["thi"], k0 + j + 1)
                        e.tensor_tensor(pt[1], ps_t[j % 3][:, :].rearrange("p (k q) -> p k q", q=P), pt[0].bitcast(F32),
                                        ALU.subtract).then_inc(s3["tlo"], 1)
                add_to_x(e, n, c3, G == 1)

        cf = START["f3"]
        s4 = {n: sem(f"f3_{n}") for n in ("rows_rounded", "rows_int", "turned", "turned_out", "x_outliers", "out_full", "x_magnitude",
                                         "out_kept", "int_full", "int_out", "row_full", "row_out", "largest", "diag",
                                         "x_int", "summed", "masks", "magnitude", "magnitude_used", "hi", "lo", "used", "h_int", "acc", "finished")}
        scale_bank = [ps_t[2][:, :], ps_o[:, :]]

        def f3_sp(e):
            def rows_in(cc):
                if cc >= 2:
                    e.wait_ge(s4["rows_int"], cc - 1)
                e.dma_start(q_nat[cc % 2][:, :], A["f3_w1n"][cc] if cc < 4 else A["f3_w2n"][cc - 4]).then_inc(s_nat[cc % 2], 16)

            def load_chunk(cc):
                role = "qo"[cc % 2]
                src = A["f3_w1"][cc] if cc < 4 else A["f3_w2"][cc - 4]
                before = ("o", cf.o + cc // 2) if role == "q" else ("q", cf.q + cc // 2 + 1)
                load(e, role, (cf.q if role == "q" else cf.o) + cc // 2, src, before)
            e.wait_ge(g_full, c3.g + L3_G + 4)
            e.dma_start(q_b1[:, :], A["f3_b1"]).then_inc(s_lay, 16)
            rows_in(0)
            load_chunk(0)
            load_chunk(1)
            e.wait_ge(g_full, cf.g - 4)
            e.dma_start(q_b2[:, :], A["f3_b2"]).then_inc(s_lay, 16)
            e.wait_ge(g_full, cf.g)
            rows_in(1)
            rows_in(2)
            load_chunk(2)
            rows_in(3)
            rows_in(4)
            load_chunk(3)
            for cc in range(5, 8):
                rows_in(cc)
            for cc in range(4, 8):
                load_chunk(cc)
            for t in range(TT):
                e.wait_ge(s4["finished"], t + 1)
                e.dma_start(out[t // 2, t % 2 * P:(t % 2 + 1) * P, :], x[:, t, :]).then_inc(s_out, 16)
            e.wait_ge(s_out, 16 * TT)

        def f3_pool(e):
            for cc in range(1, 8):
                if 2 <= cc < 6:
                    e.wait_ge(s4["out_full"], 4 * (cc - 1))
                if cc >= 6:
                    e.wait_ge(s4["used"], 4 * (cc - 5))
                split_all(e, "qo"[cc % 2], (cf.q, cf.o)[cc % 2] + cc // 2, cf.g - 4)

        def f3_pe(e):
            e.wait_ge(g_free, cf.g)
            e.wait_ge(s4["x_outliers"], 1)

            def turn_rows(cc):
                e.wait_ge(s4["rows_int"], cc + 1)
                for part in range(2):
                    n = 2 * cc + part
                    if n >= 2:
                        e.wait_ge(s4["turned_out"], n - 1)
                    for k in range(8):
                        if cc < 4:
                            a = (k % 4) * 512 + (2 * part + k // 4) * P
                        else:
                            a = (8 * part + k) * P
                        mm = e.transpose(ps_t[n % 2][:, :].bitcast(BF16)[:, k * P:(k + 1) * P],
                                         q_int[cc % 2][:, a:a + P], identb[:, :])
                    mm.then_inc(s4["turned"], 1)

            def turn_largest(which):
                if which == 0:
                    e.wait_ge(s4["largest"], 1)
                else:
                    e.wait_ge(s4["magnitude_used"], HT)
                for t in range(TT):
                    mm = e.transpose(scale_bank[0][:, t * P:(t + 1) * P], q_amx[:, t * P:(t + 1) * P], ident[:, :])
                mm.then_inc(s4["row_full"], 1)

            def spread(which):
                e.wait_ge(s4["diag"], which + 1)
                if which == 2:
                    e.wait_ge(s4["row_out"], 3)
                for t in range(TT):
                    mm = e.matmul(scale_bank[1][:, t * P:(t + 1) * P], ones[:, :], diag4[:, t, :], start=True, stop=True)
                mm.then_inc(s4["row_full"], 1)
            for cc in range(9):
                for j in (2 * cc, 2 * cc + 1) if cc < 8 else ():
                    chunk, role = j // 4, "qo"[(j // 4) % 2]
                    e.wait_ge(w_rdy[role], 8 * ((cf.q, cf.o)[chunk % 2] + chunk // 2 + 1))
                    if j >= 2:
                        e.wait_ge(s4["out_kept"], j - 1)
                    for d in range(DK):
                        mm = passes(e, ring[j % 2], planes(W[role], slice(None), d, slice((j % 4) * P, (j % 4 + 1) * P)),
                                    planes(xT, slice(None), d, slice(None)), d == 0, d == DK - 1)
                    mm.then_inc(s4["out_full"], 1)
                if cc:
                    turn_rows(cc - 1)
                if cc == 6:
                    turn_largest(0)
                if cc == 7:
                    spread(0)
            e.wait_ge(s4["turned_out"], 8)
            e.wait_ge(s4["x_int"], DK)
            for j in range(HT):
                if j >= 2:
                    e.wait_ge(s4["int_out"], j - 1)
                for d in range(DK):
                    mm = e.matmul(ring[2 + j % 2], q_w1[:, d, j * P:(j + 1) * P], xq[:, d, :], start=d == 0, stop=d == DK - 1)
                mm.then_inc(s4["int_full"], 1)
                if j == 3:
                    spread(1)
            e.wait_ge(s4["int_out"], HT)
            e.wait_ge(s4["out_kept"], HT)
            for hb in range(HT):
                cc, role = 4 + hb // 4, "qo"[(hb // 4) % 2]
                e.wait_ge(w_rdy[role], 8 * ((cf.q, cf.o)[cc % 2] + cc // 2 + 1))
                e.wait_ge(s4["lo"], hb + 1)
                for t in range(TT):
                    mm = passes(e, ring[t], planes(ho, slice(None), hb % 8, slice(t * P, (t + 1) * P)),
                                planes(W[role], slice(None), hb % 4, slice(None)), hb == 0, hb == HT - 1)
                mm.then_inc(s4["used"], 1)
                if hb == 5:
                    turn_largest(1)
                if hb == 8:
                    spread(2)
            e.wait_ge(s4["row_out"], 5)
            e.wait_ge(s4["turned_out"], 16)
            for hb in range(HT):
                e.wait_ge(s4["h_int"], hb + 1)
                for t in range(TT):
                    mm = e.matmul(acc_i[t], hq[:, hb, t * P:(t + 1) * P], q_w2[:, hb, :], start=hb == 0, stop=hb == HT - 1)
                    if hb == HT - 1:
                        mm.then_inc(s4["acc"], 1)

        acc_i = [ps_t[0][:, :], ps_t[1][:, :], ps_t[2][:, :], ps_o[:, :]]

        def f3_act(e):
            e.wait_ge(s4["x_outliers"], 1)
            for d in range(DK):
                e.activation(q_xm[:, d, :], xF[:, d, :], ACT.Abs, scale=q_mi[:, d:d + 1]).then_inc(s4["x_magnitude"], 1)
            e.wait_ge(s_lay, LAY["f3"])
            for step in range(9):
                cc = step - 1
                if cc >= 0:
                    e.wait_ge(s4["rows_rounded"], cc + 1)
                    if cc >= 2:
                        e.wait_ge(s4["turned"], 2 * cc - 2)
                    e.activation(q_int[cc % 2][:, :], q_nat[cc % 2][:, :], ACT.Copy, bias=-MAGIC).then_inc(s4["rows_int"], 1)
                for j in (2 * step, 2 * step + 1) if step < 8 else ():
                    e.wait_ge(s4["out_full"], j + 1)
                    e.activation(h[:, j, :], ring[j % 2], ACT.Identity, bias=q_b1[:, j:j + 1]).then_inc(s4["out_kept"], 1)
                if cc < 0:
                    continue
                for part in range(2):
                    n = 2 * cc + part
                    e.wait_ge(s4["turned"], n + 1)
                    src = ps_t[n % 2][:, :].bitcast(BF16).rearrange("p (k w) -> p k w", k=2 if cc < 4 else 8)
                    dst = q_w1[:, 2 * part:2 * part + 2, cc * 512:(cc + 1) * 512] if cc < 4 else \
                        q_w2[:, 8 * part:8 * part + 8, (cc - 4) * P:(cc - 3) * P]
                    e.activation(dst, src, ACT.Copy).then_inc(s4["turned_out"], 1)
            e.wait_ge(s4["masks"], 1)

            def outlier_hi(hb):
                if hb >= 8:
                    e.wait_ge(s4["used"], hb - 7)
                e.activation(ho[0][:, hb % 8, :], h[:, hb, :], ACT.Copy, scale=q_mo[:, hb:hb + 1]).then_inc(s4["hi"], 1)
            for hb in range(8):
                outlier_hi(hb)
            for j in range(HT):
                if j >= 4:
                    e.wait_ge(s4["magnitude_used"], j - 3)
                e.activation(q_ab[:, j % 4, :], h[:, j, :], ACT.Abs, scale=q_mi[:, j:j + 1]).then_inc(s4["magnitude"], 1)
            for hb in range(8, HT):
                outlier_hi(hb)

        def f3_dve(e, link):
            e.memset(ones[:, :], 1.0)
            link(e.tensor_copy(identb[:, :], ident[:, :]))

            def masks(n):
                e.tensor_scalar(q_mo[:, 0:n], q_cm[:, 0:n], 3.0, None, ALU.is_gt)
                return e.tensor_scalar(q_mi[:, 0:n], q_cm[:, 0:n], 3.0, None, ALU.is_le)

            def round_rows(cc):
                nat = q_nat[cc % 2]
                e.wait_ge(s_nat[cc % 2], 16 * (cc // 2 + 1))
                if cc < 4:
                    am, sw, w = q_am[:, 4 * cc:4 * cc + 4], q_sw1[:, 4 * cc:4 * cc + 4], 4
                else:
                    am, sw, w = q_am[:, 4 * cc:4 * cc + 1], q_sw2[:, cc - 4:cc - 3], 1
                link(e.tensor_reduce(am, nat[:, :].rearrange("p (a n) -> p a n", a=w), AX.X, ALU.max,
                                     apply_absolute_value=True))
                link(e.tensor_scalar(sw, am, 1.0 / 127.0, 1e-8, ALU.mult, ALU.max))
                link(e.reciprocal(q_cm[:, 0:w], sw))
                for a in range(w):
                    v = nat[:, a * (2048 // w):(a + 1) * (2048 // w)]
                    last = e.tensor_scalar(v, v, q_cm[:, a:a + 1], MAGIC, ALU.mult, ALU.add)
                link(last)
                e.tensor_scalar(nat[:, :], nat[:, :], MAGIC + 127.0, MAGIC - 127.0, ALU.min, ALU.max)\
                    .then_inc(s4["rows_rounded"], 1)

            def make_diag(scales):
                for t in range(4):
                    last = e.tensor_scalar(diag4[:, t, :], ident[:, :], scales[:, t:t + 1], None, ALU.mult)
                last.then_inc(s4["diag"], 1)

            def token_scales(before):
                e.wait_ge(s4["row_full"], before + 1)
                e.tensor_reduce(q_tm[:, :], scale_bank[0].rearrange("p (t n) -> p t n", t=TT), AX.X, ALU.max)\
                    .then_inc(s4["row_out"], 1)
                e.wait_ge(s4["row_out"], before + 1)
                link(e.tensor_scalar(q_ts[:, :], q_tm[:, :], 1.0 / 127.0, 1e-8, ALU.mult, ALU.max))
                make_diag(q_ts)

            def scale_rows(before):
                e.wait_ge(s4["row_full"], before + 1)
                e.tensor_copy(q_srow[:, :], scale_bank[1]).then_inc(s4["row_out"], 1)
                e.wait_ge(s4["row_out"], before + 1)
                link(e.reciprocal(q_rrow[:, :], q_srow[:, :]))

            def quantise(dst, src, keep, i, done):
                t = q_t[:, i % 2, :]
                link(e.scalar_tensor_tensor(out=t, in0=src, scalar=keep, in1=q_rrow[:, :], op0=ALU.mult, op1=ALU.mult))
                link(e.tensor_scalar(t, t, MAGIC, MAGIC + 127.0, ALU.add, ALU.min))
                e.tensor_scalar(dst, t, MAGIC - 127.0, -MAGIC, ALU.max, ALU.add).then_inc(done, 1)
            link(e.tensor_tensor(xF[:, :, :].rearrange("p d t -> p (d t)"),
                                 xT[0][:, :, :].rearrange("p d t -> p (d t)").bitcast(F32),
                                 xT[1][:, :, :].rearrange("p d t -> p (d t)").bitcast(F32), ALU.add))
            link(e.tensor_reduce(q_cm[:, 0:DK], xF[:, :, :], AX.X, ALU.max, apply_absolute_value=True))
            link(masks(DK))
            for d in range(DK):
                for y in range(2):
                    last = e.tensor_scalar(xT[y][:, d, :], xT[y][:, d, :].bitcast(F32), q_mo[:, d:d + 1], None, ALU.mult)
            last.then_inc(s4["x_outliers"], 1)
            for cc in range(6):
                round_rows(cc)
            link(e.memset(q_amx[:, :], 0.0))
            for d in range(DK):
                e.wait_ge(s4["x_magnitude"], d + 1)
                last = e.tensor_tensor(q_amx[:, :], q_xm[:, d, :], q_amx[:, :], ALU.max)
                if d < DK - 1:
                    link(last)
            last.then_inc(s4["largest"], 1)
            round_rows(6)
            token_scales(0)
            round_rows(7)
            scale_rows(1)
            for d in range(DK):
                quantise(xq[:, d, :], xF[:, d, :], q_mi[:, d:d + 1], d, s4["x_int"])
            make_diag(q_sw2)
            for j in range(HT):
                e.wait_ge(s4["int_full"], j + 1)
                e.tensor_tensor(q_t[:, j % 2, :], ring[2 + j % 2], q_srow[:, :], ALU.mult).then_inc(s4["int_out"], 1)
                e.wait_ge(s4["int_out"], j + 1)
                e.wait_ge(s4["out_kept"], j + 1)
                e.scalar_tensor_tensor(out=h[:, j, :], in0=q_t[:, j % 2, :], scalar=q_sw1[:, j:j + 1], in1=h[:, j, :],
                                       op0=ALU.mult, op1=ALU.add).then_inc(s4["summed"], 1)
                if j % 4 == 3:
                    e.wait_ge(s4["summed"], j + 1)
                    last = e.tensor_reduce(q_cm[:, j - 3:j + 1], h[:, j - 3:j + 1, :], AX.X, ALU.max, apply_absolute_value=True)
            link(last)
            masks(HT).then_inc(s4["masks"], 1)
            e.wait_ge(s4["masks"], 1)

            def outlier_lo(hb):
                e.wait_ge(s4["hi"], hb + 1)
                e.scalar_tensor_tensor(out=ho[1][:, hb % 8, :], in0=h[:, hb, :], scalar=q_mo[:, hb:hb + 1],
                                       in1=ho[0][:, hb % 8, :].bitcast(F32), op0=ALU.mult, op1=ALU.subtract)\
                    .then_inc(s4["lo"], 1)
            for hb in range(8):
                outlier_lo(hb)
            link(e.memset(q_amx[:, :], 0.0))
            for j in range(HT):
                e.wait_ge(s4["magnitude"], j + 1)
                e.tensor_tensor(q_amx[:, :], q_ab[:, j % 4, :], q_amx[:, :], ALU.max).then_inc(s4["magnitude_used"], 1)
                e.wait_ge(s4["magnitude_used"], j + 1)
            e.wait_ge(s4["row_full"], 3)
            e.tensor_copy(q_s2row[:, :], scale_bank[1]).then_inc(s4["row_out"], 1)
            outlier_lo(8)
            outlier_lo(9)
            e.wait_ge(s_lay, LAY["f3"])
            add_row(e, q_b2[:, :], link)
            token_scales(3)
            outlier_lo(10)
            outlier_lo(11)
            scale_rows(4)
            for hb in range(HT):
                quantise(hq[:, hb, :], h[:, hb, :], q_mi[:, hb:hb + 1], hb, s4["h_int"])
                if 12 + hb < HT:
                    outlier_lo(12 + hb)
            e.wait_ge(s4["used"], HT)
            for t in range(TT):
                last = e.tensor_tensor(x[:, t, :], ring[t], x[:, t, :], ALU.add)
            link(last)
            for t in range(TT):
                e.wait_ge(s4["acc"], t + 1)
                link(e.scalar_tensor_tensor(out=q_t[:, t % 2, :], in0=acc_i[t], scalar=q_ts[:, t:t + 1], in1=q_s2row[:, :],
                                            op0=ALU.mult, op1=ALU.mult))
                e.tensor_tensor(x[:, t, :], x[:, t, :], q_t[:, t % 2, :], ALU.add).then_inc(s4["finished"], 1)

        norms = [Norm(i) for i in range(8)]
        a0 = Attention(L0, A, None)
        a1 = Attention(L1, A, ("o", START["l1"].o), {"q": START["f0"].g + 8, "kv": START["f0"].g})
        a2 = Attention(L2, A, ("o", START["l2"].o), {"q": START["f1"].g + 8, "kv": START["f1"].g + 4})
        LAY = {"l0": 16 * 3, "f0": 16 * 5, "f1": 16 * 7, "l3": 16 * 9, "f3": 16 * 11}

        block = ctx.enter_context(nc.Block())

        @block.sync
        def _(e):
            e.dma_start(x[:, :, :], A["x"]).then_inc(s_x, 16)
            e.dma_start(ident[:, :], A["ident"]).then_inc(s_const, 16)
            load(e, "q", a0.c.q, a0.wq[0], None)
            e.dma_start(craw[:, :, :], A["ctxT"]).then_inc(s_ctx, 16)
            load(e, "kv", a0.c.kv, a0.wkv[0], None, cols=256)
            e.dma_start(SP["l0"].cos[:, :], A["cos"]).then_inc(s_lay, 16)
            e.dma_start(SP["l0"].sin[:, :], A["sin"]).then_inc(s_lay, 16)
            e.dma_start(SP["l0"].mask[:, :, :], A["l0_mask"]).then_inc(s_lay, 16)
            a0.sp(e)
            f0_sp(e)
            a1.sp_first(e)
            a1.sp(e)
            f1_sp(e)
            a2.sp_first(e)
            a2.sp(e)
            f2_sp(e)
            l3_sp(e)
            f3_sp(e)

        @block.gpsimd
        def _(e):
            e.memset(mhalf[:, :], -0.5).then_inc(s_plink, 1)
            e.memset(one[:, :], 1.0).then_inc(s_plink, 1)
            e.wait_ge(s_plink, 2)
            norms[0].pool(e)
            split_all(e, "q", a0.c.q, None)
            for d in range(DK):
                e.wait_ge(s_chi, d + 1)
                e.tensor_tensor(cT[1][:, d, :], craw[:, d, :], cT[0][:, d, :].bitcast(F32), ALU.subtract).then_inc(s_csplit, 1)
            split_all(e, "kv", a0.c.kv, None, cols=256)
            a0.pool(e)
            f0_pool_first(e)
            norms[1].pool(e)
            f0_pool(e)
            a1.pool_first(e)
            norms[2].pool(e)
            a1.pool_second(e)
            a1.pool(e)
            f1_pool_first(e)
            norms[3].pool(e)
            f1_pool(e)
            a2.pool_first(e)
            norms[4].pool(e)
            a2.pool_second(e)
            a2.pool(e)
            f2_pool_first(e)
            norms[5].pool(e)
            f2_pool(e)
            l3_pool_first(e)
            norms[6].pool(e)
            l3_pool(e)
            norms[7].pool(e)
            f3_pool(e)

        @block.tensor
        def _(e):
            e.wait_ge(s_const, 16)
            norms[0].pe(e)
            a0.pe(e)
            norms[1].pe(e)
            f0_pe(e)
            norms[2].pe(e)
            a1.pe(e)
            norms[3].pe(e)
            f1_pe(e)
            norms[4].pe(e)
            a2.pe(e)
            norms[5].pe(e)
            f2_pe(e)
            norms[6].pe(e)
            l3_pe(e)
            norms[7].pe(e)
            f3_pe(e)

        @block.scalar
        def _(e):
            norms[0].act(e)
            e.wait_ge(s_ctx, 16)
            for d in range(DK):
                e.activation(cT[0][:, d, :], craw[:, d, :], ACT.Copy).then_inc(s_chi, 1)
            a0.act(e)
            norms[1].act(e)
            f0_act(e)
            norms[2].act(e)
            a1.act(e)
            norms[3].act(e)
            f1_act(e)
            norms[4].act(e)
            a2.act(e)
            norms[5].act(e)
            f2_act(e)
            norms[6].act(e)
            l3_act(e)
            norms[7].act(e)
            f3_act(e)

        @block.vector
        def _(e):
            links = [0]

            def link(ins):
                links[0] += 1
                ins.then_inc(s_link, 1)
                e.wait_ge(s_link, links[0])
            e.wait_ge(s_x, 16)
            norms[0].dve(e, link)
            e.wait_ge(s_lay, LAY["l0"])
            a0.dve(e, link)
            norms[1].dve(e, link)
            f0_dve(e, link)
            norms[2].dve(e, link)
            a1.dve(e, link)
            norms[3].dve(e, link)
            f1_dve(e, link)
            norms[4].dve(e, link)
            a2.dve(e, link)
            norms[5].dve(e, link)
            f2_dve(e, link)
            norms[6].dve(e, link)
            l3_dve(e, link)
            norms[7].dve(e, link)
            f3_dve(e, link)

def _layout(i):
    import numpy as np

    def k_tiles(w):
        return w.reshape(-1, 128, w.shape[1]).transpose(1, 0, 2)

    def groups(w, n):
        return np.stack([k_tiles(w[:, j * (w.shape[1] // n):(j + 1) * (w.shape[1] // n)]) for j in range(n)])

    def head_rows(w, n, hd):
        return w.reshape(n, 4, hd, 512).transpose(0, 2, 1, 3)

    def rows(b):
        return np.broadcast_to(b, (128, b.shape[0]))
    a = {"x": i["x"].reshape(4, 128, 512).transpose(1, 0, 2),
         "ctxT": k_tiles(i["ctx_4096"].reshape(1024, 512).T),
         "ident": np.eye(128, dtype=np.float32),
         "l0_mask": i["mask_BxSxS2_ff0"].reshape(4, 128, 512).transpose(1, 0, 2)}
    inv = (1.0 / np.float32(10000.0) ** (np.arange(0, 128, 2, dtype=np.float32) / np.float32(128))).astype(np.float32)
    ang = (np.arange(512, dtype=np.float32)[None, :] * inv[:, None]).astype(np.float32)
    a["cos"] = np.concatenate([np.cos(ang), np.cos(ang)]).astype(np.float32)
    a["sin"] = np.concatenate([-np.sin(ang), np.sin(ang)]).astype(np.float32)
    a["l0_wq"] = groups(i["L0_xattn_wq"], 8)
    a["l0_wkv"] = np.concatenate([groups(i["L0_xattn_wk"], 8), groups(i["L0_xattn_wv"], 8)], -1)
    a["l0_wo"] = head_rows(i["L0_xattn_wo"], 8, 128)
    a["l1_wq"] = groups(i["L1_xattn_Wq"].T, 4)
    a["l1_wkv"] = np.concatenate([groups(i["L1_xattn_Wk"].T, 4), groups(i["L1_xattn_Wv"].T, 4)], -1)
    a["l1_wo"] = head_rows(i["L1_xattn_Wo"].T, 4, 96)
    a["l2_wq"] = groups(i["L2_xattn_Wq"], 8)
    a["l2_wkv"] = np.concatenate([groups(i["L2_xattn_Wk"], 4), groups(i["L2_xattn_Wv"], 4)], -1)
    a["l2_wo"] = head_rows(i["L2_xattn_Wo"], 8, 128)
    a["f0_w12"] = groups(i["L0_ffn_w12"].T, 2)
    a["f0_w3"] = k_tiles(i["L0_ffn_w3"].T)
    a["f0_b12"] = i["L0_ffn_b12"].reshape(8, 128).T
    a["f0_b3"] = rows(i["L0_ffn_b3"])
    a["f1_wb"] = k_tiles(i["L1_ffn_W_base"].T)
    a["f1_bb"] = rows(i["L1_ffn_b_base"])
    a["f1_br"] = rows(i["L1_ffn_b_router"])
    a["f1_wa"] = k_tiles(np.concatenate([i["L1_ffn_lora_A"].transpose(1, 0, 2).reshape(512, 128), i["L1_ffn_W_router"].T,
                                         np.zeros((512, 120), np.float32)], 1))
    a["f1_lb"] = i["L1_ffn_lora_B"].reshape(128, 4, 128)
    a["f2_wr"] = k_tiles(i["L2_ffn_Wr"].T)
    a["f2_wa"] = groups(i["L2_ffn_A"].reshape(1024, 512).T, 2)
    a["f2_wb"] = i["L2_ffn_B"].transpose(0, 2, 1).reshape(2, 4, 128, 512).transpose(0, 2, 1, 3)
    wq = i["L3_xattn_w_q"].reshape(2, 4, 4, 16, 512).transpose(0, 2, 1, 3, 4)
    wq = np.stack([wq, wq], 3).reshape(1024, 512)
    wk = i["L3_xattn_w_k"].reshape(2, 4, 16, 512)
    wk = np.stack([wk, wk], 2).reshape(256, 512)
    a["l3_wq"] = groups(wq.T, 2)
    a["l3_wkv"] = np.concatenate([groups(wk.T, 2), groups(i["L3_xattn_w_v"].T, 2)], -1)
    wo = i["L3_xattn_w_out"].T.reshape(2, 4, 4, 16, 512).transpose(0, 2, 1, 3, 4)
    a["l3_wo"] = np.stack([wo, wo], 3).reshape(2, 4, 128, 512).transpose(0, 2, 1, 3)
    a["l3_mask"] = i["mask_SxS2_bk0"].reshape(2, 128, 512).transpose(1, 0, 2)
    lo = (np.arange(128) % 32 >= 16).astype(np.float32)
    a["l3_sel"] = np.stack([lo * np.float32(0.25), 1 - 2 * lo], 1).astype(np.float32)
    a["f3_w1"] = groups(i["L3_ffn_W1"].T, 4)
    a["f3_w1n"] = i["L3_ffn_W1"].reshape(4, 4, 128, 512).transpose(0, 2, 1, 3).reshape(4, 128, 2048)
    a["f3_w2"] = i["L3_ffn_W2"].T.reshape(4, 4, 128, 512).transpose(0, 2, 1, 3)
    a["f3_w2n"] = i["L3_ffn_W2"].reshape(4, 128, 2048)
    a["f3_b1"] = i["L3_ffn_b1"].reshape(16, 128).T
    a["f3_b2"] = rows(i["L3_ffn_b2"])
    return {k: np.ascontiguousarray(v) for k, v in a.items()}

def kernel(**inputs):
    import numpy as _np
    import concourse.bacc as _bacc
    from concourse import mybir as _mybir
    from concourse.bass_utils import run_bass_kernel_spmd as _run

    nc = _bacc.Bacc("TRN2", target_bir_lowering=False, num_devices=1)
    arrays = _layout({k: _np.asarray(v) for k, v in inputs.items()})
    arrays = {f"in_{k}": v for k, v in arrays.items()}
    A = {k[3:]: nc.dram_tensor(k, v.shape, _mybir.dt.from_np(v.dtype), kind="ExternalInput").ap() for k, v in arrays.items()}
    out = nc.dram_tensor("out", (2, 256, 512), _mybir.dt.float32, kind="ExternalOutput").ap()
    program(nc, A, out)
    r = _run(nc, [arrays], core_ids=[0])
    return r.results[0]["out"]
```
